# Optimizing a Trainium2 kernel written in Bass

```python
import numpy as np
import jax
import jax.numpy as jnp

def _softmax(x, axis=-1):
    return jax.nn.softmax(x, axis=axis)

def _gelu(x):
    return jax.nn.gelu(x, approximate=True)

def _silu(x):
    return jax.nn.silu(x)

def _sigmoid(x):
    return jax.nn.sigmoid(x)

def _layernorm(x, axis=-1, eps=1e-05):
    m = jnp.mean(x, axis=axis, keepdims=True)
    v = jnp.var(x, axis=axis, keepdims=True)
    return (x - m) / jnp.sqrt(v + eps)

def _scatter_add(tgt, idx, src, axis=0):
    return tgt.at[idx].add(src)

def _segment_sum(src, seg, n):
    return jax.ops.segment_sum(src, seg, n)
kernel_name = 'mk_gnn_resnorm_d4_gnn_r32_0616af'

def setup_inputs(seed: int=0):
    np.random.seed(seed)
    _w = jnp.asarray

    def _rec_inputs():
        import jax
        import jax.numpy as jnp
        _gk = jax.random.key(seed)
        x = -0.0003713 + 1 * jax.random.normal(jax.random.fold_in(_gk, 1), (3125, 128), jnp.float32)
        src = jax.random.randint(jax.random.fold_in(_gk, 2), (100000,), 0, 3125, jnp.int32)
        dst = jax.random.randint(jax.random.fold_in(_gk, 3), (100000,), 0, 3125, jnp.int32)
        _o = jnp.argsort(dst, stable=True)
        src = src[_o]
        dst = dst[_o]
        edge_attr_64 = 0.000189758 + 1.00013 * jax.random.normal(jax.random.fold_in(_gk, 12), (100000, 64), jnp.float32)
        return (x, src, dst, edge_attr_64)
    x, src, dst, edge_attr_64 = _rec_inputs()

    def _L0_gnn_setup():
        import jax, jax.numpy as jnp
        import numpy as np
        N_NODES = 3125
        N_EDGES = 50000
        F_IN = 128
        F_HID = 128

        def _sage_mean(x, src, dst, W_self, W_neigh, b, n_nodes):
            deg = jax.ops.segment_sum(jnp.ones_like(dst, dtype=x.dtype), dst, num_segments=n_nodes)
            agg = jax.ops.segment_sum(x[src], dst, num_segments=n_nodes)
            agg = agg / jnp.maximum(deg, 1.0)[:, None]
            return x @ W_self + agg @ W_neigh + b
        key = jax.random.key(seed)
        ks = jax.random.split(key, 8)
        s_in = 1.0 / np.sqrt(F_IN)
        s_hid = 1.0 / np.sqrt(F_HID)
        return {'x': jax.random.normal(ks[0], (N_NODES, F_IN), dtype=jnp.float32), 'W_self1': jax.random.normal(ks[1], (F_IN, F_HID), dtype=jnp.float32) * s_in, 'W_neigh1': jax.random.normal(ks[2], (F_IN, F_HID), dtype=jnp.float32) * s_in, 'b1': jnp.zeros((F_HID,), dtype=jnp.float32), 'W_self2': jax.random.normal(ks[3], (F_HID, F_HID), dtype=jnp.float32) * s_hid, 'W_neigh2': jax.random.normal(ks[4], (F_HID, F_HID), dtype=jnp.float32) * s_hid, 'b2': jnp.zeros((F_HID,), dtype=jnp.float32), 'src': jax.random.randint(ks[5], (N_EDGES,), 0, N_NODES, dtype=jnp.int32), 'dst': jax.random.randint(ks[6], (N_EDGES,), 0, N_NODES, dtype=jnp.int32)}
    _L0_gnn_all = _L0_gnn_setup()
    _L0_gnn_in = {k: v for k, v in _L0_gnn_all.items() if k in ('W_self1', 'W_neigh1', 'b1', 'W_self2', 'W_neigh2', 'b2')}
    del _L0_gnn_all

    def _L1_gnn_setup():
        import jax, jax.numpy as jnp
        import numpy as np
        N_NODES = 50000
        N_EDGES = 25000
        HIDDEN = 128
        REL = 64

        def _layer_norm(x, gamma, beta, eps=1e-05):
            mu = jnp.mean(x, axis=-1, keepdims=True)
            var = jnp.mean(jnp.square(x - mu), axis=-1, keepdims=True)
            return (x - mu) * jax.lax.rsqrt(var + eps) * gamma + beta
        key = jax.random.key(seed)
        ks = jax.random.split(key, 12)
        s = lambda fan_in: 1.0 / np.sqrt(fan_in)
        inp = {'node_states': jax.random.normal(ks[0], (N_NODES, HIDDEN), dtype=jnp.float32), 'edge_index': jax.random.randint(ks[1], (2, N_EDGES), 0, N_NODES, dtype=jnp.int64), 'edge_rel_emb': jax.random.normal(ks[2], (N_EDGES, REL), dtype=jnp.float32), 'W1': jax.random.uniform(ks[3], (2 * HIDDEN + REL, HIDDEN), jnp.float32, -s(2 * HIDDEN + REL), s(2 * HIDDEN + REL)), 'b1': jax.random.uniform(ks[4], (HIDDEN,), jnp.float32, -s(2 * HIDDEN + REL), s(2 * HIDDEN + REL)), 'W2': jax.random.uniform(ks[5], (HIDDEN, HIDDEN), jnp.float32, -s(HIDDEN), s(HIDDEN)), 'b2': jax.random.uniform(ks[6], (HIDDEN,), jnp.float32, -s(HIDDEN), s(HIDDEN)), 'Wn': jax.random.uniform(ks[7], (HIDDEN, HIDDEN), jnp.float32, -s(HIDDEN), s(HIDDEN)), 'bn': jax.random.uniform(ks[8], (HIDDEN,), jnp.float32, -s(HIDDEN), s(HIDDEN)), 'gamma': jnp.ones((HIDDEN,), jnp.float32), 'beta': jnp.zeros((HIDDEN,), jnp.float32)}
        return inp
    _L1_gnn_all = _L1_gnn_setup()
    _L1_gnn_in = {k: v for k, v in _L1_gnn_all.items() if k in ('W1', 'b1', 'W2', 'b2', 'Wn', 'bn', 'gamma', 'beta')}
    del _L1_gnn_all

    def _L2_gnn_setup():
        import jax, jax.numpy as jnp
        import numpy as np
        N_NODES = 3125
        N_EDGES = 100000
        DIM = 128
        LN_EPS = 1e-05
        key = jax.random.key(seed)
        k1, k2, k3, k4 = jax.random.split(key, 4)
        x = jax.random.normal(k1, (N_NODES, DIM), dtype=jnp.float32)
        edge_index = jax.random.randint(k2, (2, N_EDGES), 0, N_NODES, dtype=jnp.int64)
        scale = 1.0 / np.sqrt(DIM)
        W = jax.random.uniform(k3, (DIM, DIM), minval=-scale, maxval=scale, dtype=jnp.float32)
        b = jax.random.uniform(k4, (DIM,), minval=-scale, maxval=scale, dtype=jnp.float32)
        gamma = jnp.ones((DIM,), dtype=jnp.float32)
        beta = jnp.zeros((DIM,), dtype=jnp.float32)
        return {'x': x, 'edge_index': edge_index, 'W': W, 'b': b, 'gamma': gamma, 'beta': beta}
    _L2_gnn_all = _L2_gnn_setup()
    _L2_gnn_in = {k: v for k, v in _L2_gnn_all.items() if k in ('W', 'b', 'gamma', 'beta')}
    del _L2_gnn_all

    def _L3_gnn_setup():
        import jax, jax.numpy as jnp
        import numpy as np
        N, E, D = (1250, 20000, 128)
        BN_EPS = 1e-05
        key = jax.random.key(seed)
        ks = jax.random.split(key, 4)
        x = jax.random.normal(ks[0], (N, D), dtype=jnp.float32)
        edge_index = jax.random.randint(ks[1], (2, E), 0, N, dtype=jnp.int32)
        W = jax.random.normal(ks[2], (D, D), dtype=jnp.float32) / np.sqrt(D).astype(np.float32)
        b = jnp.zeros((D,), jnp.float32)
        gamma = jnp.ones((D,), jnp.float32)
        beta = jnp.zeros((D,), jnp.float32)
        gin_eps = jnp.zeros((1,), jnp.float32)
        return {'x': x, 'edge_index': edge_index, 'W': W, 'b': b, 'gamma': gamma, 'beta': beta, 'gin_eps': gin_eps}
    _L3_gnn_all = _L3_gnn_setup()
    _L3_gnn_in = {k: v for k, v in _L3_gnn_all.items() if k in ('W', 'b', 'gamma', 'beta', 'gin_eps')}
    del _L3_gnn_all
    return {'x': x, 'src': src, 'dst': dst, 'edge_attr_64': edge_attr_64, 'L0_gnn_W_self1': _L0_gnn_in['W_self1'], 'L0_gnn_W_neigh1': _L0_gnn_in['W_neigh1'], 'L0_gnn_b1': _L0_gnn_in['b1'], 'L0_gnn_W_self2': _L0_gnn_in['W_self2'], 'L0_gnn_W_neigh2': _L0_gnn_in['W_neigh2'], 'L0_gnn_b2': _L0_gnn_in['b2'], 'L1_gnn_W1': _L1_gnn_in['W1'], 'L1_gnn_b1': _L1_gnn_in['b1'], 'L1_gnn_W2': _L1_gnn_in['W2'], 'L1_gnn_b2': _L1_gnn_in['b2'], 'L1_gnn_Wn': _L1_gnn_in['Wn'], 'L1_gnn_bn': _L1_gnn_in['bn'], 'L1_gnn_gamma': _L1_gnn_in['gamma'], 'L1_gnn_beta': _L1_gnn_in['beta'], 'L2_gnn_W': _L2_gnn_in['W'], 'L2_gnn_b': _L2_gnn_in['b'], 'L2_gnn_gamma': _L2_gnn_in['gamma'], 'L2_gnn_beta': _L2_gnn_in['beta'], 'L3_gnn_W': _L3_gnn_in['W'], 'L3_gnn_b': _L3_gnn_in['b'], 'L3_gnn_gamma': _L3_gnn_in['gamma'], 'L3_gnn_beta': _L3_gnn_in['beta'], 'L3_gnn_gin_eps': _L3_gnn_in['gin_eps']}

def reference(x, src, dst, edge_attr_64, L0_gnn_W_self1, L0_gnn_W_neigh1, L0_gnn_b1, L0_gnn_W_self2, L0_gnn_W_neigh2, L0_gnn_b2, L1_gnn_W1, L1_gnn_b1, L1_gnn_W2, L1_gnn_b2, L1_gnn_Wn, L1_gnn_bn, L1_gnn_gamma, L1_gnn_beta, L2_gnn_W, L2_gnn_b, L2_gnn_gamma, L2_gnn_beta, L3_gnn_W, L3_gnn_b, L3_gnn_gamma, L3_gnn_beta, L3_gnn_gin_eps):
    import jax
    import jax.numpy as jnp

    def _L0_gnn_ref(x, W_self1, W_neigh1, b1, W_self2, W_neigh2, b2, src, dst):
        import jax, jax.numpy as jnp
        import numpy as np
        N_NODES = 3125
        N_EDGES = 50000
        F_IN = 128
        F_HID = 128

        def _sage_mean(x, src, dst, W_self, W_neigh, b, n_nodes):
            deg = jax.ops.segment_sum(jnp.ones_like(dst, dtype=x.dtype), dst, num_segments=n_nodes)
            agg = jax.ops.segment_sum(x[src], dst, num_segments=n_nodes)
            agg = agg / jnp.maximum(deg, 1.0)[:, None]
            return x @ W_self + agg @ W_neigh + b
        n = x.shape[0]
        h = _sage_mean(x, src, dst, W_self1, W_neigh1, b1, n)
        h = jax.nn.relu(h)
        h = _sage_mean(h, src, dst, W_self2, W_neigh2, b2, n)
        return h

    def _L1_gnn_ref(node_states, edge_index, edge_rel_emb, W1, b1, W2, b2, Wn, bn, gamma, beta):
        import jax, jax.numpy as jnp
        import numpy as np
        N_NODES = 50000
        N_EDGES = 25000
        HIDDEN = 128
        REL = 64

        def _layer_norm(x, gamma, beta, eps=1e-05):
            mu = jnp.mean(x, axis=-1, keepdims=True)
            var = jnp.mean(jnp.square(x - mu), axis=-1, keepdims=True)
            return (x - mu) * jax.lax.rsqrt(var + eps) * gamma + beta
        src, dst = (edge_index[0], edge_index[1])
        m_input = jnp.concatenate([node_states[src], node_states[dst], edge_rel_emb], axis=-1)
        h = jax.nn.relu(m_input @ W1 + b1)
        messages = jax.nn.relu(h @ W2 + b2)
        agg = jax.ops.segment_sum(messages, dst, num_segments=node_states.shape[0])
        updated = node_states + jax.nn.relu(agg @ Wn + bn)
        return _layer_norm(updated, gamma, beta)

    def _L2_gnn_ref(x, edge_index, W, b, gamma, beta):
        import jax, jax.numpy as jnp
        import numpy as np
        N_NODES = 3125
        N_EDGES = 100000
        DIM = 128
        LN_EPS = 1e-05
        N = x.shape[0]
        loops = jnp.arange(N, dtype=edge_index.dtype)
        row = jnp.concatenate([edge_index[0], loops])
        col = jnp.concatenate([edge_index[1], loops])
        deg = jax.ops.segment_sum(jnp.ones_like(col, dtype=x.dtype), col, num_segments=N)
        deg_inv_sqrt = jnp.where(deg > 0, jax.lax.rsqrt(jnp.maximum(deg, 1.0)), 0.0)
        norm = deg_inv_sqrt[row] * deg_inv_sqrt[col]
        msg = norm[:, None] * x[row]
        agg = jax.ops.segment_sum(msg, col, num_segments=N)
        out = agg @ W.T + b
        mean = jnp.mean(out, axis=-1, keepdims=True)
        var = jnp.mean(jnp.square(out - mean), axis=-1, keepdims=True)
        out = (out - mean) * jax.lax.rsqrt(var + LN_EPS) * gamma + beta
        return out

    def _L3_gnn_ref(x, edge_index, W, b, gamma, beta, gin_eps):
        import jax, jax.numpy as jnp
        import numpy as np
        N, E, D = (1250, 20000, 128)
        BN_EPS = 1e-05
        src, dst = (edge_index[0], edge_index[1])
        agg = jax.ops.segment_sum(x[src], dst, num_segments=x.shape[0])
        h = (1.0 + gin_eps[0]) * x + agg
        h = h @ W.T + b
        mean = jnp.mean(h, axis=0)
        var = jnp.mean(jnp.square(h - mean), axis=0)
        h = gamma * (h - mean) * jax.lax.rsqrt(var + BN_EPS) + beta
        h = jax.nn.relu(h)
        return h + x
    edge_index = jnp.stack([src, dst])
    x = _layernorm(x + _L0_gnn_ref(x, L0_gnn_W_self1, L0_gnn_W_neigh1, L0_gnn_b1, L0_gnn_W_self2, L0_gnn_W_neigh2, L0_gnn_b2, src, dst), axis=-1)
    x = _layernorm(x + _L1_gnn_ref(x, edge_index, edge_attr_64, L1_gnn_W1, L1_gnn_b1, L1_gnn_W2, L1_gnn_b2, L1_gnn_Wn, L1_gnn_bn, L1_gnn_gamma, L1_gnn_beta), axis=-1)
    x = _layernorm(x + _L2_gnn_ref(x, edge_index, L2_gnn_W, L2_gnn_b, L2_gnn_gamma, L2_gnn_beta), axis=-1)
    x = _layernorm(x + _L3_gnn_ref(x, edge_index, L3_gnn_W, L3_gnn_b, L3_gnn_gamma, L3_gnn_beta, L3_gnn_gin_eps), axis=-1)
    return x

_drawn_inputs = setup_inputs


def setup_inputs(seed=0):
    import zlib

    import numpy as np

    out = dict(_drawn_inputs(seed))
    spreads = {'L0_gnn_b1': (0.0, 0.1),
     'L0_gnn_b2': (0.0, 0.1),
     'L1_gnn_gamma': (1.0, 0.2),
     'L1_gnn_beta': (0.0, 0.1),
     'L2_gnn_gamma': (1.0, 0.2),
     'L2_gnn_beta': (0.0, 0.1),
     'L3_gnn_b': (0.0, 0.8),
     'L3_gnn_gamma': (1.0, 0.2),
     'L3_gnn_beta': (0.0, 0.272)}
    factors = {'L1_gnn_bn': 3.051}
    for name, (base, spread) in spreads.items():
        noise = np.random.default_rng([zlib.crc32(name.encode()), seed]).standard_normal(out[name].shape)
        drawn = base * np.exp(spread * noise) if base else spread * noise
        out[name] = jnp.asarray(drawn.astype(out[name].dtype))
    for name, factor in factors.items():
        out[name] = (out[name] * factor).astype(out[name].dtype)
    return out
```

```python
from contextlib import ExitStack

import concourse.bass as bass
from concourse import mybir

F32 = mybir.dt.float32
BF16 = mybir.dt.bfloat16
I32 = mybir.dt.int32
I16 = mybir.dt.int16
ALU = mybir.AluOpType
ACT = mybir.ActivationFunctionType

P = 128
N = 3125
E = 100000
D = 128
R = 64
EPS = 1e-5
NT = (N + P - 1) // P
NP = NT * P
TAIL = N - (NT - 1) * P
J = 4
BLK = J * P
NB = (E + BLK - 1) // BLK
GRP = NB // 2
DUP = NB * BLK - E
WIN = 24
H0 = 13
CH = 4
CHUNKS = [(c, min(CH, NT - c)) for c in range(0, NT, CH)]
NFULL = NT // CH
PAIRS = NFULL // 2
NC = len(CHUNKS)
assert NB % 2 == 0 and NFULL % 2 == 0 and GRP <= P


def build(nc, t, out, x1_d, xa_d, xb_d):
    ctx = ExitStack()
    with ctx:
        def sb(name, shape, dt):
            return ctx.enter_context(nc.sbuf_tensor(name, shape, dt))

        def sem(name):
            return ctx.enter_context(nc.semaphore(name))

        adj = sb("adj", [P, NT, NP], BF16)
        arena = sb("arena", [P, 9600], F32)
        src_idx = sb("src_idx", [P, NB, J], I32)
        drel = sb("drel", [P, NB, J], F32)
        base_row = sb("base_row", [1, NB], I32)
        w_a = sb("w_a", [P, D], F32)
        w_b = sb("w_b", [P, D], F32)
        w_c = sb("w_c", [P, D], F32)
        bias_b = sb("bias_b", [P, D], F32)
        gamma_b = sb("gamma_b", [P, D], F32)
        beta_b = sb("beta_b", [P, D], F32)
        bias_row = sb("bias_row", [1, D], F32)
        ident_f = sb("ident_f", [P, P], F32)
        ident_h = sb("ident_h", [P, P], BF16)
        iota_c = sb("iota_c", [P, NT * WIN], I16)
        ones_h = sb("ones_h", [P, 2], BF16)
        ones_row = sb("ones_row", [1, P], F32)
        inv_deg = sb("inv_deg", [P, NT], F32)
        dinv = sb("dinv", [P, NT], F32)
        std_deg = sb("std_deg", [P, NT], F32)
        stats = sb("stats", [P, CH * 2, 6], F32)
        mv = sb("mv", [P, CH, 2], F32)
        std = sb("std", [P, CH], F32)
        rstd = sb("rstd", [P, CH], F32)
        cols = sb("cols", [P, 8], F32)
        idx = sb("idx", [P, 2, J], I32)
        win_i = sb("win_i", [P, WIN], F32)

        parts = [arena[:, 1600 * q:1600 * (q + 1)].bitcast(BF16).rearrange("p (k d) -> p k d", d=D)
                 for q in range(3)]
        xn = arena[:, 4800:8000].rearrange("p (k d) -> p k d", d=D)
        self_t = arena[:, 8000:8512]
        agg_t = arena[:, 8512:9024]
        node = arena[:, 9024:9536].rearrange("p (j d) -> p j d", d=D)

        prep = adj[:, 20:25, :].rearrange("p k n -> p (k n)").bitcast(F32)
        raw_src = prep[:, 0:1024].bitcast(I32)
        raw_dst = prep[:, 1024:2048].bitcast(I32)
        hi_i = prep[:, 2048:3072].bitcast(I32)
        lo_i = prep[:, 3072:4096].bitcast(I32)
        p_src = prep[:, 4096:5120]
        p_lo = prep[:, 5120:6144]
        p_drel = prep[:, 6144:7168]
        p_comb = raw_dst.bitcast(F32)
        oh_src = [arena[:, 256 * u:256 * (u + 1)].bitcast(BF16).rearrange("p (j n) -> p j n", j=J)
                  for u in range(2)]
        oh_dst = [arena[:, 512 + 1200 * u:512 + 1200 * (u + 1)].bitcast(BF16)
                  .rearrange("p (j n) -> p j n", j=J) for u in range(2)]
        comb = arena[:, 2912:2912 + NB * J].rearrange("p (s j) -> p s j", j=J)
        lo_f = arena[:, 2912 + NB * J:2912 + 2 * NB * J].rearrange("p (s j) -> p s j", j=J)
        KE = R + WIN

        def edge(a, n):
            return arena[:, a:a + n]

        ec = [edge(J * KE * u, J * KE).rearrange("p (j f) -> p j f", j=J) for u in range(2)]
        o = 2 * J * KE
        g_x = [edge(o + 512 * u, 512) for u in range(2)]
        z_e = [edge(o + 1024 + 512 * u, 512) for u in range(2)]
        h_t = [edge(o + 2048 + 512 * u, 512) for u in range(2)]
        msg = [edge(o + 3072 + 512 * u, 512) for u in range(2)]
        assert o + 4096 <= 4800
        ec_t = [arena[:, 8000 + 512 * u:8512 + 512 * u] for u in range(2)]
        w_e = [arena[:, 9024 + 128 * u:9152 + 128 * u] for u in range(2)]
        oh_e = [arena[:, 9280 + 96 * u:9376 + 96 * u].rearrange("p (j w) -> p j w", j=J)
                for u in range(2)]
        res = [arena[:, a:a + 512].rearrange("p (j d) -> p j d", d=D) for a in (8000, 8512)]
        agg_all = arena[:, 4800:8000]

        ps = ctx.enter_context(nc.psum_tensor("ps", [P, 8, 512], F32))

        phase_ends = sem("phase_ends")
        loads = [sem(f"loads{i}") for i in range(10)]
        v_own = sem("v_own")
        a_own = sem("a_own")
        g_own = sem("g_own")
        prep_ready = sem("prep_ready")
        prep_t = sem("prep_t")
        prep_out = sem("prep_out")
        oh_ready = [sem(f"oh_ready{u}") for u in range(2)]
        oh_used = [sem(f"oh_used{u}") for u in range(2)]
        cnt_ready = [sem(f"cnt_ready{u}") for u in range(2)]
        adj_written = [sem(f"adj_written{u}") for u in range(2)]
        lin_base = {0: 0, 1: NC, 2: 3 * NC}
        adj_zero = sem("adj_zero")
        deg_ready = sem("deg_ready")
        agg_ready = sem("agg_ready")
        self_ready = sem("self_ready")
        agg_out = sem("agg_out")
        self_out = sem("self_out")
        lin_ready = sem("lin_ready")
        lin_used = sem("lin_used")
        selfs_ready = sem("selfs_ready")
        var_ready = sem("var_ready")
        std_ready = sem("std_ready")
        hi_ready = sem("hi_ready")
        res_ready = sem("res_ready")
        mid_ready = sem("mid_ready")
        low_ready = sem("low_ready")
        proj_t = sem("proj_t")
        proj_ts = sem("proj_ts")
        proj_ready = sem("proj_ready")
        proj_out = [sem(f"proj_out{h}") for h in range(2)]
        node_used = sem("node_used")
        stored = [sem(f"stored{i}") for i in range(2)]
        ec_loaded = [sem(f"ec_loaded{u}") for u in range(2)]
        ec_onehot = [sem(f"ec_onehot{u}") for u in range(2)]
        ec_used = [sem(f"ec_used{u}") for u in range(2)]
        w_loaded = [sem(f"w_loaded{u}") for u in range(2)]
        oh_e_ready = [sem(f"oh_e_ready{u}") for u in range(2)]
        ect_ready = [sem(f"ect_ready{u}") for u in range(2)]
        ect_out = [sem(f"ect_out{u}") for u in range(2)]
        z_ready = [sem(f"z_ready{u}") for u in range(2)]
        z_sum = [sem(f"z_sum{u}") for u in range(2)]
        zt_ready = [sem(f"zt_ready{u}") for u in range(2)]
        h_ready = [sem(f"h_ready{u}") for u in range(2)]
        m_ready = [sem(f"m_ready{u}") for u in range(2)]
        m_sum = [sem(f"m_sum{u}") for u in range(2)]
        msg_ready = [sem(f"msg_ready{u}") for u in range(2)]
        win_ready = [sem(f"win_ready{u}") for u in range(2)]
        win_added = sem("win_added")
        g_loaded = [sem(f"g_loaded{u}") for u in range(2)]
        idx_ready = sem("idx_ready")
        gather_mark = sem("gather_mark")
        gin_ready = sem("gin_ready")
        gin_out = sem("gin_out")
        bn_ready = sem("bn_ready")
        bn_relu = sem("bn_relu")
        fin_ready = sem("fin_ready")
        out_ready = sem("out_ready")
        twice_ready = sem("twice_ready")
        out_stored = sem("out_stored")

        block = ctx.enter_context(nc.Block())

        def phase_end(eng, n):
            eng.drain().then_inc(phase_ends, 1)
            eng.wait_ge(phase_ends, 5 * n)

        class Count:
            def __init__(self, eng, s):
                self.eng, self.s, self.n = eng, s, 0

            def add(self, inst):
                self.n += 1
                inst.then_inc(self.s, 1)

            def wait(self):
                self.eng.wait_ge(self.s, self.n)

        def bcast(v, n=P):
            return v.rearrange("(a d) -> a d", a=1).broadcast_to([n, v.shape[0]])

        def row(v):
            return v.rearrange("(a d) -> a d", a=1)

        def col(v):
            return v.rearrange("(d a) -> d a", a=1)

        @block.sync
        def _(sp):
            def block_rows(dst, src, s):
                last = (NB - 1 - GRP) * 512
                v = src[0:(NB - 1) * BLK].rearrange("(s e) -> s e", e=BLK)
                sp.dma_start(dst[0:GRP, 0:512], v[0:GRP]).then_inc(s, 16)
                sp.dma_start(dst[0:GRP - 1, 512:1024], v[GRP:NB - 1]).then_inc(s, 16)
                sp.dma_start(dst[GRP - 1:GRP, 512:1024],
                             src[E - BLK:E].rearrange("(s e) -> s e", s=1)).then_inc(s, 16)

            block_rows(raw_src, t["src"], loads[0])
            block_rows(raw_dst, t["dst"], loads[1])
            with nc.allow_non_contiguous_dma(reason="one word per block"):
                sp.dma_start(base_row[0:1, 0:NB - 1],
                             t["dst"][0:(NB - 1) * BLK].rearrange("(s e) -> e s", e=BLK)[0:1, :]).then_inc(loads[2], 16)
            sp.dma_start(base_row[0:1, NB - 1:NB], t["dst"][E - BLK:E - BLK + 1].rearrange("(s e) -> e s", e=1)).then_inc(loads[2], 16)

            def load_nodes(dst, src, s):
                sp.dma_start(dst[:, 0:NT - 1, :],
                             src[0:(NT - 1) * P, :].rearrange("(k p) d -> p k d", p=P)).then_inc(s, 16)
                sp.dma_start(dst[0:TAIL, NT - 1, :], src[(NT - 1) * P:N, :]).then_inc(s, 16)

            sp.wait_ge(g_own, 1)
            load_nodes(xn, t["x"], loads[3])
            sp.dma_start(w_a[:, :], t["L0_gnn_W_self1"]).then_inc(loads[4], 16)
            sp.dma_start(w_b[:, :], t["L0_gnn_W_neigh1"]).then_inc(loads[4], 16)
            sp.dma_start(bias_row[:, :], row(t["L0_gnn_b1"])).then_inc(loads[4], 16)
            sp.wait_ge(loads[2], 32)
            for n in range(1, 5):
                phase_end(sp, n)
            sp.dma_start(w_a[:, :], t["L0_gnn_W_self2"]).then_inc(loads[4], 16)
            sp.dma_start(w_b[:, :], t["L0_gnn_W_neigh2"]).then_inc(loads[4], 16)
            sp.dma_start(bias_row[:, :], row(t["L0_gnn_b2"])).then_inc(loads[4], 16)
            sp.wait_ge(res_ready, 2 * NC)
            load_nodes(xn, t["x"], loads[3])
            phase_end(sp, 5)
            sp.dma_start(w_a[:, :], t["L1_gnn_W1"][0:D, :]).then_inc(loads[4], 16)
            sp.dma_start(w_b[:, :], t["L1_gnn_W1"][D:2 * D, :]).then_inc(loads[4], 16)
            sp.dma_start(x1_d[:, :].rearrange("(k p) d -> p k d", p=P), xn).then_inc(loads[5], 16)
            for c, (k0, nt) in enumerate(CHUNKS):
                for h, dd in enumerate((xa_d, xb_d)):
                    sp.wait_ge(proj_out[h], c + 1)
                    sp.dma_start(dd[k0 * P:(k0 + nt) * P, :].rearrange("(k p) d -> p k d", p=P),
                                 arena[:, 1024 + 1024 * (c % 2) + 512 * h:1024 + 1024 * (c % 2) + 512 * h + nt * D]
                                 .rearrange("p (k d) -> p k d", d=D)).then_inc(stored[c % 2], 16)
            for u in range(2):
                sp.wait_ge(stored[u], 32 * len(CHUNKS[u::2]))
            sp.wait_ge(loads[5], 16)
            phase_end(sp, 6)
            sp.dma_start(w_b[:, :], t["L1_gnn_W2"]).then_inc(loads[6], 16)
            sp.dma_start(cols[:, 0:1], col(t["L1_gnn_b1"])).then_inc(loads[6], 16)
            sp.dma_start(bias_b[:, :], bcast(t["L1_gnn_b2"])).then_inc(loads[6], 16)
            for u in range(2):
                sp.dma_start(w_e[u][0:R, :], t["L1_gnn_W1"][2 * D:2 * D + R, :]).then_inc(loads[6], 16)

            def edge_loads(i, u, last=False):
                s = 2 * i + u
                e0 = E - BLK if last else s * BLK
                sp.wait_ge(ec_used[u], i)
                sp.dma_start(ec[u][:, :, 0:R],
                             t["edge_attr_64"][bass.ds(e0, BLK), :].rearrange("(j p) f -> p j f", p=P)
                             ).then_inc(ec_loaded[u], 16)
                b = sp.value_load(base_row[0:1, bass.ds(s, 1)], min_val=0, max_val=N - 1)
                sp.wait_ge(z_ready[u], i)
                sp.dma_start(w_e[u][R:KE, :], xb_d[bass.ds(b, WIN), :]).then_inc(w_loaded[u], 16)

            with sp.Fori(0, NB // 2 - 1) as i:
                edge_loads(i, 0)
                edge_loads(i, 1)
            edge_loads(NB // 2 - 1, 0)
            edge_loads(NB // 2 - 1, 1, last=True)
            phase_end(sp, 7)
            sp.dma_start(w_a[:, :], t["L1_gnn_Wn"]).then_inc(loads[7], 16)
            sp.dma_start(bias_row[:, :], row(t["L1_gnn_bn"])).then_inc(loads[7], 16)
            sp.dma_start(gamma_b[:, :], bcast(t["L1_gnn_gamma"])).then_inc(loads[7], 16)
            sp.dma_start(beta_b[:, :], bcast(t["L1_gnn_beta"])).then_inc(loads[7], 16)
            sp.dma_start(arena[:, 0:3200].rearrange("p (k d) -> p k d", d=D),
                         x1_d[:, :].rearrange("(k p) d -> p k d", p=P)).then_inc(loads[7], 16)
            phase_end(sp, 8)
            sp.dma_start(w_b[:, :], t["L2_gnn_W"]).then_inc(loads[8], 16)
            sp.dma_start(bias_b[:, :], bcast(t["L2_gnn_b"])).then_inc(loads[8], 16)
            sp.dma_start(gamma_b[:, :], bcast(t["L2_gnn_gamma"])).then_inc(loads[8], 16)
            sp.dma_start(beta_b[:, :], bcast(t["L2_gnn_beta"])).then_inc(loads[8], 16)
            phase_end(sp, 9)
            phase_end(sp, 10)
            sp.dma_start(w_b[:, :], t["L3_gnn_W"]).then_inc(loads[9], 16)
            sp.dma_start(cols[:, 0:1], col(t["L3_gnn_b"])).then_inc(loads[9], 16)
            sp.dma_start(cols[:, 1:2], col(t["L3_gnn_gamma"])).then_inc(loads[9], 16)
            sp.dma_start(cols[:, 2:3], col(t["L3_gnn_beta"])).then_inc(loads[9], 16)
            sp.dma_start(cols[:, 3:4], bcast(t["L3_gnn_gin_eps"])).then_inc(loads[9], 16)
            phase_end(sp, 11)
            phase_end(sp, 12)
            for c, (k0, nt) in enumerate(CHUNKS):
                sp.wait_ge(out_ready, c + 1)
                if nt == CH:
                    sp.dma_start(out[k0 * P:(k0 + nt) * P, :].rearrange("(k p) d -> p k d", p=P),
                                 arena[:, 4800 + k0 * D:4800 + (k0 + nt) * D].rearrange("p (k d) -> p k d", d=D)).then_inc(out_stored, 16)
                else:
                    sp.dma_start(out[k0 * P:N, :], arena[0:TAIL, 4800 + k0 * D:4800 + (k0 + 1) * D]).then_inc(out_stored, 16)
            sp.wait_ge(out_stored, 16 * NC)

        @block.gpsimd
        def _(pool):
            g = Count(pool, g_own)
            g.add(pool.memset(xn[:, NT - 1, :], 0.0))
            g.add(pool.memset(ident_f[:, :], 0.0))
            g.add(pool.memset(ident_h[:, :], 0.0))
            g.wait()
            g.add(pool.affine_select(out=ident_f[:, :], in_=ident_f[:, :], compare_op=ALU.not_equal, fill=1.0,
                                     base=0, pattern=[[-1, P]], channel_multiplier=1))
            g.add(pool.affine_select(out=ident_h[:, :], in_=ident_h[:, :], compare_op=ALU.not_equal, fill=1.0,
                                     base=0, pattern=[[-1, P]], channel_multiplier=1))
            g.add(pool.iota(iota_c[:, :], pattern=[[1, NT * WIN]], base=0, channel_multiplier=0))
            g.add(pool.iota(win_i[:, :], pattern=[[1, WIN]], base=0, channel_multiplier=0,
                            allow_small_or_imprecise_dtypes=True))
            g.add(pool.memset(ones_h[:, :], 1.0))
            g.add(pool.memset(ones_row[:, :], 1.0))
            pool.memset(adj[:, 10:20, :].rearrange("p k n -> p (k n)").bitcast(I32), 0).then_inc(adj_zero, 1)
            phase_end(pool, 1)
            for n in range(2, 7):
                phase_end(pool, n)

            def gather(i, u):
                s = 2 * i + u
                pool.wait_ge(g_loaded[u], 64 * i)
                pool.wait_ge(z_sum[u], i)
                pool.sem_inc(gather_mark, 1)
                pool.tensor_copy(idx[:, u, :], src_idx[:, bass.ds(s, 1), :].rearrange("p a j -> p (a j)")).then_inc(idx_ready, 1)
                pool.wait_ge(idx_ready, s + 1)
                pool.sem_inc(gather_mark, 1)
                for j in range(J):
                    pool.indirect_dma_start(out=g_x[u][:, j * D:(j + 1) * D], out_offset=None, in_=xa_d[:, :],
                                            in_offset=bass.IndirectOffsetOnAxis(ap=idx[:, u, j:j + 1], axis=0)
                                            ).then_inc(g_loaded[u], 16)

            with pool.Fori(0, NB // 2) as i:
                gather(i, 0)
                gather(i, 1)
            for n in range(7, 13):
                phase_end(pool, n)

        @block.tensor
        def _(pe):
            pe.wait_ge(prep_ready, 1)
            pe.wait_ge(g_own, 9)
            n = 0
            for half in range(2):
                for a, v in enumerate((p_comb, p_lo, p_drel, p_src)):
                    if n >= 2:
                        pe.wait_ge(prep_out, n - 1)
                    for j in range(J):
                        c0 = 512 * half + j * P
                        last = pe.transpose(ps[:, n % 2, GRP * j:GRP * (j + 1)], v[0:GRP, c0:c0 + P],
                                            ident_f[0:GRP, 0:GRP])
                    last.then_inc(prep_t, 1)
                    n += 1
            phase_end(pe, 1)

            def counts(i, u):
                s = 2 * i + u
                b = pe.value_load(base_row[0:1, bass.ds(s, 1)], min_val=0, max_val=N - 1)
                pe.wait_ge(oh_ready[u], i + 1)
                pe.wait_ge(adj_written[u], i)
                for h, (k0, k1) in enumerate(((0, H0), (H0, NT))):
                    for j in range(J):
                        last = pe.matmul(ps[:, 2 * u + h, 0:(k1 - k0) * WIN], oh_src[u][:, j, :],
                                         oh_dst[u][:, j, k0 * WIN:k1 * WIN], start=(j == 0), stop=False)
                last.then_inc(oh_used[u], 1)
                pe.wait_ge(adj_written[1 - u], i + u)
                for h, (k0, k1) in enumerate(((0, H0), (H0, NT))):
                    last = pe.matmul(ps[:, 2 * u + h, 0:(k1 - k0) * WIN], ident_h[:, :],
                                     adj[:, k0:k1, bass.ds(b, WIN)], start=False, stop=True)
                last.then_inc(cnt_ready[u], 1)

            with pe.Fori(0, NB // 2) as i:
                counts(i, 0)
                counts(i, 1)
            phase_end(pe, 2)

            for k in range(NT):
                for q in range(NT):
                    last = pe.matmul(ps[:, 7, k:k + 1], adj[:, q, k * P:(k + 1) * P], ones_h[:, 0:1],
                                     start=(q == 0), stop=(q == NT - 1))
            last.then_inc(deg_ready, 1)

            def aggregate(call, i, u, c0, nt):
                w = nt * P
                pe.wait_ge(agg_out, call * NC + 2 * i)
                for k in range(NT):
                    for q in range(3):
                        last = pe.matmul(ps[:, u, 0:w], parts[q][:, k, :], adj[:, k, bass.ds(c0, w)],
                                         start=(k == 0 and q == 0), stop=(k == NT - 1 and q == 2))
                last.then_inc(agg_ready, 1)

            def own_t(call, c, nt):
                pe.wait_ge(self_out, call * NC + c)
                for j in range(nt):
                    for q in range(3):
                        last = pe.matmul(ps[:, 2, j * P:(j + 1) * P],
                                         parts[q][:, bass.ds(CH * c + j, 1), :].rearrange("p a d -> p (a d)"),
                                         ident_h[:, :], start=(q == 0), stop=(q == 2))
                last.then_inc(self_ready, 1)

            def layer(call, linear):
                with pe.Fori(0, PAIRS) as i:
                    for u in range(2):
                        aggregate(call, i, u, (2 * i + u) * CH * P, CH)
                        if u == 0:
                            own_t(call, 2 * i, CH)
                    linear(call, 2 * i, CH)
                    own_t(call, 2 * i + 1, CH)
                    linear(call, 2 * i + 1, CH)
                k0, nt = CHUNKS[-1]
                aggregate(call, PAIRS, 0, k0 * P, nt)
                own_t(call, NFULL, nt)
                linear(call, NFULL, nt)

            def sage(call, c, nt):
                n0 = call * NC
                pe.wait_ge(selfs_ready, n0 + c)
                pe.wait_ge(lin_used, n0 + c)
                pe.wait_ge(self_out, n0 + c + 1)
                for j in range(nt):
                    pe.matmul(ps[:, 3, j * D:(j + 1) * D], self_t[:, j * P:(j + 1) * P], w_a[:, :],
                              start=True, stop=False)
                    last = pe.matmul(ps[:, 3, j * D:(j + 1) * D], ones_row[:, :], bias_row[:, :],
                                     start=False, stop=True)
                pe.wait_ge(agg_out, n0 + c + 1)
                for j in range(nt):
                    last = pe.matmul(ps[:, 4, j * D:(j + 1) * D], agg_t[:, j * P:(j + 1) * P], w_b[:, :],
                                     start=True, stop=True)
                last.then_inc(lin_ready, 1)

            pe.wait_ge(loads[4], 48)
            phase_end(pe, 3)
            layer(0, sage)
            phase_end(pe, 4)
            pe.wait_ge(loads[4], 96)
            pe.wait_ge(low_ready, 2 * NC)
            layer(1, sage)
            phase_end(pe, 5)

            pe.wait_ge(loads[4], 128)
            for c, (k0, nt) in enumerate(CHUNKS):
                if c >= 2:
                    pe.wait_ge(proj_ts, c - 1)
                for j in range(nt):
                    last = pe.transpose(ps[:, c % 2, j * P:(j + 1) * P], xn[:, k0 + j, :], ident_f[:, :])
                last.then_inc(proj_t, 1)
                pe.wait_ge(proj_ts, c + 1)
                if c >= 2:
                    for h in range(2):
                        pe.wait_ge(proj_out[h], c - 1)
                for h, w in enumerate((w_a, w_b)):
                    for j in range(nt):
                        last = pe.matmul(ps[:, 2 + 2 * (c % 2) + h, j * D:(j + 1) * D],
                                         arena[:, 512 * (c % 2) + j * P:512 * (c % 2) + (j + 1) * P], w[:, :],
                                         start=True, stop=True)
                last.then_inc(proj_ready, 1)
            phase_end(pe, 6)

            pe.wait_ge(loads[6], 80)

            def inputs_t(i, u):
                pe.wait_ge(ec_loaded[u], 16 * (i + 1))
                pe.wait_ge(ec_onehot[u], i + 1)
                pe.wait_ge(ect_out[u], i)
                for j in range(J):
                    last = pe.transpose(ps[0:KE, u, j * P:(j + 1) * P], ec[u][:, j, :], ident_f[:, :])
                last.then_inc(ec_used[u], 1)

            def hidden(i, u):
                pe.wait_ge(ect_out[u], i + 1)
                pe.wait_ge(w_loaded[u], 16 * (i + 1))
                pe.wait_ge(z_sum[u], i)
                for j in range(J):
                    last = pe.matmul(ps[:, 2 + u, j * P:(j + 1) * P], ec_t[u][0:KE, j * P:(j + 1) * P],
                                     w_e[u][0:KE, :], start=True, stop=True)
                last.then_inc(z_ready[u], 1)

            def hidden_t(i, u):
                pe.wait_ge(z_sum[u], i + 1)
                pe.wait_ge(h_ready[1 - u], i + u)
                for j in range(J):
                    last = pe.transpose(ps[:, 4, j * P:(j + 1) * P], z_e[u][:, j * P:(j + 1) * P], ident_f[:, :])
                last.then_inc(zt_ready[u], 1)

            def messages(i, u):
                pe.wait_ge(h_ready[u], i + 1)
                pe.wait_ge(m_sum[u], i)
                for j in range(J):
                    last = pe.matmul(ps[:, 5 + u, j * P:(j + 1) * P], h_t[u][:, j * P:(j + 1) * P], w_b[:, :],
                                     start=True, stop=True)
                last.then_inc(m_ready[u], 1)

            def window(i, u):
                pe.wait_ge(msg_ready[u], i + 1)
                pe.wait_ge(win_added, 2 * i + u)
                for j in range(J):
                    last = pe.matmul(ps[:, 7, 0:WIN], msg[u][:, j * P:(j + 1) * P], oh_e[u][:, j, :],
                                     start=(j == 0), stop=(j == J - 1))
                last.then_inc(win_ready[u], 1)

            def step(i, u, i2):
                hidden_t(i, u)
                inputs_t(i2, 1 - u)
                messages(i, u)
                hidden(i2, 1 - u)
                window(i, u)

            inputs_t(0, 0)
            hidden(0, 0)
            with pe.Fori(0, NB // 2 - 1) as i:
                step(i, 0, i)
                step(i, 1, i + 1)
            i = NB // 2 - 1
            step(i, 0, i)
            hidden_t(i, 1)
            messages(i, 1)
            window(i, 1)
            phase_end(pe, 7)

            pe.wait_ge(loads[7], 80)
            for c, (k0, nt) in enumerate(CHUNKS):
                if c >= 2:
                    pe.wait_ge(lin_used, 2 * NC + c - 1)
                for j in range(nt):
                    pe.matmul(ps[:, c % 2, j * D:(j + 1) * D], agg_all[:, (k0 + j) * P:(k0 + j + 1) * P], w_a[:, :],
                              start=True, stop=False)
                    last = pe.matmul(ps[:, c % 2, j * D:(j + 1) * D], ones_row[:, :], bias_row[:, :],
                                     start=False, stop=True)
                last.then_inc(lin_ready, 1)
            phase_end(pe, 8)
            pe.wait_ge(loads[8], 64)
            pe.transpose(ps[:, 7, 0:P], w_b[:, :], ident_f[:, :]).then_inc(proj_t, 1)
            phase_end(pe, 9)

            def gcn(call, c, nt):
                pe.wait_ge(lin_used, lin_base[call] + c)
                pe.wait_ge(agg_out, call * NC + c + 1)
                for j in range(nt):
                    last = pe.matmul(ps[:, 4, j * D:(j + 1) * D], agg_t[:, j * P:(j + 1) * P], w_c[:, :],
                                     start=True, stop=True)
                last.then_inc(lin_ready, 1)

            layer(2, gcn)
            phase_end(pe, 10)
            pe.wait_ge(loads[9], 80)
            pe.transpose(ps[:, 7, 0:P], w_b[:, :], ident_f[:, :]).then_inc(proj_t, 1)
            phase_end(pe, 11)

            def gin(call, c, nt):
                pe.wait_ge(gin_out, c)
                pe.wait_ge(agg_out, call * NC + c + 1)
                pe.matmul(ps[:, 4, 0:nt * P], w_c[:, :], agg_t[:, 0:nt * P], start=True, stop=True
                          ).then_inc(gin_ready, 1)

            layer(3, gin)
            phase_end(pe, 12)
            pe.wait_ge(twice_ready, 1)
            for c, (k0, nt) in enumerate(CHUNKS):
                pe.wait_ge(bn_relu, c + 1)
                if c >= 2:
                    pe.wait_ge(out_ready, c - 1)
                for j in range(nt):
                    k = k0 + j
                    for q in range(3):
                        pe.matmul(ps[:, c % 2, j * D:(j + 1) * D], ident_h[:, :], parts[q][:, k, :],
                                  start=(q == 0), stop=False)
                    last = pe.matmul(ps[:, c % 2, j * D:(j + 1) * D], agg_all[:, k * P:(k + 1) * P], ident_f[:, :],
                                     start=False, stop=True)
                last.then_inc(fin_ready, 1)

        @block.scalar
        def _(act):
            for n in range(8):
                half, a = n // 4, n % 4
                dst = (comb, lo_f, drel, src_idx)[a]
                act.wait_ge(prep_t, n + 1)
                act.activation(dst[:, GRP * half:GRP * (half + 1), :],
                               ps[:, n % 2, 0:GRP * J].rearrange("p (j s) -> p s j", j=J), ACT.Copy
                               ).then_inc(prep_out, 1)
            phase_end(act, 1)

            def to_adj(i, u):
                s = 2 * i + u
                b = act.value_load(base_row[0:1, bass.ds(s, 1)], min_val=0, max_val=N - 1)
                act.wait_ge(cnt_ready[u], i + 1)
                act.activation(adj[:, 0:H0, bass.ds(b, WIN)],
                               ps[:, 2 * u, 0:H0 * WIN].rearrange("p (k w) -> p k w", w=WIN), ACT.Copy)
                act.activation(adj[:, H0:NT, bass.ds(b, WIN)],
                               ps[:, 2 * u + 1, 0:(NT - H0) * WIN].rearrange("p (k w) -> p k w", w=WIN), ACT.Copy
                               ).then_inc(adj_written[u], 1)

            with act.Fori(0, NB // 2) as i:
                to_adj(i, 0)
                to_adj(i, 1)
            phase_end(act, 2)

            def split(call, scale=None):
                for c, (k0, nt) in enumerate(CHUNKS):
                    if scale is None:
                        act.activation(parts[0][:, k0:k0 + nt, :], xn[:, k0:k0 + nt, :], ACT.Copy).then_inc(hi_ready, 1)
                    else:
                        for k in range(k0, k0 + nt):
                            last = act.activation(parts[0][:, k, :], xn[:, k, :], ACT.Copy, scale=scale[:, k:k + 1])
                        last.then_inc(hi_ready, 1)
                for c, (k0, nt) in enumerate(CHUNKS):
                    act.wait_ge(res_ready, call * NC + c + 1)
                    act.activation(parts[1][:, k0:k0 + nt, :], res[c % 2][:, 0:nt, :], ACT.Copy).then_inc(mid_ready, 1)

            roots = [0]

            def root(nt):
                roots[0] += 1
                act.wait_ge(var_ready, roots[0])
                act.activation(std[:, 0:nt], mv[:, 0:nt, 1], ACT.Sqrt, bias=cols[:, 7:8]).then_inc(std_ready, 1)

            act.wait_ge(loads[3], 32)
            split(0)
            act.wait_ge(deg_ready, 2)
            act.activation(std_deg[:, :], dinv[:, :], ACT.Sqrt).then_inc(deg_ready, 1)
            phase_end(act, 3)

            def sage(call, norm):
                for c, (k0, nt) in enumerate(CHUNKS):
                    n = call * NC + c
                    act.wait_ge(self_ready, n + 1)
                    act.wait_ge(lin_ready, n)
                    act.activation(self_t[:, 0:nt * P], ps[:, 2, 0:nt * P], ACT.Copy).then_inc(self_out, 1)
                    act.wait_ge(lin_ready, n + 1)
                    act.wait_ge(node_used, n)
                    act.activation(node[:, 0:nt, :], ps[:, 3, 0:nt * D].rearrange("p (j d) -> p j d", d=D),
                                   ACT.Copy).then_inc(selfs_ready, 1)
                    if norm:
                        root(nt)

            sage(0, False)
            phase_end(act, 4)
            split(1)
            sage(1, True)
            phase_end(act, 5)
            for c, (k0, nt) in enumerate(CHUNKS):
                act.wait_ge(proj_t, c + 1)
                if c >= 2:
                    act.wait_ge(proj_ready, c - 1)
                act.activation(arena[:, 512 * (c % 2):512 * (c % 2) + nt * P], ps[:, c % 2, 0:nt * P], ACT.Copy
                               ).then_inc(proj_ts, 1)
                act.wait_ge(proj_ready, c + 1)
                if c >= 2:
                    act.wait_ge(stored[c % 2], 32 * (c // 2))
                act.activation(arena[:, 1024 + 1024 * (c % 2):1024 + 1024 * (c % 2) + nt * D],
                               ps[:, 2 + 2 * (c % 2), 0:nt * D], ACT.Copy).then_inc(proj_out[0], 1)
            phase_end(act, 6)

            act.wait_ge(loads[6], 80)

            def inputs_out(i, u):
                act.wait_ge(ec_used[u], i + 1)
                act.wait_ge(z_ready[u], i)
                act.activation(ec_t[u][0:KE, :], ps[0:KE, u, :], ACT.Copy).then_inc(ect_out[u], 1)

            def hidden_relu(i, u):
                act.wait_ge(zt_ready[u], i + 1)
                act.wait_ge(m_ready[u], i)
                act.activation(h_t[u], ps[:, 4, :], ACT.Relu, bias=cols[:, 0:1]).then_inc(h_ready[u], 1)

            def message_relu(i, u):
                act.wait_ge(m_sum[u], i + 1)
                act.activation(msg[u], msg[u], ACT.Relu).then_inc(msg_ready[u], 1)

            def step(i, u, i2):
                hidden_relu(i, u)
                inputs_out(i2, 1 - u)
                message_relu(i, u)

            inputs_out(0, 0)
            with act.Fori(0, NB // 2 - 1) as i:
                step(i, 0, i)
                step(i, 1, i + 1)
            i = NB // 2 - 1
            step(i, 0, i)
            hidden_relu(i, 1)
            message_relu(i, 1)
            phase_end(act, 7)
            for c, (k0, nt) in enumerate(CHUNKS):
                act.wait_ge(lin_ready, 2 * NC + c + 1)
                act.wait_ge(node_used, 2 * NC + c)
                act.activation(node[:, 0:nt, :], ps[:, c % 2, 0:nt * D].rearrange("p (j d) -> p j d", d=D),
                               ACT.Relu).then_inc(lin_used, 1)
                root(nt)
                root(nt)
            phase_end(act, 8)
            split(2, scale=dinv)
            act.wait_ge(proj_t, NC + 1)
            act.activation(w_c[:, :], ps[:, 7, 0:P], ACT.Copy)
            phase_end(act, 9)
            for c, (k0, nt) in enumerate(CHUNKS):
                act.wait_ge(self_ready, 2 * NC + c + 1)
                act.wait_ge(agg_out, 2 * NC + c)
                act.activation(self_t[:, 0:nt * P], ps[:, 2, 0:nt * P], ACT.Copy).then_inc(self_out, 1)
                root(nt)
                root(nt)
            phase_end(act, 10)
            split(3)
            act.wait_ge(proj_t, NC + 2)
            act.activation(w_c[:, :], ps[:, 7, 0:P], ACT.Copy)
            phase_end(act, 11)
            for c, (k0, nt) in enumerate(CHUNKS):
                act.wait_ge(self_ready, 3 * NC + c + 1)
                act.wait_ge(agg_out, 3 * NC + c)
                act.activation(self_t[:, 0:nt * P], ps[:, 2, 0:nt * P], ACT.Copy, scale=cols[:, 4:5]).then_inc(self_out, 1)
                act.wait_ge(gin_ready, c + 1)
                act.activation(agg_all[:, k0 * P:(k0 + nt) * P], ps[:, 4, 0:nt * P], ACT.Identity,
                               bias=cols[:, 0:1]).then_inc(gin_out, 1)
            root(1)
            phase_end(act, 12)
            for c, (k0, nt) in enumerate(CHUNKS):
                act.activation(agg_all[:, k0 * P:(k0 + nt) * P], agg_all[:, k0 * P:(k0 + nt) * P], ACT.Relu,
                               bias=cols[:, 6:7], scale=cols[:, 5:6]).then_inc(bn_relu, 1)
            for c, (k0, nt) in enumerate(CHUNKS):
                root(nt)

        @block.vector
        def _(dve):
            v = Count(dve, v_own)
            dve.memset(cols[:, 7:8], EPS)
            dve.wait_ge(loads[0], 48)
            v.add(dve.tensor_scalar(hi_i[0:GRP, :], raw_src[0:GRP, :], 7, None, ALU.arith_shift_right))
            v.add(dve.tensor_scalar(lo_i[0:GRP, :], raw_src[0:GRP, :], P - 1, None, ALU.bitwise_and))
            v.add(dve.tensor_copy(p_src[0:GRP, :], raw_src[0:GRP, :]))
            dve.wait_ge(loads[1], 48)
            for half in range(2):
                h = slice(512 * half, 512 * half + 512)
                v.add(dve.tensor_scalar(p_drel[0:GRP, h], raw_dst[0:GRP, h],
                                        raw_dst[0:GRP, 512 * half:512 * half + 1], None, ALU.subtract))
            v.wait()
            v.add(dve.tensor_copy(p_lo[0:GRP, :], lo_i[0:GRP, :]))
            dve.scalar_tensor_tensor(out=p_comb[0:GRP, :], in0=hi_i[0:GRP, :], scalar=float(WIN),
                                     in1=p_drel[0:GRP, :], op0=ALU.mult, op1=ALU.add).then_inc(prep_ready, 1)
            dve.memset(adj[:, 0:10, :].rearrange("p k n -> p (k n)").bitcast(I32), 0)
            dve.wait_ge(prep_t, 8)
            dve.memset(prep.bitcast(I32), 0)
            dve.wait_ge(prep_out, 8)
            for a in (comb, drel):
                dve.memset(a[:, NB - 1, 0:DUP // P], -1.0)
                dve.memset(a[0:DUP % P, NB - 1, DUP // P:DUP // P + 1], -1.0)
            dve.wait_ge(adj_zero, 1)
            phase_end(dve, 1)

            def onehots(i, u):
                s = 2 * i + u
                dve.wait_ge(oh_used[u], i)
                for j in range(J):
                    dve.tensor_scalar(oh_src[u][:, j, :], iota_c[:, 0:P], lo_f[:, bass.ds(s, 1), j], None, ALU.is_equal)
                for j in range(J):
                    last = dve.tensor_scalar(oh_dst[u][:, j, :], iota_c[:, :], comb[:, bass.ds(s, 1), j], None, ALU.is_equal)
                last.then_inc(oh_ready[u], 1)

            with dve.Fori(0, NB // 2) as i:
                onehots(i, 0)
                onehots(i, 1)
            phase_end(dve, 2)

            def split(call, scale=None):
                def low(c):
                    k0, nt = CHUNKS[c]
                    dve.wait_ge(mid_ready, call * NC + c + 1)
                    dve.tensor_tensor(parts[2][:, k0:k0 + nt, :], res[c % 2][:, 0:nt, :], parts[1][:, k0:k0 + nt, :],
                                      ALU.subtract).then_inc(low_ready, 1)

                for c, (k0, nt) in enumerate(CHUNKS):
                    dve.wait_ge(hi_ready, call * NC + c + 1)
                    if c >= 2:
                        dve.wait_ge(low_ready, call * NC + c - 1)
                    if scale is None:
                        last = dve.tensor_tensor(res[c % 2][:, 0:nt, :], xn[:, k0:k0 + nt, :],
                                                 parts[0][:, k0:k0 + nt, :], ALU.subtract)
                    else:
                        for j in range(nt):
                            last = dve.scalar_tensor_tensor(out=res[c % 2][:, j, :], in0=xn[:, k0 + j, :],
                                                            scalar=scale[:, k0 + j:k0 + j + 1], in1=parts[0][:, k0 + j, :],
                                                            op0=ALU.mult, op1=ALU.subtract)
                    last.then_inc(res_ready, 1)
                    if c:
                        low(c - 1)
                low(NC - 1)

            roots = [0]

            def layernorm(src, dst, nt, done=None):
                for j in range(nt):
                    v.add(dve.bn_stats(stats[:, j, :], src[:, j, :]))
                v.wait()
                for j in range(nt):
                    last = dve.bn_aggr(mv[:, j, :], stats[:, j, :])
                last.then_inc(var_ready, 1)
                roots[0] += 1
                dve.wait_ge(std_ready, roots[0])
                v.add(dve.reciprocal(rstd[:, 0:nt], std[:, 0:nt]))
                v.wait()
                for j in range(nt):
                    last = dve.tensor_scalar(dst[:, j, :], src[:, j, :], mv[:, j, 0:1], rstd[:, j:j + 1],
                                             ALU.subtract, ALU.mult)
                    if done is None or j < nt - 1:
                        v.add(last)
                if done is not None:
                    last.then_inc(done, 1)
                else:
                    v.wait()

            def affine(a, nt):
                for op, b in ((ALU.mult, gamma_b), (ALU.add, beta_b)):
                    v.add(dve.tensor_tensor(a[:, 0:nt, :], a[:, 0:nt, :],
                                            b[:, :].rearrange("p (a d) -> p a d", a=1).broadcast_to([P, nt, D]), op))
                    v.wait()

            dve.wait_ge(loads[3], 32)
            split(0)
            dve.wait_ge(deg_ready, 1)
            v.add(dve.tensor_scalar(inv_deg[:, :], ps[:, 7, 0:NT], 1.0, None, ALU.max))
            dve.tensor_scalar(dinv[:, :], ps[:, 7, 0:NT], 1.0, None, ALU.add).then_inc(deg_ready, 1)
            v.wait()
            v.add(dve.reciprocal(inv_deg[:, :], inv_deg[:, :]))
            dve.wait_ge(deg_ready, 3)
            dve.reciprocal(dinv[:, :], std_deg[:, :])
            phase_end(dve, 3)

            def sage(call, final):
                for c, (k0, nt) in enumerate(CHUNKS):
                    n = call * NC + c
                    dve.wait_ge(agg_ready, n + 1)
                    dve.wait_ge(lin_ready, n)
                    dve.tensor_copy(agg_t[:, 0:nt * P], ps[:, c % 2, 0:nt * P]).then_inc(agg_out, 1)
                    dve.wait_ge(lin_ready, n + 1)
                    dve.wait_ge(selfs_ready, n + 1)
                    dst = node if final else xn[:, k0:k0 + nt, :]
                    for j in range(nt):
                        last = dve.scalar_tensor_tensor(out=dst[:, j, :], in0=ps[:, 4, j * D:(j + 1) * D],
                                                        scalar=inv_deg[:, k0 + j:k0 + j + 1], in1=node[:, j, :],
                                                        op0=ALU.mult, op1=ALU.add)
                    last.then_inc(lin_used, 1)
                    dve.wait_ge(lin_used, n + 1)
                    if final:
                        v.add(dve.tensor_tensor(node[:, 0:nt, :], node[:, 0:nt, :], xn[:, k0:k0 + nt, :], ALU.add))
                        v.wait()
                        layernorm(node, xn[:, k0:k0 + nt, :], nt, done=node_used)
                    else:
                        dve.tensor_scalar(dst, dst, 0.0, None, ALU.max).then_inc(node_used, 1)

            sage(0, False)
            phase_end(dve, 4)
            split(1)
            dve.wait_ge(loads[3], 64)
            sage(1, True)
            phase_end(dve, 5)
            for c, (k0, nt) in enumerate(CHUNKS):
                dve.wait_ge(proj_ready, c + 1)
                if c >= 2:
                    dve.wait_ge(stored[c % 2], 32 * (c // 2))
                b0 = 1536 + 1024 * (c % 2)
                dve.tensor_copy(arena[:, b0:b0 + nt * D], ps[:, 3 + 2 * (c % 2), 0:nt * D]).then_inc(proj_out[1], 1)
            phase_end(dve, 6)

            v.add(dve.memset(agg_all, 0.0))
            dve.wait_ge(loads[6], 80)
            dve.wait_ge(v_own, v.n)

            def onehot_e(i, u):
                s = 2 * i + u
                dve.wait_ge(ec_used[u], i)
                dve.wait_ge(win_ready[u], i)
                rel = drel[:, bass.ds(s, 1), :].rearrange("p a j -> p j a").broadcast_to([P, J, WIN])
                w = win_i[:, :].rearrange("p (a w) -> p a w", a=1).broadcast_to([P, J, WIN])
                dve.tensor_tensor(ec[u][:, :, R:KE], w, rel, ALU.is_equal).then_inc(ec_onehot[u], 1)
                dve.tensor_tensor(oh_e[u], w, rel, ALU.is_equal).then_inc(oh_e_ready[u], 1)

            def add_gathered(i, u):
                dve.wait_ge(z_ready[u], i + 1)
                dve.wait_ge(g_loaded[u], 64 * (i + 1))
                dve.wait_ge(zt_ready[u], i)
                dve.tensor_tensor(z_e[u], ps[:, 2 + u, :], g_x[u], ALU.add).then_inc(z_sum[u], 1)

            def add_bias(i, u):
                dve.wait_ge(m_ready[u], i + 1)
                dve.wait_ge(win_ready[u], i)
                dve.tensor_tensor(msg[u].rearrange("p (j d) -> p j d", d=D), ps[:, 5 + u, :].rearrange("p (j d) -> p j d", d=D),
                                  bias_b[:, :].rearrange("p (a d) -> p a d", a=1).broadcast_to([P, J, D]),
                                  ALU.add).then_inc(m_sum[u], 1)

            def add_window(i, u):
                s = 2 * i + u
                b = dve.value_load(base_row[0:1, bass.ds(s, 1)], min_val=0, max_val=N - 1)
                dve.wait_ge(win_ready[u], i + 1)
                dve.wait_ge(win_added, s)
                dve.tensor_tensor(agg_all[:, bass.ds(b, WIN)], ps[:, 7, 0:WIN], agg_all[:, bass.ds(b, WIN)], ALU.add
                                  ).then_inc(win_added, 1)

            def step(i, u, i2):
                onehot_e(i2, 1 - u)
                add_bias(i, u)
                add_gathered(i2, 1 - u)
                add_window(i, u)

            onehot_e(0, 0)
            add_gathered(0, 0)
            with dve.Fori(0, NB // 2 - 1) as i:
                step(i, 0, i)
                step(i, 1, i + 1)
            i = NB // 2 - 1
            step(i, 0, i)
            add_bias(i, 1)
            add_window(i, 1)
            phase_end(dve, 7)

            dve.wait_ge(loads[7], 80)
            x1 = arena[:, 0:3200].rearrange("p (k d) -> p k d", d=D)
            for c, (k0, nt) in enumerate(CHUNKS):
                dve.wait_ge(lin_used, 2 * NC + c + 1)
                v.add(dve.tensor_tensor(node[:, 0:nt, :], node[:, 0:nt, :], x1[:, k0:k0 + nt, :], ALU.add))
                v.wait()
                layernorm(node, node, nt)
                affine(node, nt)
                v.add(dve.tensor_tensor(node[:, 0:nt, :], node[:, 0:nt, :], x1[:, k0:k0 + nt, :], ALU.add))
                v.wait()
                layernorm(node, xn[:, k0:k0 + nt, :], nt, done=node_used)
            phase_end(dve, 8)
            split(2, scale=dinv)
            phase_end(dve, 9)
            for c, (k0, nt) in enumerate(CHUNKS):
                n = 2 * NC + c
                dve.wait_ge(agg_ready, n + 1)
                dve.wait_ge(lin_ready, 3 * NC + c)
                dve.wait_ge(self_out, n + 1)
                dve.tensor_tensor(agg_t[:, 0:nt * P], ps[:, c % 2, 0:nt * P], self_t[:, 0:nt * P], ALU.add).then_inc(agg_out, 1)
                dve.wait_ge(lin_ready, 3 * NC + c + 1)
                for j in range(nt):
                    last = dve.scalar_tensor_tensor(out=node[:, j, :], in0=ps[:, 4, j * D:(j + 1) * D],
                                                    scalar=dinv[:, k0 + j:k0 + j + 1], in1=bias_b[:, :],
                                                    op0=ALU.mult, op1=ALU.add)
                last.then_inc(lin_used, 1)
                dve.wait_ge(lin_used, 3 * NC + c + 1)
                layernorm(node, node, nt)
                affine(node, nt)
                v.add(dve.tensor_tensor(node[:, 0:nt, :], node[:, 0:nt, :], xn[:, k0:k0 + nt, :], ALU.add))
                v.wait()
                layernorm(node, xn[:, k0:k0 + nt, :], nt)
            phase_end(dve, 10)
            split(3)
            dve.wait_ge(loads[9], 80)
            dve.tensor_scalar(cols[:, 4:5], cols[:, 3:4], 1.0, None, ALU.add)
            phase_end(dve, 11)
            for c, (k0, nt) in enumerate(CHUNKS):
                n = 3 * NC + c
                dve.wait_ge(agg_ready, n + 1)
                dve.wait_ge(gin_ready, c)
                dve.wait_ge(self_out, n + 1)
                dve.tensor_tensor(agg_t[:, 0:nt * P], ps[:, c % 2, 0:nt * P], self_t[:, 0:nt * P], ALU.add).then_inc(agg_out, 1)
                dve.wait_ge(gin_out, c + 1)
                w = nt * P if nt == CH else TAIL
                v.add(dve.bn_stats(stats[:, c, :], agg_all[:, k0 * P:k0 * P + w]))
            v.wait()
            dve.bn_aggr(mv[:, 0, :], stats[:, 0:NC, :]).then_inc(var_ready, 1)
            roots[0] += 1
            dve.wait_ge(std_ready, roots[0])
            v.add(dve.reciprocal(rstd[:, 0:1], std[:, 0:1]))
            v.wait()
            v.add(dve.tensor_tensor(cols[:, 5:6], rstd[:, 0:1], cols[:, 1:2], ALU.mult))
            v.wait()
            v.add(dve.tensor_tensor(rstd[:, 1:2], cols[:, 5:6], mv[:, 0, 0:1], ALU.mult))
            v.wait()
            dve.tensor_tensor(cols[:, 6:7], cols[:, 2:3], rstd[:, 1:2], ALU.subtract)
            phase_end(dve, 12)
            dve.tensor_scalar(ident_h[:, :], ident_h[:, :], 2.0, None, ALU.mult).then_inc(twice_ready, 1)
            for c, (k0, nt) in enumerate(CHUNKS):
                dve.wait_ge(fin_ready, c + 1)
                layernorm(ps[:, c % 2, :].rearrange("p (j d) -> p j d", d=D), xn[:, k0:k0 + nt, :], nt, done=out_ready)


_INS = ["x", "src", "dst", "edge_attr_64", "L0_gnn_W_self1", "L0_gnn_W_neigh1", "L0_gnn_b1", "L0_gnn_W_self2",
        "L0_gnn_W_neigh2", "L0_gnn_b2", "L1_gnn_W1", "L1_gnn_b1", "L1_gnn_W2", "L1_gnn_b2", "L1_gnn_Wn", "L1_gnn_bn",
        "L1_gnn_gamma", "L1_gnn_beta", "L2_gnn_W", "L2_gnn_b", "L2_gnn_gamma", "L2_gnn_beta", "L3_gnn_W", "L3_gnn_b",
        "L3_gnn_gamma", "L3_gnn_beta", "L3_gnn_gin_eps"]


def kernel(**inputs):
    import numpy as _np
    import concourse.bacc as _bacc
    from concourse import mybir as _mybir
    from concourse.bass_utils import run_bass_kernel_spmd as _run

    nc = _bacc.Bacc("TRN2", target_bir_lowering=False, num_devices=1)
    arrays, t = {}, {}
    for name in _INS:
        a = _np.ascontiguousarray(inputs[name])
        arrays[f"in_{name}"] = a
        t[name] = nc.dram_tensor(f"in_{name}", a.shape, _mybir.dt.from_np(a.dtype), kind="ExternalInput").ap()
    out = nc.dram_tensor("out_x", (N, D), F32, kind="ExternalOutput").ap()
    x1_d = nc.dram_tensor("x1_spill", (NP, D), F32, kind="Internal").ap()
    xa_d = nc.dram_tensor("x1_w1a", (NP, D), F32, kind="Internal").ap()
    xb_d = nc.dram_tensor("x1_w1b", (NP, D), F32, kind="Internal").ap()
    build(nc, t, out, x1_d, xa_d, xb_d)
    r = _run(nc, [arrays], core_ids=[0])
    return r.results[0]["out_x"]
```

```python
from contextlib import ExitStack

import concourse.bass as bass
from concourse import mybir

F32 = mybir.dt.float32
BF16 = mybir.dt.bfloat16
I32 = mybir.dt.int32
I16 = mybir.dt.int16
ALU = mybir.AluOpType
ACT = mybir.ActivationFunctionType

P = 128
N = 3125
E = 100000
D = 128
R = 64
EPS = 1e-5
NT = (N + P - 1) // P
NP = NT * P
TAIL = N - (NT - 1) * P
J = 4
BLK = J * P
NB = (E + BLK - 1) // BLK
GRP = NB // 2
DUP = NB * BLK - E
WIN = 24
H0 = 13
CH = 4
CHUNKS = [(c, min(CH, NT - c)) for c in range(0, NT, CH)]
NFULL = NT // CH
PAIRS = NFULL // 2
NC = len(CHUNKS)
PAIR = [(k, min(2 * CH, NT - k)) for k in range(0, NT, 2 * CH)]
SLOTS = 4
assert NB % SLOTS == 0 and NFULL % 2 == 0 and GRP <= P


def build(nc, t, out, x1_d, xa_d, xb_d):
    ctx = ExitStack()
    with ctx:
        def sb(name, shape, dt):
            return ctx.enter_context(nc.sbuf_tensor(name, shape, dt))

        def sem(name):
            return ctx.enter_context(nc.semaphore(name))

        adj = sb("adj", [P, NT, NP], BF16)
        arena = sb("arena", [P, 10112], F32)
        src_idx = sb("src_idx", [P, NB, J], I32)
        drel = sb("drel", [P, NB, J], F32)
        base_row = sb("base_row", [1, NB], I32)
        w_a = sb("w_a", [P, D], F32)
        w_b = sb("w_b", [P, D], F32)
        w_c = sb("w_c", [P, D], F32)
        bias_b = sb("bias_b", [P, D], F32)
        gamma_b = sb("gamma_b", [P, D], F32)
        beta_b = sb("beta_b", [P, D], F32)
        ident_f = sb("ident_f", [P, P], F32)
        ident_h = sb("ident_h", [P, P], BF16)
        ones_h = sb("ones_h", [P, 2], BF16)
        inv_deg = sb("inv_deg", [P, NT], F32)
        dinv = sb("dinv", [P, NT], F32)
        std_deg = sb("std_deg", [P, NT], F32)
        stats = sb("stats", [P, CH * 2, 6], F32)
        mv = sb("mv", [P, 2 * CH, 2], F32)
        std = sb("std", [P, 2 * CH], F32)
        rstd = sb("rstd", [P, 2 * CH], F32)
        cols = sb("cols", [P, 8], F32)
        idx = sb("idx", [P, SLOTS, J], I32)
        win_i = sb("win_i", [P, WIN], F32)

        parts = [arena[:, 1600 * q:1600 * (q + 1)].bitcast(BF16).rearrange("p (k d) -> p k d", d=D)
                 for q in range(3)]
        xn = arena[:, 4800:8000].rearrange("p (k d) -> p k d", d=D)
        self_t = arena[:, 8000:8512]
        agg_t = arena[:, 8512:9024]
        node = arena[:, 9024:10048].rearrange("p (j d) -> p j d", d=D)

        prep = adj[:, 20:25, :].rearrange("p k n -> p (k n)").bitcast(F32)
        raw_src = prep[:, 0:1024].bitcast(I32)
        raw_dst = prep[:, 1024:2048].bitcast(I32)
        hi_i = prep[:, 2048:3072].bitcast(I32)
        lo_i = prep[:, 3072:4096].bitcast(I32)
        p_src = prep[:, 4096:5120]
        p_lo = prep[:, 5120:6144]
        p_drel = prep[:, 6144:7168]
        p_comb = raw_dst.bitcast(F32)
        oh_src = [arena[:, 256 * u:256 * (u + 1)].bitcast(BF16).rearrange("p (n j) -> p n j", j=J)
                  for u in range(2)]
        oh_dst = [arena[:, 512 + 1200 * u:512 + 1200 * (u + 1)].bitcast(BF16)
                  .rearrange("p (j n) -> p j n", j=J) for u in range(2)]
        comb = arena[:, 2912:2912 + NB * J].rearrange("p (s j) -> p s j", j=J)
        lo_h = arena[:, 3696:3696 + NB * J // 2].bitcast(BF16).rearrange("p (s j) -> p s j", j=J)
        iota_c = arena[:, 8000:8000 + NT * WIN // 2].bitcast(I16)
        iota_j = arena[:, 8512:8512 + P * J // 2].bitcast(BF16).rearrange("p (n j) -> p n j", j=J)
        KE = R + WIN

        def edge(a, n):
            return arena[:, a:a + n]

        ec = [edge(J * KE * u, J * KE).rearrange("p (j f) -> p j f", j=J) for u in range(2)]
        o = 2 * J * KE
        z_e = [edge(o + 512 * v, 512) for v in range(SLOTS)]
        h_t = [edge(o + 2048 + 512 * u, 512) for u in range(2)]
        msg = [edge(o + 3072 + 512 * u, 512) for u in range(2)]
        assert o + 4096 <= 4800
        ec_t = [arena[:, 8000 + 512 * u:8512 + 512 * u] for u in range(2)]
        w_e = [arena[:, 9024 + 128 * u:9152 + 128 * u] for u in range(2)]
        oh_e = [arena[:, 9280 + 96 * v:9376 + 96 * v].rearrange("p (j w) -> p j w", j=J)
                for v in range(SLOTS)]
        res = [arena[:, a:a + 512].rearrange("p (j d) -> p j d", d=D) for a in (8000, 8512)]
        agg_all = arena[:, 4800:8000]

        ps = ctx.enter_context(nc.psum_tensor("ps", [P, 8, 512], F32))

        phase_ends = sem("phase_ends")
        loads = [sem(f"loads{i}") for i in range(10)]
        v_own = sem("v_own")
        g_own = sem("g_own")
        prep_ready = sem("prep_ready")
        prep_t = sem("prep_t")
        prep_out = sem("prep_out")
        oh_ready = [sem(f"oh_ready{v}") for v in range(SLOTS)]
        oh_used = [sem(f"oh_used{v}") for v in range(SLOTS)]
        cnt_ready = [sem(f"cnt_ready{v}") for v in range(SLOTS)]
        adj_written = [sem(f"adj_written{v}") for v in range(SLOTS)]
        lin_base = {0: 0, 1: NC, 2: 3 * NC}
        adj_zero = sem("adj_zero")
        deg_ready = sem("deg_ready")
        agg_ready = sem("agg_ready")
        self_ready = sem("self_ready")
        agg_out = sem("agg_out")
        self_out = sem("self_out")
        lin_ready = sem("lin_ready")
        lin_used = sem("lin_used")
        var_ready = sem("var_ready")
        std_ready = sem("std_ready")
        hi_ready = sem("hi_ready")
        res_ready = sem("res_ready")
        mid_ready = sem("mid_ready")
        low_ready = sem("low_ready")
        proj_t = sem("proj_t")
        proj_ts = sem("proj_ts")
        proj_ready = sem("proj_ready")
        proj_out = [sem(f"proj_out{h}") for h in range(2)]
        stored = [sem(f"stored{i}") for i in range(2)]
        ec_loaded = [sem(f"ec_loaded{v}") for v in range(SLOTS)]
        ec_onehot = [sem(f"ec_onehot{v}") for v in range(SLOTS)]
        ec_used = [sem(f"ec_used{v}") for v in range(SLOTS)]
        w_loaded = [sem(f"w_loaded{v}") for v in range(SLOTS)]
        oh_e_ready = [sem(f"oh_e_ready{v}") for v in range(SLOTS)]
        ect_out = [sem(f"ect_out{v}") for v in range(SLOTS)]
        z_ready = [sem(f"z_ready{v}") for v in range(SLOTS)]
        z_sum = [sem(f"z_sum{v}") for v in range(SLOTS)]
        zt_ready = [sem(f"zt_ready{v}") for v in range(SLOTS)]
        h_ready = [sem(f"h_ready{v}") for v in range(SLOTS)]
        m_ready = [sem(f"m_ready{v}") for v in range(SLOTS)]
        m_sum = [sem(f"m_sum{v}") for v in range(SLOTS)]
        msg_ready = [sem(f"msg_ready{v}") for v in range(SLOTS)]
        win_ready = [sem(f"win_ready{v}") for v in range(SLOTS)]
        win_added = [sem(f"win_added{v}") for v in range(SLOTS)]
        g_loaded = [sem(f"g_loaded{v}") for v in range(SLOTS)]
        idx_ready = [sem(f"idx_ready{v}") for v in range(SLOTS)]
        gather_mark = sem("gather_mark")
        relu_done = sem("relu_done")
        wt_ready = sem("wt_ready")
        eps_ready = sem("eps_ready")
        gin_ready = sem("gin_ready")
        gin_out = sem("gin_out")
        bn_ready = sem("bn_ready")
        bn_relu = sem("bn_relu")
        fin_ready = sem("fin_ready")
        out_ready = sem("out_ready")
        twice_ready = sem("twice_ready")
        out_stored = sem("out_stored")

        block = ctx.enter_context(nc.Block())

        def phase_end(eng, n):
            eng.drain().then_inc(phase_ends, 1)
            eng.wait_ge(phase_ends, 5 * n)

        def passed(eng, sems, i, v, back=0, by=1):
            w = v - back
            eng.wait_ge(sems[w % SLOTS], by * (i + 1) if w >= 0 else by * i)

        def at(i, v):
            return (i, v) if v in range(SLOTS) else (i + v // SLOTS, v % SLOTS)

        def bases(eng, regs, i, v0=0):
            eng.load(regs, base_row[0:1, bass.ds(SLOTS * i + v0, SLOTS)])
            return [eng.snap(r, min_val=0, max_val=N - 1) for r in regs]

        class Count:
            def __init__(self, eng, s):
                self.eng, self.s, self.n = eng, s, 0

            def add(self, inst):
                self.n += 1
                inst.then_inc(self.s, 1)

            def wait(self):
                self.eng.wait_ge(self.s, self.n)

        def bcast(v, n=P):
            return v.rearrange("(a d) -> a d", a=1).broadcast_to([n, v.shape[0]])

        def row(v):
            return v.rearrange("(a d) -> a d", a=1)

        def col(v):
            return v.rearrange("(d a) -> d a", a=1)

        @block.sync
        def _(sp):
            def block_rows(dst, src, s):
                last = (NB - 1 - GRP) * 512
                v = src[0:(NB - 1) * BLK].rearrange("(s e) -> s e", e=BLK)
                sp.dma_start(dst[0:GRP, 0:512], v[0:GRP]).then_inc(s, 16)
                sp.dma_start(dst[0:GRP - 1, 512:1024], v[GRP:NB - 1]).then_inc(s, 16)
                sp.dma_start(dst[GRP - 1:GRP, 512:1024],
                             src[E - BLK:E].rearrange("(s e) -> s e", s=1)).then_inc(s, 16)

            block_rows(raw_src, t["src"], loads[0])
            block_rows(raw_dst, t["dst"], loads[1])
            with nc.allow_non_contiguous_dma(reason="one word per block"):
                sp.dma_start(base_row[0:1, 0:NB - 1],
                             t["dst"][0:(NB - 1) * BLK].rearrange("(s e) -> e s", e=BLK)[0:1, :]).then_inc(loads[2], 16)
            sp.dma_start(base_row[0:1, NB - 1:NB], t["dst"][E - BLK:E - BLK + 1].rearrange("(s e) -> e s", e=1)).then_inc(loads[2], 16)

            def load_nodes(dst, src, s):
                sp.dma_start(dst[:, 0:NT - 1, :],
                             src[0:(NT - 1) * P, :].rearrange("(k p) d -> p k d", p=P)).then_inc(s, 16)
                sp.dma_start(dst[0:TAIL, NT - 1, :], src[(NT - 1) * P:N, :]).then_inc(s, 16)

            sp.wait_ge(g_own, 1)
            load_nodes(xn, t["x"], loads[3])
            sp.dma_start(w_a[:, :], t["L0_gnn_W_self1"]).then_inc(loads[4], 16)
            sp.dma_start(w_b[:, :], t["L0_gnn_W_neigh1"]).then_inc(loads[4], 16)
            sp.dma_start(bias_b[:, :], bcast(t["L0_gnn_b1"])).then_inc(loads[4], 16)
            sp.wait_ge(loads[2], 32)
            for n in range(1, 4):
                phase_end(sp, n)
            sp.dma_start(w_a[:, :], t["L0_gnn_W_self2"]).then_inc(loads[4], 16)
            sp.dma_start(w_b[:, :], t["L0_gnn_W_neigh2"]).then_inc(loads[4], 16)
            sp.dma_start(bias_b[:, :], bcast(t["L0_gnn_b2"])).then_inc(loads[4], 16)
            sp.wait_ge(res_ready, 2 * NC)
            load_nodes(xn, t["x"], loads[3])
            phase_end(sp, 4)
            sp.dma_start(w_a[:, :], t["L1_gnn_W1"][0:D, :]).then_inc(loads[4], 16)
            sp.dma_start(w_b[:, :], t["L1_gnn_W1"][D:2 * D, :]).then_inc(loads[4], 16)
            sp.dma_start(x1_d[:, :].rearrange("(k p) d -> p k d", p=P), xn).then_inc(loads[5], 16)
            for c, (k0, nt) in enumerate(CHUNKS):
                for h, dd in enumerate((xa_d, xb_d)):
                    sp.wait_ge(proj_out[h], c + 1)
                    sp.dma_start(dd[k0 * P:(k0 + nt) * P, :].rearrange("(k p) d -> p k d", p=P),
                                 arena[:, 1024 + 1024 * (c % 2) + 512 * h:1024 + 1024 * (c % 2) + 512 * h + nt * D]
                                 .rearrange("p (k d) -> p k d", d=D)).then_inc(stored[c % 2], 16)
            for u in range(2):
                sp.wait_ge(stored[u], 32 * len(CHUNKS[u::2]))
            sp.wait_ge(loads[5], 16)
            phase_end(sp, 5)
            sp.dma_start(w_b[:, :], t["L1_gnn_W2"]).then_inc(loads[6], 16)
            sp.dma_start(cols[:, 0:1], col(t["L1_gnn_b1"])).then_inc(loads[6], 16)
            sp.dma_start(bias_b[:, :], bcast(t["L1_gnn_b2"])).then_inc(loads[6], 16)
            for u in range(2):
                sp.dma_start(w_e[u][0:R, :], t["L1_gnn_W1"][2 * D:2 * D + R, :]).then_inc(loads[6], 16)

            base_regs = [sp.alloc_register(f"sp_base{v}") for v in range(SLOTS)]

            def edge_loads(i, v, b, last=False):
                e0 = E - BLK if last else (SLOTS * i + v) * BLK
                passed(sp, ec_used, i, v, back=2)
                sp.dma_start(ec[v % 2][:, :, 0:R],
                             t["edge_attr_64"][bass.ds(e0, BLK), :].rearrange("(j p) f -> p j f", p=P)
                             ).then_inc(ec_loaded[v], 16)
                passed(sp, z_ready, i, v, back=2)
                sp.dma_start(w_e[v % 2][R:KE, :], xb_d[bass.ds(b, WIN), :]).then_inc(w_loaded[v], 16)

            with sp.Fori(0, NB // SLOTS - 1) as i:
                b = bases(sp, base_regs, i)
                for v in range(SLOTS):
                    edge_loads(i, v, b[v])
            b = bases(sp, base_regs, NB // SLOTS - 1)
            for v in range(SLOTS):
                edge_loads(NB // SLOTS - 1, v, b[v], last=(v == SLOTS - 1))
            phase_end(sp, 6)
            sp.dma_start(w_a[:, :], t["L1_gnn_Wn"]).then_inc(loads[7], 16)
            sp.dma_start(bias_b[:, :], bcast(t["L1_gnn_bn"])).then_inc(loads[7], 16)
            sp.dma_start(gamma_b[:, :], bcast(t["L1_gnn_gamma"])).then_inc(loads[7], 16)
            sp.dma_start(beta_b[:, :], bcast(t["L1_gnn_beta"])).then_inc(loads[7], 16)
            sp.dma_start(arena[:, 0:3200].rearrange("p (k d) -> p k d", d=D),
                         x1_d[:, :].rearrange("(k p) d -> p k d", p=P)).then_inc(loads[7], 16)
            phase_end(sp, 7)
            sp.dma_start(w_b[:, :], t["L2_gnn_W"]).then_inc(loads[8], 16)
            sp.dma_start(bias_b[:, :], bcast(t["L2_gnn_b"])).then_inc(loads[8], 16)
            sp.dma_start(gamma_b[:, :], bcast(t["L2_gnn_gamma"])).then_inc(loads[8], 16)
            sp.dma_start(beta_b[:, :], bcast(t["L2_gnn_beta"])).then_inc(loads[8], 16)
            phase_end(sp, 8)
            sp.dma_start(w_b[:, :], t["L3_gnn_W"]).then_inc(loads[9], 16)
            sp.dma_start(cols[:, 0:1], col(t["L3_gnn_b"])).then_inc(loads[9], 16)
            sp.dma_start(cols[:, 1:2], col(t["L3_gnn_gamma"])).then_inc(loads[9], 16)
            sp.dma_start(cols[:, 2:3], col(t["L3_gnn_beta"])).then_inc(loads[9], 16)
            sp.dma_start(cols[:, 3:4], bcast(t["L3_gnn_gin_eps"])).then_inc(loads[9], 16)
            phase_end(sp, 9)
            for g, (k0, nt) in enumerate(PAIR):
                sp.wait_ge(out_ready, g + 1)
                if nt == 2 * CH:
                    sp.dma_start(out[k0 * P:(k0 + nt) * P, :].rearrange("(k p) d -> p k d", p=P),
                                 xn[:, k0:k0 + nt, :]).then_inc(out_stored, 16)
                else:
                    sp.dma_start(out[k0 * P:N, :], xn[0:TAIL, k0, :]).then_inc(out_stored, 16)
            sp.wait_ge(out_stored, 16 * len(PAIR))

        @block.gpsimd
        def _(pool):
            g = Count(pool, g_own)
            g.add(pool.memset(xn[:, NT - 1, :], 0.0))
            g.add(pool.memset(ident_f[:, :], 0.0))
            g.add(pool.memset(ident_h[:, :], 0.0))
            g.wait()
            g.add(pool.affine_select(out=ident_f[:, :], in_=ident_f[:, :], compare_op=ALU.not_equal, fill=1.0,
                                     base=0, pattern=[[-1, P]], channel_multiplier=1))
            g.add(pool.affine_select(out=ident_h[:, :], in_=ident_h[:, :], compare_op=ALU.not_equal, fill=1.0,
                                     base=0, pattern=[[-1, P]], channel_multiplier=1))
            g.add(pool.iota(iota_c, pattern=[[1, NT * WIN]], base=0, channel_multiplier=0))
            g.add(pool.iota(win_i[:, :], pattern=[[1, WIN]], base=0, channel_multiplier=0,
                            allow_small_or_imprecise_dtypes=True))
            g.add(pool.memset(ones_h[:, :], 1.0))
            g.add(pool.iota(iota_j, pattern=[[1, P], [0, J]], base=0, channel_multiplier=0,
                            allow_small_or_imprecise_dtypes=True))
            pool.memset(adj[:, 10:20, :].rearrange("p k n -> p (k n)").bitcast(I32), 0).then_inc(adj_zero, 1)
            phase_end(pool, 1)
            for n in range(2, 6):
                phase_end(pool, n)

            def gather(i, v):
                passed(pool, idx_ready, i, v)
                pool.wait_ge(zt_ready[v], i)
                pool.sem_inc(gather_mark, 1)
                for j in range(J):
                    pool.indirect_dma_start(out=z_e[v][:, j * D:(j + 1) * D], out_offset=None, in_=xa_d[:, :],
                                            in_offset=bass.IndirectOffsetOnAxis(ap=idx[:, v, j:j + 1], axis=0)
                                            ).then_inc(g_loaded[v], 16)

            with pool.Fori(0, NB // SLOTS) as i:
                for v in range(SLOTS):
                    gather(i, v)
            for n in range(6, 10):
                phase_end(pool, n)

        @block.tensor
        def _(pe):
            pe.wait_ge(prep_ready, 1)
            pe.wait_ge(g_own, 9)
            n = 0
            for half in range(2):
                for a, v in enumerate((p_comb, p_lo, p_drel, p_src)):
                    if n >= 2:
                        pe.wait_ge(prep_out, n - 1)
                    for j in range(J):
                        c0 = 512 * half + j * P
                        last = pe.transpose(ps[:, n % 2, GRP * j:GRP * (j + 1)], v[0:GRP, c0:c0 + P],
                                            ident_f[0:GRP, 0:GRP])
                    last.then_inc(prep_t, 1)
                    n += 1
            phase_end(pe, 1)

            base_regs = [pe.alloc_register(f"pe_base{v}") for v in range(SLOTS)]

            def counts(i, v, b):
                u = v % 2
                passed(pe, oh_ready, i, v)
                passed(pe, adj_written, i, v, back=2)
                for h, (k0, k1) in enumerate(((0, H0), (H0, NT))):
                    for j in range(J):
                        last = pe.matmul(ps[:, 2 * u + h, 0:(k1 - k0) * WIN], oh_src[u][:, :, j],
                                         oh_dst[u][:, j, k0 * WIN:k1 * WIN], start=(j == 0), stop=False)
                last.then_inc(oh_used[v], 1)
                passed(pe, adj_written, i, v, back=1)
                for h, (k0, k1) in enumerate(((0, H0), (H0, NT))):
                    last = pe.matmul(ps[:, 2 * u + h, 0:(k1 - k0) * WIN], ident_h[:, :],
                                     adj[:, k0:k1, bass.ds(b, WIN)], start=False, stop=True)
                last.then_inc(cnt_ready[v], 1)

            with pe.Fori(0, NB // SLOTS) as i:
                b = bases(pe, base_regs, i)
                for v in range(SLOTS):
                    counts(i, v, b[v])
            phase_end(pe, 2)

            for k in range(NT):
                for q in range(NT):
                    last = pe.matmul(ps[:, 7, k:k + 1], adj[:, q, k * P:(k + 1) * P], ones_h[:, 0:1],
                                     start=(q == 0), stop=(q == NT - 1))
            last.then_inc(deg_ready, 1)

            def aggregate(call, i, u, c0, nt):
                w = nt * P
                pe.wait_ge(agg_out, call * NC + 2 * i)
                for k in range(NT):
                    if u == 0 and k % CH == 0:
                        pe.wait_ge(low_ready, call * NC + k // CH + 1)
                    for q in range(3):
                        last = pe.matmul(ps[:, u, 0:w], parts[q][:, k, :], adj[:, k, bass.ds(c0, w)],
                                         start=(k == 0 and q == 0), stop=(k == NT - 1 and q == 2))
                last.then_inc(agg_ready, 1)

            def own_t(call, c, nt):
                pe.wait_ge(self_out, call * NC + c)
                for j in range(nt):
                    for q in range(3):
                        last = pe.matmul(ps[:, 2, j * P:(j + 1) * P],
                                         parts[q][:, bass.ds(CH * c + j, 1), :].rearrange("p a d -> p (a d)"),
                                         ident_h[:, :], start=(q == 0), stop=(q == 2))
                last.then_inc(self_ready, 1)

            def layer(call, linear):
                with pe.Fori(0, PAIRS) as i:
                    for u in range(2):
                        aggregate(call, i, u, (2 * i + u) * CH * P, CH)
                        if u == 0:
                            own_t(call, 2 * i, CH)
                    linear(call, 2 * i, CH)
                    own_t(call, 2 * i + 1, CH)
                    linear(call, 2 * i + 1, CH)
                k0, nt = CHUNKS[-1]
                aggregate(call, PAIRS, 0, k0 * P, nt)
                own_t(call, NFULL, nt)
                linear(call, NFULL, nt)

            def sage(call, c, nt):
                n0 = call * NC
                pe.wait_ge(lin_used, n0 + c)
                pe.wait_ge(self_out, n0 + c + 1)
                for j in range(nt):
                    pe.matmul(ps[:, 3, j * D:(j + 1) * D], self_t[:, j * P:(j + 1) * P], w_a[:, :],
                              start=True, stop=True)
                pe.wait_ge(agg_out, n0 + c + 1)
                for j in range(nt):
                    last = pe.matmul(ps[:, 4, j * D:(j + 1) * D], agg_t[:, j * P:(j + 1) * P], w_b[:, :],
                                     start=True, stop=True)
                last.then_inc(lin_ready, 1)

            pe.wait_ge(loads[4], 48)
            layer(0, sage)
            phase_end(pe, 3)
            pe.wait_ge(loads[4], 96)
            layer(1, sage)
            phase_end(pe, 4)

            pe.wait_ge(loads[4], 128)
            for c, (k0, nt) in enumerate(CHUNKS):
                if c >= 2:
                    pe.wait_ge(proj_ts, c - 1)
                for j in range(nt):
                    last = pe.transpose(ps[:, c % 2, j * P:(j + 1) * P], xn[:, k0 + j, :], ident_f[:, :])
                last.then_inc(proj_t, 1)
                pe.wait_ge(proj_ts, c + 1)
                if c >= 2:
                    for h in range(2):
                        pe.wait_ge(proj_out[h], c - 1)
                for h, w in enumerate((w_a, w_b)):
                    for j in range(nt):
                        last = pe.matmul(ps[:, 2 + 2 * (c % 2) + h, j * D:(j + 1) * D],
                                         arena[:, 512 * (c % 2) + j * P:512 * (c % 2) + (j + 1) * P], w[:, :],
                                         start=True, stop=True)
                last.then_inc(proj_ready, 1)
            phase_end(pe, 5)

            pe.wait_ge(loads[6], 80)

            def inputs_t(i, v):
                passed(pe, ec_loaded, i, v, by=16)
                passed(pe, ec_onehot, i, v)
                passed(pe, ect_out, i, v, back=2)
                for j in range(J):
                    last = pe.transpose(ps[0:KE, v % 2, j * P:(j + 1) * P], ec[v % 2][:, j, :], ident_f[:, :])
                last.then_inc(ec_used[v], 1)

            def hidden(i, v):
                passed(pe, ect_out, i, v)
                passed(pe, w_loaded, i, v, by=16)
                passed(pe, z_sum, i, v, back=2)
                for j in range(J):
                    last = pe.matmul(ps[:, 2 + v % 2, j * P:(j + 1) * P], ec_t[v % 2][0:KE, j * P:(j + 1) * P],
                                     w_e[v % 2][0:KE, :], start=True, stop=True)
                last.then_inc(z_ready[v], 1)

            def hidden_t(i, v):
                passed(pe, z_sum, i, v)
                passed(pe, h_ready, i, v, back=1)
                for j in range(J):
                    last = pe.transpose(ps[:, 4, j * P:(j + 1) * P], z_e[v][:, j * P:(j + 1) * P], ident_f[:, :])
                last.then_inc(zt_ready[v], 1)

            def messages(i, v):
                passed(pe, h_ready, i, v)
                passed(pe, m_sum, i, v, back=2)
                for j in range(J):
                    last = pe.matmul(ps[:, 5 + v % 2, j * P:(j + 1) * P], h_t[v % 2][:, j * P:(j + 1) * P], w_b[:, :],
                                     start=True, stop=True)
                last.then_inc(m_ready[v], 1)

            def window(i, v):
                passed(pe, msg_ready, i, v)
                passed(pe, oh_e_ready, i, v)
                passed(pe, win_added, i, v, back=1)
                for j in range(J):
                    last = pe.matmul(ps[:, 7, 0:WIN], msg[v % 2][:, j * P:(j + 1) * P], oh_e[v][:, j, :],
                                     start=(j == 0), stop=(j == J - 1))
                last.then_inc(win_ready[v], 1)

            def step(i, v, first=False, left=2):
                if left >= 1:
                    hidden(*at(i, v + 1))
                hidden_t(i, v)
                if left >= 2:
                    inputs_t(*at(i, v + 2))
                if not first:
                    window(*at(i, v - 1))
                messages(i, v)

            inputs_t(0, 0)
            hidden(0, 0)
            inputs_t(0, 1)
            step(0, 0, first=True)
            with pe.Fori(0, NB // SLOTS - 1) as i:
                for v in range(1, SLOTS + 1):
                    step(*at(i, v))
            for v in range(1, SLOTS):
                step(NB // SLOTS - 1, v, left=SLOTS - 1 - v)
            window(NB // SLOTS - 1, SLOTS - 1)
            phase_end(pe, 6)

            pe.wait_ge(loads[7], 80)
            for c, (k0, nt) in enumerate(CHUNKS):
                if c >= 4:
                    pe.wait_ge(lin_used, 2 * NC + c - 3)
                for j in range(nt):
                    last = pe.matmul(ps[:, c % 4, j * D:(j + 1) * D], agg_all[:, (k0 + j) * P:(k0 + j + 1) * P], w_a[:, :],
                                     start=True, stop=True)
                last.then_inc(lin_ready, 1)
            phase_end(pe, 7)

            def transposed_weight():
                pe.transpose(ps[:, 7, 0:P], w_b[:, :], ident_f[:, :]).then_inc(proj_t, 1)

            pe.wait_ge(loads[8], 64)
            transposed_weight()

            def gcn(call, c, nt):
                pe.wait_ge(wt_ready, 1)
                pe.wait_ge(lin_used, lin_base[call] + c)
                pe.wait_ge(agg_out, call * NC + c + 1)
                for j in range(nt):
                    last = pe.matmul(ps[:, 4, j * D:(j + 1) * D], agg_t[:, j * P:(j + 1) * P], w_c[:, :],
                                     start=True, stop=True)
                last.then_inc(lin_ready, 1)

            layer(2, gcn)
            phase_end(pe, 8)
            pe.wait_ge(loads[9], 80)
            transposed_weight()

            def gin(call, c, nt):
                pe.wait_ge(wt_ready, 2)
                pe.wait_ge(gin_out, c)
                pe.wait_ge(agg_out, call * NC + c + 1)
                pe.matmul(ps[:, 4, 0:nt * P], w_c[:, :], agg_t[:, 0:nt * P], start=True, stop=True
                          ).then_inc(gin_ready, 1)

            layer(3, gin)
            phase_end(pe, 9)
            pe.wait_ge(twice_ready, 1)
            for g, (k0, nt) in enumerate(PAIR):
                pe.wait_ge(bn_relu, g + 1)
                if g >= 2:
                    pe.wait_ge(out_ready, g - 1)
                for j in range(nt):
                    k = k0 + j
                    o = ps[:, 2 * (g % 2) + j // CH, (j % CH) * D:(j % CH + 1) * D]
                    for q in range(3):
                        pe.matmul(o, ident_h[:, :], parts[q][:, k, :], start=(q == 0), stop=False)
                    last = pe.matmul(o, agg_all[:, k * P:(k + 1) * P], ident_f[:, :], start=False, stop=True)
                last.then_inc(fin_ready, 1)

        @block.scalar
        def _(act):
            for n in range(8):
                half, a = n // 4, n % 4
                dst = (comb, lo_h, drel, src_idx)[a]
                act.wait_ge(prep_t, n + 1)
                act.activation(dst[:, GRP * half:GRP * (half + 1), :],
                               ps[:, n % 2, 0:GRP * J].rearrange("p (j s) -> p s j", j=J), ACT.Copy
                               ).then_inc(prep_out, 1)
            phase_end(act, 1)

            base_regs = [act.alloc_register(f"act_base{v}") for v in range(SLOTS)]

            def to_adj(i, v, b):
                passed(act, cnt_ready, i, v)
                for h, (k0, k1) in enumerate(((0, H0), (H0, NT))):
                    last = act.activation(adj[:, k0:k1, bass.ds(b, WIN)],
                                          ps[:, 2 * (v % 2) + h, 0:(k1 - k0) * WIN].rearrange("p (k w) -> p k w", w=WIN),
                                          ACT.Copy)
                last.then_inc(adj_written[v], 1)

            with act.Fori(0, NB // SLOTS) as i:
                b = bases(act, base_regs, i)
                for v in range(SLOTS):
                    to_adj(i, v, b[v])
            phase_end(act, 2)

            def split(call, scale=None):
                for c, (k0, nt) in enumerate(CHUNKS):
                    if scale is None:
                        act.activation(parts[0][:, k0:k0 + nt, :], xn[:, k0:k0 + nt, :], ACT.Copy).then_inc(hi_ready, 1)
                    else:
                        for k in range(k0, k0 + nt):
                            last = act.activation(parts[0][:, k, :], xn[:, k, :], ACT.Copy, scale=scale[:, k:k + 1])
                        last.then_inc(hi_ready, 1)
                for c, (k0, nt) in enumerate(CHUNKS):
                    act.wait_ge(res_ready, call * NC + c + 1)
                    act.activation(parts[1][:, k0:k0 + nt, :], res[c % 2][:, 0:nt, :], ACT.Copy).then_inc(mid_ready, 1)

            roots = [0]

            def root(nt):
                roots[0] += 1
                act.wait_ge(var_ready, roots[0])
                act.activation(std[:, 0:nt], mv[:, 0:nt, 1], ACT.Sqrt, bias=cols[:, 7:8]).then_inc(std_ready, 1)

            def self_chunks(call, read, n_read, scale=1.0, then=None):
                for c, (k0, nt) in enumerate(CHUNKS):
                    act.wait_ge(self_ready, call * NC + c + 1)
                    act.wait_ge(read, n_read + c)
                    act.activation(self_t[:, 0:nt * P], ps[:, 2, 0:nt * P], ACT.Copy, scale=scale).then_inc(self_out, 1)
                    if then is not None:
                        then(c, k0, nt)

            act.wait_ge(loads[3], 32)
            split(0)
            act.wait_ge(deg_ready, 2)
            act.activation(std_deg[:, :], dinv[:, :], ACT.Sqrt).then_inc(deg_ready, 1)

            def relu_pair(c, k0, nt):
                if c % 2 or c == NC - 1:
                    g = c // 2
                    act.wait_ge(lin_used, c + 1)
                    p0, pt = PAIR[g]
                    act.activation(xn[:, p0:p0 + pt, :], node[:, 0:pt, :], ACT.Relu).then_inc(relu_done, 1)

            self_chunks(0, lin_ready, 0, then=relu_pair)
            phase_end(act, 3)

            def root_pair(times):
                def roots_of(c, k0, nt):
                    if c % 2 or c == NC - 1:
                        for _ in range(times):
                            root(PAIR[c // 2][1])
                return roots_of

            split(1)
            self_chunks(1, lin_ready, NC, then=root_pair(1))
            phase_end(act, 4)
            for c, (k0, nt) in enumerate(CHUNKS):
                act.wait_ge(proj_t, c + 1)
                if c >= 2:
                    act.wait_ge(proj_ready, c - 1)
                act.activation(arena[:, 512 * (c % 2):512 * (c % 2) + nt * P], ps[:, c % 2, 0:nt * P], ACT.Copy
                               ).then_inc(proj_ts, 1)
                act.wait_ge(proj_ready, c + 1)
                if c >= 2:
                    act.wait_ge(stored[c % 2], 32 * (c // 2))
                act.activation(arena[:, 1024 + 1024 * (c % 2):1024 + 1024 * (c % 2) + nt * D],
                               ps[:, 2 + 2 * (c % 2), 0:nt * D], ACT.Copy).then_inc(proj_out[0], 1)
            phase_end(act, 5)

            act.wait_ge(loads[6], 80)

            def inputs_out(i, v):
                passed(act, ec_used, i, v)
                passed(act, z_ready, i, v, back=2)
                act.activation(ec_t[v % 2][0:KE, :], ps[0:KE, v % 2, :], ACT.Copy).then_inc(ect_out[v], 1)

            def hidden_relu(i, v):
                passed(act, zt_ready, i, v)
                passed(act, m_ready, i, v, back=2)
                act.activation(h_t[v % 2], ps[:, 4, :], ACT.Relu, bias=cols[:, 0:1]).then_inc(h_ready[v], 1)

            def message_relu(i, v):
                passed(act, m_sum, i, v)
                act.activation(msg[v % 2], msg[v % 2], ACT.Relu).then_inc(msg_ready[v], 1)

            def step(i, v, left=2):
                hidden_relu(i, v)
                if left >= 2:
                    inputs_out(*at(i, v + 2))
                message_relu(i, v)

            inputs_out(0, 0)
            inputs_out(0, 1)
            with act.Fori(0, NB // SLOTS - 1) as i:
                for v in range(SLOTS):
                    step(i, v)
            for v in range(SLOTS):
                step(NB // SLOTS - 1, v, left=SLOTS - 1 - v)
            phase_end(act, 6)
            for k0, nt in PAIR:
                root(nt)
                root(nt)
            phase_end(act, 7)
            split(2, scale=dinv)
            act.wait_ge(proj_t, NC + 1)
            act.activation(w_c[:, :], ps[:, 7, 0:P], ACT.Copy).then_inc(wt_ready, 1)
            self_chunks(2, agg_out, 2 * NC, then=root_pair(2))
            phase_end(act, 8)
            split(3)
            act.wait_ge(proj_t, NC + 2)
            act.activation(w_c[:, :], ps[:, 7, 0:P], ACT.Copy).then_inc(wt_ready, 1)
            act.wait_ge(eps_ready, 1)

            def gin_chunk(c, k0, nt):
                act.wait_ge(gin_ready, c + 1)
                act.activation(agg_all[:, k0 * P:(k0 + nt) * P], ps[:, 4, 0:nt * P], ACT.Identity,
                               bias=cols[:, 0:1]).then_inc(gin_out, 1)

            self_chunks(3, agg_out, 3 * NC, scale=cols[:, 4:5], then=gin_chunk)
            root(1)
            phase_end(act, 9)
            for k0, nt in PAIR:
                act.activation(agg_all[:, k0 * P:(k0 + nt) * P], agg_all[:, k0 * P:(k0 + nt) * P], ACT.Relu,
                               bias=cols[:, 6:7], scale=cols[:, 5:6]).then_inc(bn_relu, 1)
            for k0, nt in PAIR:
                root(nt)

        @block.vector
        def _(dve):
            own = Count(dve, v_own)
            dve.memset(cols[:, 7:8], EPS)
            dve.wait_ge(loads[0], 48)
            own.add(dve.tensor_scalar(hi_i[0:GRP, :], raw_src[0:GRP, :], 7, None, ALU.arith_shift_right))
            own.add(dve.tensor_scalar(lo_i[0:GRP, :], raw_src[0:GRP, :], P - 1, None, ALU.bitwise_and))
            own.add(dve.tensor_copy(p_src[0:GRP, :], raw_src[0:GRP, :]))
            dve.wait_ge(loads[1], 48)
            for half in range(2):
                h = slice(512 * half, 512 * half + 512)
                own.add(dve.tensor_scalar(p_drel[0:GRP, h], raw_dst[0:GRP, h],
                                        raw_dst[0:GRP, 512 * half:512 * half + 1], None, ALU.subtract))
            own.wait()
            own.add(dve.tensor_copy(p_lo[0:GRP, :], lo_i[0:GRP, :]))
            dve.scalar_tensor_tensor(out=p_comb[0:GRP, :], in0=hi_i[0:GRP, :], scalar=float(WIN),
                                     in1=p_drel[0:GRP, :], op0=ALU.mult, op1=ALU.add).then_inc(prep_ready, 1)
            dve.memset(adj[:, 0:10, :].rearrange("p k n -> p (k n)").bitcast(I32), 0)
            dve.wait_ge(prep_t, 8)
            dve.memset(prep.bitcast(I32), 0)
            dve.wait_ge(prep_out, 8)
            for a in (comb, drel):
                dve.memset(a[:, NB - 1, 0:DUP // P], -1.0)
                dve.memset(a[0:DUP % P, NB - 1, DUP // P:DUP // P + 1], -1.0)
            dve.wait_ge(adj_zero, 1)
            phase_end(dve, 1)

            def onehots(i, v):
                s = SLOTS * i + v
                passed(dve, oh_used, i, v, back=2)
                dve.tensor_tensor(oh_src[v % 2], iota_j, lo_h[:, bass.ds(s, 1), :].broadcast_to([P, P, J]), ALU.is_equal)
                for j in range(J):
                    last = dve.tensor_scalar(oh_dst[v % 2][:, j, :], iota_c, comb[:, bass.ds(s, 1), j], None, ALU.is_equal)
                last.then_inc(oh_ready[v], 1)

            with dve.Fori(0, NB // SLOTS) as i:
                for v in range(SLOTS):
                    onehots(i, v)
            phase_end(dve, 2)

            def split(call, scale=None):
                def low(c):
                    k0, nt = CHUNKS[c]
                    dve.wait_ge(mid_ready, call * NC + c + 1)
                    dve.tensor_tensor(parts[2][:, k0:k0 + nt, :], res[c % 2][:, 0:nt, :], parts[1][:, k0:k0 + nt, :],
                                      ALU.subtract).then_inc(low_ready, 1)

                for c, (k0, nt) in enumerate(CHUNKS):
                    dve.wait_ge(hi_ready, call * NC + c + 1)
                    if c >= 2:
                        dve.wait_ge(low_ready, call * NC + c - 1)
                    if scale is None:
                        last = dve.tensor_tensor(res[c % 2][:, 0:nt, :], xn[:, k0:k0 + nt, :],
                                                 parts[0][:, k0:k0 + nt, :], ALU.subtract)
                    else:
                        for j in range(nt):
                            last = dve.scalar_tensor_tensor(out=res[c % 2][:, j, :], in0=xn[:, k0 + j, :],
                                                            scalar=scale[:, k0 + j:k0 + j + 1], in1=parts[0][:, k0 + j, :],
                                                            op0=ALU.mult, op1=ALU.subtract)
                    last.then_inc(res_ready, 1)
                    if c:
                        low(c - 1)
                low(NC - 1)

            roots = [0]

            def layernorm(src, dst, nt, done=None):
                for j in range(nt):
                    own.add(dve.bn_stats(stats[:, j, :], src[:, j, :]))
                own.wait()
                for j in range(nt):
                    last = dve.bn_aggr(mv[:, j, :], stats[:, j, :])
                last.then_inc(var_ready, 1)
                roots[0] += 1
                dve.wait_ge(std_ready, roots[0])
                own.add(dve.reciprocal(rstd[:, 0:nt], std[:, 0:nt]))
                own.wait()
                for j in range(nt):
                    last = dve.tensor_scalar(dst[:, j, :], src[:, j, :], mv[:, j, 0:1], rstd[:, j:j + 1],
                                             ALU.subtract, ALU.mult)
                    if done is None or j < nt - 1:
                        own.add(last)
                if done is not None:
                    last.then_inc(done, 1)
                own.wait()

            def over(b, nt):
                return b[:, :].rearrange("p (a d) -> p a d", a=1).broadcast_to([P, nt, D])

            def affine(a, nt):
                for op, b in ((ALU.mult, gamma_b), (ALU.add, beta_b)):
                    own.add(dve.tensor_tensor(a[:, 0:nt, :], a[:, 0:nt, :], over(b, nt), op))
                    own.wait()

            dve.wait_ge(loads[3], 32)
            split(0)
            dve.wait_ge(deg_ready, 1)
            own.add(dve.tensor_scalar(inv_deg[:, :], ps[:, 7, 0:NT], 1.0, None, ALU.max))
            dve.tensor_scalar(dinv[:, :], ps[:, 7, 0:NT], 1.0, None, ALU.add).then_inc(deg_ready, 1)
            own.wait()
            own.add(dve.reciprocal(inv_deg[:, :], inv_deg[:, :]))
            dve.wait_ge(deg_ready, 3)
            dve.reciprocal(dinv[:, :], std_deg[:, :])

            def bank(b, nt):
                return ps[:, b, 0:nt * D].rearrange("p (j d) -> p j d", d=D)

            def combine(call, c):
                k0, nt = CHUNKS[c]
                n = call * NC + c
                half = node[:, CH * (c % 2):CH * (c % 2) + nt, :]
                dve.wait_ge(agg_ready, n + 1)
                dve.wait_ge(lin_ready, n)
                dve.tensor_copy(agg_t[:, 0:nt * P], ps[:, c % 2, 0:nt * P]).then_inc(agg_out, 1)
                dve.wait_ge(lin_ready, n + 1)
                own.add(dve.tensor_tensor(half, bank(3, nt), over(bias_b, nt), ALU.add))
                own.wait()
                for j in range(nt):
                    last = dve.scalar_tensor_tensor(out=half[:, j, :], in0=ps[:, 4, j * D:(j + 1) * D],
                                                    scalar=inv_deg[:, k0 + j:k0 + j + 1], in1=half[:, j, :],
                                                    op0=ALU.mult, op1=ALU.add)
                last.then_inc(lin_used, 1)
                dve.wait_ge(lin_used, n + 1)

            def chunks_of(g):
                return [c for c in (2 * g, 2 * g + 1) if c < NC]

            for g in range(len(PAIR)):
                dve.wait_ge(relu_done, g)
                for c in chunks_of(g):
                    combine(0, c)
            phase_end(dve, 3)
            split(1)
            dve.wait_ge(loads[3], 64)
            for g, (k0, nt) in enumerate(PAIR):
                for c in chunks_of(g):
                    combine(1, c)
                own.add(dve.tensor_tensor(node[:, 0:nt, :], node[:, 0:nt, :], xn[:, k0:k0 + nt, :], ALU.add))
                own.wait()
                layernorm(node, xn[:, k0:k0 + nt, :], nt)
            phase_end(dve, 4)
            for c, (k0, nt) in enumerate(CHUNKS):
                dve.wait_ge(proj_ready, c + 1)
                if c >= 2:
                    dve.wait_ge(stored[c % 2], 32 * (c // 2))
                b0 = 1536 + 1024 * (c % 2)
                dve.tensor_copy(arena[:, b0:b0 + nt * D], ps[:, 3 + 2 * (c % 2), 0:nt * D]).then_inc(proj_out[1], 1)
            phase_end(dve, 5)

            own.add(dve.memset(agg_all, 0.0))
            dve.wait_ge(loads[6], 80)
            own.wait()

            base_regs = [dve.alloc_register(f"dve_base{v}") for v in range(SLOTS)]

            def gather_index(i, v):
                dve.wait_ge(g_loaded[v], 64 * i)
                dve.tensor_copy(idx[:, v, :], src_idx[:, bass.ds(SLOTS * i + v, 1), :].rearrange("p a j -> p (a j)")
                                ).then_inc(idx_ready[v], 1)

            def block_start(i, v):
                passed(dve, ec_used, i, v, back=2)
                dve.wait_ge(win_ready[v], i)
                rel = drel[:, bass.ds(SLOTS * i + v, 1), :].rearrange("p a j -> p j a").broadcast_to([P, J, WIN])
                w = win_i[:, :].rearrange("p (a w) -> p a w", a=1).broadcast_to([P, J, WIN])
                dve.tensor_tensor(ec[v % 2][:, :, R:KE], w, rel, ALU.is_equal).then_inc(ec_onehot[v], 1)
                dve.tensor_tensor(oh_e[v], w, rel, ALU.is_equal).then_inc(oh_e_ready[v], 1)

            def add_gathered(i, v):
                passed(dve, z_ready, i, v)
                passed(dve, g_loaded, i, v, by=64)
                dve.tensor_tensor(z_e[v], ps[:, 2 + v % 2, :], z_e[v], ALU.add).then_inc(z_sum[v], 1)

            def add_bias(i, v):
                passed(dve, m_ready, i, v)
                passed(dve, win_ready, i, v, back=2)
                dve.tensor_tensor(msg[v % 2].rearrange("p (j d) -> p j d", d=D), bank(5 + v % 2, J), over(bias_b, J),
                                  ALU.add).then_inc(m_sum[v], 1)

            def add_window(i, v, b):
                passed(dve, win_ready, i, v)
                passed(dve, win_added, i, v, back=1)
                dve.tensor_tensor(agg_all[:, bass.ds(b, WIN)], ps[:, 7, 0:WIN], agg_all[:, bass.ds(b, WIN)], ALU.add
                                  ).then_inc(win_added[v], 1)

            def step(i, v, b=None, left=3):
                if left >= 1:
                    add_gathered(*at(i, v + 1))
                if b is not None:
                    add_window(*at(i, v - 1), b)
                if left >= 3:
                    gather_index(*at(i, v + 3))
                    block_start(*at(i, v + 3))
                add_bias(i, v)

            for v in range(3):
                gather_index(0, v)
                block_start(0, v)
            add_gathered(0, 0)
            step(0, 0)
            with dve.Fori(0, NB // SLOTS - 1) as i:
                b = bases(dve, base_regs, i)
                for v in range(1, SLOTS + 1):
                    step(*at(i, v), b[v - 1])
            b = bases(dve, base_regs, NB // SLOTS - 1)
            for v in range(1, SLOTS):
                step(NB // SLOTS - 1, v, b[v - 1], left=SLOTS - 1 - v)
            add_window(NB // SLOTS - 1, SLOTS - 1, b[SLOTS - 1])
            phase_end(dve, 6)

            dve.wait_ge(loads[7], 80)
            x1 = arena[:, 0:3200].rearrange("p (k d) -> p k d", d=D)
            for g, (k0, nt) in enumerate(PAIR):
                for c in chunks_of(g):
                    ct = CHUNKS[c][1]
                    dve.wait_ge(lin_ready, 2 * NC + c + 1)
                    dve.tensor_tensor(node[:, CH * (c % 2):CH * (c % 2) + ct, :], bank(c % 4, ct), over(bias_b, ct),
                                      ALU.add).then_inc(lin_used, 1)
                dve.wait_ge(lin_used, 2 * NC + chunks_of(g)[-1] + 1)
                own.add(dve.scalar_tensor_tensor(out=node[:, 0:nt, :], in0=node[:, 0:nt, :], scalar=0.0,
                                               in1=x1[:, k0:k0 + nt, :], op0=ALU.max, op1=ALU.add))
                own.wait()
                layernorm(node, node, nt)
                affine(node, nt)
                own.add(dve.tensor_tensor(node[:, 0:nt, :], node[:, 0:nt, :], x1[:, k0:k0 + nt, :], ALU.add))
                own.wait()
                layernorm(node, xn[:, k0:k0 + nt, :], nt)
            phase_end(dve, 7)

            split(2, scale=dinv)

            def add_self(call, c, read, n_read):
                nt = CHUNKS[c][1]
                n = call * NC + c
                dve.wait_ge(agg_ready, n + 1)
                dve.wait_ge(read, n_read + c)
                dve.wait_ge(self_out, n + 1)
                dve.tensor_tensor(agg_t[:, 0:nt * P], ps[:, c % 2, 0:nt * P], self_t[:, 0:nt * P], ALU.add
                                  ).then_inc(agg_out, 1)

            for g, (k0, nt) in enumerate(PAIR):
                for c in chunks_of(g):
                    add_self(2, c, lin_ready, 3 * NC)
                    dve.wait_ge(lin_ready, 3 * NC + c + 1)
                    for j in range(CHUNKS[c][1]):
                        k = CHUNKS[c][0] + j
                        last = dve.scalar_tensor_tensor(out=node[:, k - k0, :], in0=ps[:, 4, j * D:(j + 1) * D],
                                                        scalar=dinv[:, k:k + 1], in1=bias_b[:, :],
                                                        op0=ALU.mult, op1=ALU.add)
                    last.then_inc(lin_used, 1)
                dve.wait_ge(lin_used, 3 * NC + chunks_of(g)[-1] + 1)
                layernorm(node, node, nt)
                affine(node, nt)
                own.add(dve.tensor_tensor(node[:, 0:nt, :], node[:, 0:nt, :], xn[:, k0:k0 + nt, :], ALU.add))
                own.wait()
                layernorm(node, xn[:, k0:k0 + nt, :], nt)
            phase_end(dve, 8)

            dve.wait_ge(loads[9], 80)
            dve.tensor_scalar(cols[:, 4:5], cols[:, 3:4], 1.0, None, ALU.add).then_inc(eps_ready, 1)
            split(3)

            def zt_stats(c):
                k0, nt = CHUNKS[c]
                dve.wait_ge(gin_out, c + 1)
                w = nt * P if nt == CH else TAIL
                own.add(dve.bn_stats(stats[:, c, :], agg_all[:, k0 * P:k0 * P + w]))

            for c in range(NC):
                add_self(3, c, gin_ready, 0)
                zt_stats(c)
            own.wait()
            dve.bn_aggr(mv[:, 0, :], stats[:, 0:NC, :]).then_inc(var_ready, 1)
            roots[0] += 1
            dve.wait_ge(std_ready, roots[0])
            own.add(dve.reciprocal(rstd[:, 0:1], std[:, 0:1]))
            own.wait()
            own.add(dve.tensor_tensor(cols[:, 5:6], rstd[:, 0:1], cols[:, 1:2], ALU.mult))
            own.wait()
            own.add(dve.tensor_tensor(rstd[:, 1:2], cols[:, 5:6], mv[:, 0, 0:1], ALU.mult))
            own.wait()
            dve.tensor_tensor(cols[:, 6:7], cols[:, 2:3], rstd[:, 1:2], ALU.subtract)
            phase_end(dve, 9)
            dve.tensor_scalar(ident_h[:, :], ident_h[:, :], 2.0, None, ALU.mult).then_inc(twice_ready, 1)
            for g, (k0, nt) in enumerate(PAIR):
                dve.wait_ge(fin_ready, g + 1)
                b = 2 * (g % 2)
                layernorm(ps[:, b:b + 2, :].rearrange("p a (j d) -> p (a j) d", d=D), xn[:, k0:k0 + nt, :], nt, done=out_ready)


_INS = ["x", "src", "dst", "edge_attr_64", "L0_gnn_W_self1", "L0_gnn_W_neigh1", "L0_gnn_b1", "L0_gnn_W_self2",
        "L0_gnn_W_neigh2", "L0_gnn_b2", "L1_gnn_W1", "L1_gnn_b1", "L1_gnn_W2", "L1_gnn_b2", "L1_gnn_Wn", "L1_gnn_bn",
        "L1_gnn_gamma", "L1_gnn_beta", "L2_gnn_W", "L2_gnn_b", "L2_gnn_gamma", "L2_gnn_beta", "L3_gnn_W", "L3_gnn_b",
        "L3_gnn_gamma", "L3_gnn_beta", "L3_gnn_gin_eps"]


def kernel(**inputs):
    import numpy as _np
    import concourse.bacc as _bacc
    from concourse import mybir as _mybir
    from concourse.bass_utils import run_bass_kernel_spmd as _run

    nc = _bacc.Bacc("TRN2", target_bir_lowering=False, num_devices=1)
    arrays, t = {}, {}
    for name in _INS:
        a = _np.ascontiguousarray(inputs[name])
        arrays[f"in_{name}"] = a
        t[name] = nc.dram_tensor(f"in_{name}", a.shape, _mybir.dt.from_np(a.dtype), kind="ExternalInput").ap()
    out = nc.dram_tensor("out_x", (N, D), F32, kind="ExternalOutput").ap()
    x1_d = nc.dram_tensor("x1_spill", (NP, D), F32, kind="Internal").ap()
    xa_d = nc.dram_tensor("x1_w1a", (NP, D), F32, kind="Internal").ap()
    xb_d = nc.dram_tensor("x1_w1b", (NP, D), F32, kind="Internal").ap()
    build(nc, t, out, x1_d, xa_d, xb_d)
    r = _run(nc, [arrays], core_ids=[0])
    return r.results[0]["out_x"]
```

```python
from contextlib import ExitStack

import concourse.bass as bass
from concourse import mybir

F32 = mybir.dt.float32
BF16 = mybir.dt.bfloat16
I32 = mybir.dt.int32
I16 = mybir.dt.int16
ALU = mybir.AluOpType
ACT = mybir.ActivationFunctionType

P = 128
N = 3125
E = 100000
D = 128
R = 64
EPS = 1e-5
NT = (N + P - 1) // P
NP = NT * P
TAIL = N - (NT - 1) * P
J = 4
BLK = J * P
NB = (E + BLK - 1) // BLK
GRP = NB // 2
DUP = NB * BLK - E
WIN = 24
SUB = BLK // 2
WIN_A = 12
CH = 4
CHUNKS = [(c, min(CH, NT - c)) for c in range(0, NT, CH)]
NFULL = NT // CH
PAIRS = NFULL // 2
NC = len(CHUNKS)
PAIR = [(k, min(2 * CH, NT - k)) for k in range(0, NT, 2 * CH)]
SLOTS = 4
assert NT * WIN_A <= 512 and GRP % 2 == 0
assert NB % SLOTS == 0 and NFULL % 2 == 0 and GRP <= P


ET = (E + P - 1) // P
ETAIL = E - (ET - 1) * P
SCANS = 6
assert NC * 512 >= NP and NC < 8


def build(nc, t, out, x1_d, xa_d, xb_d, table_d):
    ctx = ExitStack()
    with ctx:
        def sb(name, shape, dt):
            return ctx.enter_context(nc.sbuf_tensor(name, shape, dt))

        def sem(name):
            return ctx.enter_context(nc.semaphore(name))

        adj = sb("adj", [P, NT, NP], BF16)
        arena = sb("arena", [P, 10112], F32)
        src_idx = sb("src_idx", [P, NB, J], I32)
        drel = sb("drel", [P, NB, J], F32)
        base_row = sb("base_row", [1, NB], I32)
        w_a = sb("w_a", [P, D], F32)
        w_b = sb("w_b", [P, D], F32)
        w_c = sb("w_c", [P, D], F32)
        bias_b = sb("bias_b", [P, D], F32)
        gamma_b = sb("gamma_b", [P, D], F32)
        beta_b = sb("beta_b", [P, D], F32)
        ident_f = sb("ident_f", [P, P], F32)
        ident_h = sb("ident_h", [P, P], BF16)
        ones_h = sb("ones_h", [P, 2], BF16)
        inv_deg = sb("inv_deg", [P, NT], F32)
        dinv = sb("dinv", [P, NT], F32)
        std_deg = sb("std_deg", [P, NT], F32)
        stats = sb("stats", [P, CH * 2, 6], F32)
        mv = sb("mv", [P, 2 * CH, 2], F32)
        nbias = sb("nbias", [P, 2 * CH], F32)
        scaled = sb("scaled", [P, 2 * CH], F32)
        std = sb("std", [P, 2 * CH], F32)
        rstd = sb("rstd", [P, 2 * CH], F32)
        cols = sb("cols", [P, 8], F32)
        idx = sb("idx", [P, SLOTS, J], I32)
        win_i = sb("win_i", [P, WIN], F32)
        off = sb("off", [P, 9], F32)
        general = sb("general", [1, 1], I32)

        parts = [arena[:, 1600 * q:1600 * (q + 1)].bitcast(BF16).rearrange("p (k d) -> p k d", d=D)
                 for q in range(3)]
        xn = arena[:, 4800:8000].rearrange("p (k d) -> p k d", d=D)
        self_t = arena[:, 8000:8512]
        agg_t = arena[:, 8512:9024]
        node = arena[:, 9024:10048].rearrange("p (j d) -> p j d", d=D)

        def words(k0, k1):
            return adj[:, k0:k1, :].rearrange("p k n -> p (k n)").bitcast(I32)

        prep = adj[:, 20:25, :].rearrange("p k n -> p (k n)").bitcast(F32)
        raw_src = prep[:, 0:1024].bitcast(I32)
        raw_dst = prep[:, 1024:2048].bitcast(I32)
        hi_i = prep[:, 2048:3072].bitcast(I32)
        lo_i = prep[:, 3072:4096].bitcast(I32)
        p_src = prep[:, 4096:5120]
        p_lo = prep[:, 5120:6144]
        p_drel = prep[:, 6144:7168]
        p_comb = raw_dst.bitcast(F32)
        p_rel = raw_src.bitcast(F32)
        oh_dst = [arena[:, 600 * v:600 * v + J * NT * WIN_A // 2].bitcast(BF16)
                  .rearrange("p (j n) -> p j n", j=J) for v in range(4)]
        oh_src = [arena[:, 9024 + 256 * v:9280 + 256 * v].bitcast(BF16).rearrange("p (n j) -> p n j", j=J)
                  for v in range(4)]
        comb = arena[:, 2912:2912 + NB * J].rearrange("p (s j) -> p s j", j=J)
        lo_h = arena[:, 3696:3696 + NB * J // 2].bitcast(BF16).rearrange("p (s j) -> p s j", j=J)
        base_a = arena[0:1, 4088:4088 + 2 * NB].bitcast(I32)
        falls = arena[0:1, 2400:2400 + 2 * NB - 2]
        iota_c = arena[:, 8000:8000 + NT * WIN_A // 2].bitcast(I16)
        iota_j = arena[:, 8512:8512 + P * J // 2].bitcast(BF16).rearrange("p (n j) -> p n j", j=J)
        KE = R + WIN

        def edge(a, n):
            return arena[:, a:a + n]

        ec = [edge(J * KE * u, J * KE).rearrange("p (j f) -> p j f", j=J) for u in range(2)]
        o = 2 * J * KE
        z_e = [edge(o + 512 * v, 512) for v in range(SLOTS)]
        h_t = [edge(o + 2048 + 512 * u, 512) for u in range(2)]
        msg = [edge(o + 3072 + 512 * u, 512) for u in range(2)]
        assert o + 4096 <= 4800
        ec_t = [arena[:, 8000 + 512 * u:8512 + 512 * u] for u in range(2)]
        w_e = [arena[:, 9024 + 128 * u:9152 + 128 * u] for u in range(2)]
        oh_e = [arena[:, 9280 + 96 * v:9376 + 96 * v].rearrange("p (j w) -> p j w", j=J)
                for v in range(SLOTS)]
        res = [arena[:, a:a + 512].rearrange("p (j d) -> p j d", d=D) for a in (8000, 8512)]
        x1 = {c: arena[:, 1600 + 512 * u:1600 + 512 * u + CHUNKS[c][1] * D].rearrange("p (k d) -> p k d", d=D)
              for u, c in enumerate((0, 2, 4, 1, 3, 5, 6))}

        def third(a):
            return a[:, :, :].rearrange("p s j -> p (s j)")[:, 0:CH * D].rearrange("p (j d) -> p j d", d=D)

        node3 = [node[:, 0:CH, :], node[:, CH:2 * CH, :], third(drel)]
        res3 = res + [third(src_idx).bitcast(F32)]
        agg_all = arena[:, 4800:8000]

        room = adj[:, :, :].rearrange("p k n -> p (k n)").bitcast(F32)
        g_hot = room[:, 0:NP]
        g_iota = room[:, NP:2 * NP]
        g_agg = room[:, 2 * NP:3 * NP]
        g_x = room[:, 3 * NP:4 * NP].rearrange("p (k d) -> p k d", d=D)
        g0 = 4 * NP
        g_rows, g_rows_b, g_ones, g_z, g_h, g_msg, g_e_t = (room[:, g0 + D * q:g0 + D * (q + 1)] for q in range(7))
        g_e = room[:, g0 + 7 * D:g0 + 7 * D + R]
        g1 = g0 + 8 * D
        g_src, g_dst = (room[:, g1 + q:g1 + q + 1].bitcast(I32) for q in range(2))
        g_dst_f = room[:, g1 + 2:g1 + 3]

        ps = ctx.enter_context(nc.psum_tensor("ps", [P, 8, 512], F32))

        phase_ends = sem("phase_ends")
        loads = [sem(f"loads{i}") for i in range(10)]
        v_own = sem("v_own")
        g_own = sem("g_own")
        prep_ready = sem("prep_ready")
        prep_t = sem("prep_t")
        prep_out = sem("prep_out")
        oh_ready = sem("oh_ready")
        oh_used = sem("oh_used")
        cnt_ready = sem("cnt_ready")
        adj_written = sem("adj_written")
        lin_base = {0: 0, 1: NC, 2: 3 * NC}
        zero_ready = sem("zero_ready")
        deg_ready = sem("deg_ready")
        agg_ready = sem("agg_ready")
        self_ready = sem("self_ready")
        agg_out = sem("agg_out")
        self_out = sem("self_out")
        lin_ready = sem("lin_ready")
        lin_used = sem("lin_used")
        var_ready = sem("var_ready")
        std_ready = sem("std_ready")
        hi_ready = sem("hi_ready")
        res_ready = sem("res_ready")
        mid_ready = sem("mid_ready")
        low_ready = sem("low_ready")
        proj_t = sem("proj_t")
        proj_ts = sem("proj_ts")
        proj_ready = sem("proj_ready")
        proj_out = sem("proj_out")
        stored = [[sem(f"stored{h}_{u}") for u in range(2)] for h in range(2)]
        ec_loaded = [sem(f"ec_loaded{v}") for v in range(SLOTS)]
        ec_onehot = [sem(f"ec_onehot{v}") for v in range(SLOTS)]
        ec_used = [sem(f"ec_used{v}") for v in range(SLOTS)]
        w_loaded = [sem(f"w_loaded{v}") for v in range(SLOTS)]
        oh_e_ready = [sem(f"oh_e_ready{v}") for v in range(SLOTS)]
        ect_out = [sem(f"ect_out{v}") for v in range(SLOTS)]
        z_ready = [sem(f"z_ready{v}") for v in range(SLOTS)]
        z_sum = [sem(f"z_sum{v}") for v in range(SLOTS)]
        zt_ready = [sem(f"zt_ready{v}") for v in range(SLOTS)]
        h_ready = [sem(f"h_ready{v}") for v in range(SLOTS)]
        m_ready = [sem(f"m_ready{v}") for v in range(SLOTS)]
        m_sum = [sem(f"m_sum{v}") for v in range(SLOTS)]
        msg_ready = [sem(f"msg_ready{v}") for v in range(SLOTS)]
        win_ready = [sem(f"win_ready{v}") for v in range(SLOTS)]
        win_added = [sem(f"win_added{v}") for v in range(SLOTS)]
        g_loaded = [sem(f"g_loaded{v}") for v in range(SLOTS)]
        idx_ready = [sem(f"idx_ready{v}") for v in range(SLOTS)]
        gather_mark = sem("gather_mark")
        relu_done = sem("relu_done")
        wt_ready = sem("wt_ready")
        eps_ready = sem("eps_ready")
        gin_ready = sem("gin_ready")
        gin_out = sem("gin_out")
        bn_loaded = sem("bn_loaded")
        update_loaded = sem("update_loaded")
        x1_loaded = [sem(f"x1_loaded{u}") for u in range(2)]
        norm_ready = sem("norm_ready")
        normed = sem("normed")
        xb_ready = sem("xb_ready")
        agg_zero = sem("agg_zero")
        xs_ready = sem("xs_ready")
        bn_relu = sem("bn_relu")
        fin_ready = sem("fin_ready")
        out_ready = sem("out_ready")
        twice_ready = sem("twice_ready")
        out_stored = sem("out_stored")
        off_ready = sem("off_ready")
        off_t = sem("off_t")
        general_ready = sem("general_ready")
        tile_pe, tile_act, tile_dve = sem("tile_pe"), sem("tile_act"), sem("tile_dve")
        scan_ends = sem("scan_ends")
        gx_ready = sem("gx_ready")
        table_stored = sem("table_stored")
        tile_loaded = [sem(f"tile_loaded{s}") for s in range(SCANS)]
        rows_gathered = [sem(f"rows_gathered{s}") for s in range(SCANS)]
        dst_ready = sem("dst_ready")
        hot_ready = sem("hot_ready")
        hot_used = sem("hot_used")

        block = ctx.enter_context(nc.Block())

        def phase_end(eng, n):
            eng.drain().then_inc(phase_ends, 1)
            eng.wait_ge(phase_ends, 5 * n)

        def wait_from_one(eng, s, n):
            if not (isinstance(n, int) and n == 0):
                eng.wait_ge(s, n)

        def passed(eng, sems, i, v, back=0, by=1):
            w = v - back
            n = by * (i + 1) if w >= 0 else by * i
            wait_from_one(eng, sems[w % SLOTS], n)

        def at(i, v):
            return (i, v) if v in range(SLOTS) else (i + v // SLOTS, v % SLOTS)

        def bases(eng, regs, i, v0=0):
            eng.load(regs, base_row[0:1, bass.ds(SLOTS * i + v0, SLOTS)])
            return [eng.snap(r, min_val=0, max_val=N - 1) for r in regs]

        def unit_block(i, v):
            return GRP * (v % 2) + 2 * i + v // 2

        def unit(q):
            return 2 * (q // 4) + q % 2

        def a_bases(eng, regs, i):
            eng.load(regs, base_a[0:1, bass.ds(8 * i, 8)])
            return [eng.snap(r, min_val=0, max_val=N - 1) for r in regs]

        STEPS5 = [(n, h, *CHUNKS[c]) for n, (h, c) in enumerate((h, c) for h in range(2) for c in range(NC))]

        def x1_t(n):
            return arena[:, 8000 + 512 * (n % 2):8512 + 512 * (n % 2)]

        def proj(n):
            return arena[:, 2752 + 512 * (n % 2):3264 + 512 * (n % 2)]

        def stores(h, u):
            return [n for n, hh, _, _ in STEPS5 if hh == h and n % 2 == u]

        BEGUN = 3

        def sum_bank(call, c):
            return 6 if (call, c) == (2, 2) else c % 2

        class Count:
            def __init__(self, eng, s):
                self.eng, self.s, self.n = eng, s, 0

            def add(self, inst):
                self.n += 1
                inst.then_inc(self.s, 1)

            def wait(self):
                self.eng.wait_ge(self.s, self.n)

        def over(b, nt):
            return b[:, :].rearrange("p (a d) -> p a d", a=1).broadcast_to([P, nt, D])

        def x1_wait(eng, c):
            eng.wait_ge(x1_loaded[c > 0], 16 if c == 0 else 16 * (NC - 1))

        def bcast(v, n=P):
            return v.rearrange("(a d) -> a d", a=1).broadcast_to([n, v.shape[0]])

        def col(v):
            return v.rearrange("(d a) -> d a", a=1)

        ONES, X, H, MLP, X2, X3 = range(SCANS)

        def scan_end(eng, n):
            eng.drain().then_inc(scan_ends, 1)
            eng.wait_ge(scan_ends, 5 * n)

        def scan(eng, s, tile, before=None, after=None):
            if before is not None:
                before()
            scan_end(eng, 2 * s + 1)
            tile(s, 0, P, True, False)
            with eng.Fori(1, ET - 1) as i:
                tile(s, i, P, False, False)
            tile(s, ET - 1, ETAIL, False, True)
            if after is not None:
                after()
            scan_end(eng, 2 * s + 2)

        def loaded(s):
            return 16 * (3 if s == MLP else 2)

        def is_general(eng):
            eng.wait_ge(general_ready, 1)
            r = eng.alloc_register(f"general_{eng.engine.name}")
            eng.load([r], general[0:1, 0:1])
            return r

        @block.sync
        def _(sp):
            def block_rows(dst, src, s):
                last = (NB - 1 - GRP) * 512
                v = src[0:(NB - 1) * BLK].rearrange("(s e) -> s e", e=BLK)
                sp.dma_start(dst[0:GRP, 0:512], v[0:GRP]).then_inc(s, 16)
                sp.dma_start(dst[0:GRP - 1, 512:1024], v[GRP:NB - 1]).then_inc(s, 16)
                sp.dma_start(dst[GRP - 1:GRP, 512:1024],
                             src[E - BLK:E].rearrange("(s e) -> s e", s=1)).then_inc(s, 16)

            block_rows(raw_src, t["src"], loads[0])
            block_rows(raw_dst, t["dst"], loads[1])
            with nc.allow_non_contiguous_dma(reason="one word per block"):
                for r in range(2):
                    d = base_a.rearrange("a (n r) -> a r n", r=2)[:, r, :]
                    n = NB if r == 0 else NB - 2
                    sp.dma_start(d[:, 0:n], t["dst"][r * NB * SUB:(r * NB + n) * SUB]
                                 .rearrange("(n e) -> e n", e=SUB)[0:1, :]).then_inc(loads[2], 16)
                sp.dma_start(d[:, NB - 2:NB], t["dst"][E - BLK:E].rearrange("(n e) -> e n", e=SUB)[0:1, :]
                             ).then_inc(loads[2], 16)
                sp.dma_start(base_row[0:1, 0:NB - 1],
                             t["dst"][0:(NB - 1) * BLK].rearrange("(s e) -> e s", e=BLK)[0:1, :]).then_inc(loads[2], 16)
            sp.dma_start(base_row[0:1, NB - 1:NB], t["dst"][E - BLK:E - BLK + 1].rearrange("(s e) -> e s", e=1)).then_inc(loads[2], 16)

            def load_nodes(dst, src, s):
                sp.dma_start(dst[:, 0:NT - 1, :],
                             src[0:(NT - 1) * P, :].rearrange("(k p) d -> p k d", p=P)).then_inc(s, 16)
                sp.dma_start(dst[0:TAIL, NT - 1, :], src[(NT - 1) * P:N, :]).then_inc(s, 16)

            sp.wait_ge(g_own, 1)
            load_nodes(xn, t["x"], loads[3])
            sp.dma_start(w_a[:, :], t["L0_gnn_W_self1"]).then_inc(loads[4], 16)
            sp.dma_start(w_b[:, :], t["L0_gnn_W_neigh1"]).then_inc(loads[4], 16)
            sp.dma_start(bias_b[:, :], bcast(t["L0_gnn_b1"])).then_inc(loads[4], 16)
            sp.sem_inc(oh_used, 4)
            sp.sem_inc(adj_written, 2)
            sp.wait_ge(loads[2], 80)
            for n in range(1, 3):
                phase_end(sp, n)

            def scan_tile(s, i, n, first, last):
                if not (s == 0 and first):
                    sp.wait_ge(hot_used, s * ET + i)
                with nc.allow_non_contiguous_dma(reason="one word per edge"):
                    for dst, src in ((g_src, t["src"]), (g_dst, t["dst"])):
                        sp.dma_start(dst[0:n, :], src[bass.ds(i * P, n)].rearrange("(e a) -> e a", a=1)
                                     ).then_inc(tile_loaded[s], 16)
                if s == MLP:
                    sp.dma_start(g_e[0:n, :], t["edge_attr_64"][bass.ds(i * P, n), :]).then_inc(tile_loaded[s], 16)

            def store_table(rows, n):
                def store():
                    sp.dma_start(table_d[:, :].rearrange("(k p) d -> p k d", p=P), rows).then_inc(table_stored, 16)
                    sp.wait_ge(table_stored, 16 * n)
                return store

            flag = is_general(sp)
            with sp.If_ne(flag, 0):
                scan(sp, ONES, scan_tile)
                scan(sp, X, scan_tile)
            phase_end(sp, 3)
            sp.dma_start(w_a[:, :], t["L0_gnn_W_self2"]).then_inc(loads[4], 16)
            sp.dma_start(w_b[:, :], t["L0_gnn_W_neigh2"]).then_inc(loads[4], 16)
            sp.dma_start(bias_b[:, :], bcast(t["L0_gnn_b2"])).then_inc(loads[4], 16)
            sp.wait_ge(res_ready, 2 * NC)
            with sp.If_ne(flag, 0):
                scan(sp, H, scan_tile, before=store_table(xn, 1))
            load_nodes(xn, t["x"], loads[3])
            phase_end(sp, 4)
            sp.dma_start(w_a[:, :], t["L1_gnn_W1"][0:D, :]).then_inc(loads[4], 16)
            sp.dma_start(w_b[:, :], t["L1_gnn_W1"][D:2 * D, :]).then_inc(loads[4], 16)
            sp.dma_start(x1_d[:, :].rearrange("(k p) d -> p k d", p=P), xn).then_inc(loads[5], 16)
            sp.dma_start(w_c[:, :], t["L1_gnn_W2"]).then_inc(loads[6], 16)
            sp.dma_start(cols[:, 0:1], col(t["L1_gnn_b1"])).then_inc(loads[6], 16)
            sp.dma_start(bias_b[:, :], bcast(t["L1_gnn_b2"])).then_inc(loads[6], 16)
            for u in range(2):
                sp.dma_start(w_e[u][0:R, :], t["L1_gnn_W1"][2 * D:2 * D + R, :]).then_inc(loads[6], 16)

            def features(i, v, last=False):
                e0 = E - BLK if last else (SLOTS * i + v) * BLK
                passed(sp, ec_used, i, v, back=2)
                sp.dma_start(ec[v % 2][:, :, 0:R],
                             t["edge_attr_64"][bass.ds(e0, BLK), :].rearrange("(j p) f -> p j f", p=P)
                             ).then_inc(ec_loaded[v], 16)

            for v in range(2):
                features(0, v)
            base_regs = [sp.alloc_register(f"sp_base{v}") for v in range(SLOTS)]
            first_bases = bases(sp, base_regs, 0)
            for n, h, k0, nt in STEPS5:
                sp.wait_ge(proj_out, n + 1)
                sp.dma_start((xa_d, xb_d)[h][k0 * P:(k0 + nt) * P, :].rearrange("(k p) d -> p k d", p=P),
                             proj(n)[:, 0:nt * D].rearrange("p (k d) -> p k d", d=D)).then_inc(stored[h][n % 2], 16)
            for h in range(2):
                for u in range(2):
                    sp.wait_ge(stored[h][u], 16 * len(stores(h, u)))
            sp.wait_ge(loads[5], 16)
            phase_end(sp, 5)

            def for_update():
                sp.dma_start(w_a[:, :], t["L1_gnn_Wn"]).then_inc(update_loaded, 16)
                sp.dma_start(gamma_b[:, :], bcast(t["L1_gnn_gamma"])).then_inc(update_loaded, 16)
                sp.dma_start(beta_b[:, :], bcast(t["L1_gnn_beta"])).then_inc(update_loaded, 16)

            def edge_loads(i, v, b, last=False):
                if not (isinstance(i, int) and i == 0 and v < 2):
                    features(i, v, last)
                passed(sp, z_ready, i, v, back=2)
                sp.dma_start(w_e[v % 2][R:KE, :], xb_d[bass.ds(b, WIN), :]).then_inc(w_loaded[v], 16)

            with sp.If_ne(flag, 0):
                for_update()
                scan(sp, MLP, scan_tile)
            with sp.Else():
                for v in range(SLOTS):
                    edge_loads(0, v, first_bases[v])
                for_update()
                with sp.Fori(1, NB // SLOTS - 1) as i:
                    b = bases(sp, base_regs, i)
                    for v in range(SLOTS):
                        edge_loads(i, v, b[v])
                b = bases(sp, base_regs, NB // SLOTS - 1)
                for v in range(SLOTS):
                    edge_loads(NB // SLOTS - 1, v, b[v], last=(v == SLOTS - 1))
            phase_end(sp, 6)
            sp.dma_start(bias_b[:, :], bcast(t["L1_gnn_bn"])).then_inc(bn_loaded, 16)
            for c, (k0, nt) in enumerate(CHUNKS):
                sp.dma_start(x1[c], x1_d[k0 * P:(k0 + nt) * P, :].rearrange("(k p) d -> p k d", p=P)
                             ).then_inc(x1_loaded[c > 0], 16)
            sp.dma_start(w_b[:, :], t["L2_gnn_W"]).then_inc(loads[7], 16)
            sp.wait_ge(low_ready, 3 * NC)
            sp.dma_start(bias_b[:, :], bcast(t["L2_gnn_b"])).then_inc(loads[8], 16)
            sp.dma_start(gamma_b[:, :], bcast(t["L2_gnn_gamma"])).then_inc(loads[8], 16)
            sp.dma_start(beta_b[:, :], bcast(t["L2_gnn_beta"])).then_inc(loads[8], 16)

            def store_scaled():
                sp.wait_ge(gx_ready, 1)
                store_table(g_x, 2)()

            with sp.If_ne(flag, 0):
                scan(sp, X2, scan_tile, before=store_scaled)
            phase_end(sp, 7)
            sp.dma_start(w_b[:, :], t["L3_gnn_W"]).then_inc(loads[9], 16)
            sp.dma_start(cols[:, 0:1], col(t["L3_gnn_b"])).then_inc(loads[9], 16)
            sp.dma_start(cols[:, 1:2], col(t["L3_gnn_gamma"])).then_inc(loads[9], 16)
            sp.dma_start(cols[:, 2:3], col(t["L3_gnn_beta"])).then_inc(loads[9], 16)
            sp.dma_start(cols[:, 3:4], bcast(t["L3_gnn_gin_eps"])).then_inc(loads[9], 16)
            with sp.If_ne(flag, 0):
                scan(sp, X3, scan_tile, before=store_table(xn, 3))
            phase_end(sp, 8)
            for g, (k0, nt) in enumerate(PAIR):
                sp.wait_ge(out_ready, g + 1)
                if nt == 2 * CH:
                    sp.dma_start(out[k0 * P:(k0 + nt) * P, :].rearrange("(k p) d -> p k d", p=P),
                                 xn[:, k0:k0 + nt, :]).then_inc(out_stored, 16)
                else:
                    sp.dma_start(out[k0 * P:N, :], xn[0:TAIL, k0, :]).then_inc(out_stored, 16)
            sp.wait_ge(out_stored, 16 * len(PAIR))

        @block.gpsimd
        def _(pool):
            g = Count(pool, g_own)
            g.add(pool.memset(xn[:, NT - 1, :], 0.0))
            g.add(pool.memset(ident_f[:, :], 0.0))
            g.add(pool.memset(ident_h[:, :], 0.0))
            g.wait()
            g.add(pool.affine_select(out=ident_f[:, :], in_=ident_f[:, :], compare_op=ALU.not_equal, fill=1.0,
                                     base=0, pattern=[[-1, P]], channel_multiplier=1))
            g.add(pool.affine_select(out=ident_h[:, :], in_=ident_h[:, :], compare_op=ALU.not_equal, fill=1.0,
                                     base=0, pattern=[[-1, P]], channel_multiplier=1))
            g.add(pool.iota(iota_c, pattern=[[1, NT * WIN_A]], base=0, channel_multiplier=0))
            g.add(pool.iota(win_i[:, :], pattern=[[1, WIN]], base=0, channel_multiplier=0,
                            allow_small_or_imprecise_dtypes=True))
            g.add(pool.memset(ones_h[:, :], 1.0))
            g.add(pool.iota(iota_j, pattern=[[1, P], [0, J]], base=0, channel_multiplier=0,
                            allow_small_or_imprecise_dtypes=True))
            pool.memset(words(8, 20), 0)
            phase_end(pool, 1)
            phase_end(pool, 2)

            def scan_tile(s, i, n, first, last):
                pool.wait_ge(tile_loaded[s], loaded(s) * (i + 1))
                if s == ONES:
                    return
                pool.sem_inc(gather_mark, 1)
                table = {X: t["x"], MLP: xa_d[:, :]}.get(s, table_d[:, :])
                pool.indirect_dma_start(out=g_rows[0:n, :], out_offset=None, in_=table,
                                        in_offset=bass.IndirectOffsetOnAxis(ap=g_src[0:n, 0:1], axis=0)
                                        ).then_inc(rows_gathered[s], 16)
                if s == MLP:
                    pool.indirect_dma_start(out=g_rows_b[0:n, :], out_offset=None, in_=xb_d[:, :],
                                            in_offset=bass.IndirectOffsetOnAxis(ap=g_dst[0:n, 0:1], axis=0)
                                            ).then_inc(rows_gathered[s], 16)

            def node_iota():
                g.add(pool.iota(g_iota, pattern=[[1, NP]], base=0, channel_multiplier=0,
                                allow_small_or_imprecise_dtypes=True))

            flag = is_general(pool)
            with pool.If_ne(flag, 0):
                for n in (1, 2):
                    if n == 1:
                        node_iota()
                    scan_end(pool, n)
                scan(pool, X, scan_tile)
            phase_end(pool, 3)
            with pool.If_ne(flag, 0):
                scan(pool, H, scan_tile)
            phase_end(pool, 4)
            pool.drain().then_inc(phase_ends, 1)
            for u in range(2):
                pool.wait_ge(stored[0][u], 16 * len(stores(0, u)))

            def gather(i, v):
                passed(pool, idx_ready, i, v)
                wait_from_one(pool, zt_ready[v], i)
                pool.sem_inc(gather_mark, 1)
                for j in range(J):
                    pool.indirect_dma_start(out=z_e[v][:, j * D:(j + 1) * D], out_offset=None, in_=xa_d[:, :],
                                            in_offset=bass.IndirectOffsetOnAxis(ap=idx[:, v, j:j + 1], axis=0)
                                            ).then_inc(g_loaded[v], 16)

            with pool.If_ne(flag, 0):
                scan(pool, MLP, scan_tile)
            with pool.Else():
                for v in range(SLOTS):
                    gather(0, v)
                with pool.Fori(1, NB // SLOTS) as i:
                    for v in range(SLOTS):
                        gather(i, v)
            phase_end(pool, 6)
            pool.wait_ge(update_loaded, 48)
            for c, (k0, nt) in enumerate(CHUNKS):
                x1_wait(pool, c)
                pool.wait_ge(lin_used, 2 * NC + c + 1)
                pool.tensor_tensor(x1[c], x1[c], over(beta_b, nt), ALU.add).then_inc(xb_ready, 1)
            with pool.If_ne(flag, 0):
                scan(pool, X2, scan_tile)
            phase_end(pool, 7)
            with pool.If_ne(flag, 0):
                scan(pool, X3, scan_tile)
            phase_end(pool, 8)

        @block.tensor
        def _(pe):
            pe.wait_ge(prep_ready, 1)
            pe.wait_ge(g_own, 9)
            n = 0
            for half in range(2):
                for a, v in enumerate((p_comb, p_lo, p_drel, p_src)):
                    if n >= 2:
                        pe.wait_ge(prep_out, n - 1)
                    for j in range(J):
                        c0 = 512 * half + j * P
                        last = pe.transpose(ps[:, n % 2, GRP * j:GRP * (j + 1)], v[0:GRP, c0:c0 + P],
                                            ident_f[0:GRP, 0:GRP])
                    last.then_inc(prep_t, 1)
                    n += 1
            phase_end(pe, 1)

            a_regs = [pe.alloc_register(f"pe_a{q}") for q in range(8)]
            base_regs = a_regs[:SLOTS]

            def counts(i, q, b):
                v, h = unit(q), q % 4 // 2
                if h == 0:
                    pe.wait_ge(oh_ready, 4 * i + v + 1)
                for j in (2 * h, 2 * h + 1):
                    last = pe.matmul(ps[:, q, 0:NT * WIN_A], oh_src[v][:, :, j], oh_dst[v][:, j, :],
                                     start=(j == 2 * h), stop=False)
                if h == 1:
                    last.then_inc(oh_used, 1)
                pe.wait_ge(adj_written, 8 * i + q + 1)
                pe.matmul(ps[:, q, 0:NT * WIN_A], ident_h[:, :], adj[:, :, bass.ds(b, WIN_A)],
                          start=False, stop=True).then_inc(cnt_ready, 1)

            with pe.Fori(0, GRP // 2) as i:
                b = a_bases(pe, a_regs, i)
                for q in range(8):
                    counts(i, q, b[q])
            phase_end(pe, 2)

            for k in range(NT):
                for q in range(NT):
                    last = pe.matmul(ps[:, 7, k:k + 1], adj[:, q, k * P:(k + 1) * P], ones_h[:, 0:1],
                                     start=(q == 0), stop=(q == NT - 1))
            last.then_inc(deg_ready, 1)

            def scan_tile(s, i, n, first, last):
                pe.wait_ge(hot_ready, s * ET + i + 1)
                rows = {ONES: g_ones, MLP: g_msg}.get(s, g_rows)
                if s == MLP:
                    pe.wait_ge(tile_loaded[s], loaded(s) * (i + 1))
                    pe.matmul(ps[0:R, 7, 0:n], g_e[0:n, :], ident_f[0:n, 0:n], start=True, stop=True).then_inc(tile_pe, 1)
                    pe.wait_ge(tile_act, 3 * i + 1)
                    pe.matmul(ps[0:n, 7, D:2 * D], g_e_t[0:R, 0:n], w_e[0][0:R, :], start=True, stop=True
                              ).then_inc(tile_pe, 1)
                    pe.wait_ge(tile_dve, 3 * i + 2)
                    pe.transpose(ps[:, 7, 2 * P:2 * P + n], g_z[0:n, :], ident_f[0:n, 0:n]).then_inc(tile_pe, 1)
                    pe.wait_ge(tile_act, 3 * i + 2)
                    pe.matmul(ps[0:n, 7, 3 * D:4 * D], g_h[:, 0:n], w_c[:, :], start=True, stop=True
                              ).then_inc(tile_pe, 1)
                    pe.wait_ge(tile_act, 3 * i + 3)
                elif s != ONES:
                    pe.wait_ge(rows_gathered[s], 16 * (i + 1))
                for c, (k0, nt) in enumerate(CHUNKS):
                    done = pe.matmul(ps[:, c, 0:nt * P], rows[0:n, :], g_hot[0:n, k0 * P:(k0 + nt) * P],
                                     start=first, stop=last)
                done.then_inc(hot_used, 1)

            def degrees():
                for k in range(NT):
                    pe.matmul(ps[:, 7, k:k + 1], g_agg[0:1, k * P:(k + 1) * P], g_ones[0:1, 0:1],
                              start=True, stop=True)

            def summed(call, i, u, c0, nt):
                w = nt * P
                b = sum_bank(call, 2 * i + u) if isinstance(i, int) else u
                pe.wait_ge(low_ready, (call + 1) * NC)
                wait_from_one(pe, agg_out, call * NC + 2 * i)
                pe.matmul(ps[:, b, 0:w], ident_f[:, :], g_agg[:, bass.ds(c0, w)], start=True, stop=True
                          ).then_inc(agg_ready, 1)

            def aggregate(call, i, u, c0, nt):
                w = nt * P
                wait_from_one(pe, agg_out, call * NC + 2 * i)
                for k in range(NT):
                    if u == 0 and k % CH == 0:
                        pe.wait_ge(low_ready, call * NC + k // CH + 1)
                    for q in range(3):
                        last = pe.matmul(ps[:, u, 0:w], parts[q][:, k, :], adj[:, k, bass.ds(c0, w)],
                                         start=(k == 0 and q == 0), stop=(k == NT - 1 and q == 2))
                last.then_inc(agg_ready, 1)

            def own_t(call, c, nt):
                wait_from_one(pe, self_out, call * NC + c)
                for j in range(nt):
                    for q in range(3):
                        last = pe.matmul(ps[:, 2, j * P:(j + 1) * P],
                                         parts[q][:, bass.ds(CH * c + j, 1), :].rearrange("p a d -> p (a d)"),
                                         ident_h[:, :], start=(q == 0), stop=(q == 2))
                last.then_inc(self_ready, 1)

            def pair(call, linear, aggregate, i, begun=0):
                for u in range(2):
                    if not (isinstance(i, int) and 2 * i + u < begun):
                        aggregate(call, i, u, (2 * i + u) * CH * P, CH)
                    if u == 0:
                        own_t(call, 2 * i, CH)
                linear(call, 2 * i, CH)
                own_t(call, 2 * i + 1, CH)
                linear(call, 2 * i + 1, CH)

            def layer(call, linear, aggregate, peeled=0, begun=0):
                for i in range(peeled):
                    pair(call, linear, aggregate, i, begun)
                with pe.Fori(peeled, PAIRS) as i:
                    pair(call, linear, aggregate, i)
                k0, nt = CHUNKS[-1]
                aggregate(call, PAIRS, 0, k0 * P, nt)
                own_t(call, NFULL, nt)
                linear(call, NFULL, nt)

            def sage(call, c, nt):
                n0 = call * NC
                wait_from_one(pe, lin_used, n0 + c)
                pe.wait_ge(self_out, n0 + c + 1)
                for j in range(nt):
                    pe.matmul(ps[:, 3, j * D:(j + 1) * D], self_t[:, j * P:(j + 1) * P], w_a[:, :],
                              start=True, stop=True)
                pe.wait_ge(agg_out, n0 + c + 1)
                for j in range(nt):
                    last = pe.matmul(ps[:, 4, j * D:(j + 1) * D], agg_t[:, j * P:(j + 1) * P], w_b[:, :],
                                     start=True, stop=True)
                last.then_inc(lin_ready, 1)

            pe.wait_ge(off_ready, 1)
            pe.transpose(ps[0:1, 7, P:2 * P], off[:, 0:1], ident_f[:, :]).then_inc(off_t, 1)
            flag = is_general(pe)
            pe.wait_ge(loads[4], 48)
            with pe.If_ne(flag, 0):
                scan(pe, ONES, scan_tile)
                scan(pe, X, scan_tile, before=degrees)
                layer(0, sage, summed, peeled=1)
            with pe.Else():
                layer(0, sage, aggregate, peeled=1)
            phase_end(pe, 3)
            pe.wait_ge(loads[4], 96)
            with pe.If_ne(flag, 0):
                scan(pe, H, scan_tile)
                layer(1, sage, summed)
            with pe.Else():
                layer(1, sage, aggregate)
            phase_end(pe, 4)

            pe.wait_ge(loads[4], 128)

            def x1_transposed(n, k0, nt):
                if n >= 2:
                    pe.wait_ge(proj_ts, n - 1)
                for j in range(nt):
                    last = pe.transpose(ps[:, n % 2, j * P:(j + 1) * P], xn[:, k0 + j, :], ident_f[:, :])
                last.then_inc(proj_t, 1)

            x1_transposed(0, *CHUNKS[0])
            for n, h, k0, nt in STEPS5:
                if n + 1 < len(STEPS5):
                    x1_transposed(n + 1, *STEPS5[n + 1][2:])
                pe.wait_ge(proj_ts, n + 1)
                if n >= 2:
                    pe.wait_ge(proj_out, n - 1)
                for j in range(nt):
                    last = pe.matmul(ps[:, 2 + n % 2, j * D:(j + 1) * D], x1_t(n)[:, j * P:(j + 1) * P],
                                     (w_a, w_b)[h][:, :], start=True, stop=True)
                last.then_inc(proj_ready, 1)
            phase_end(pe, 5)

            pe.wait_ge(loads[6], 80)

            def inputs_t(i, v):
                passed(pe, ec_loaded, i, v, by=16)
                passed(pe, ec_onehot, i, v)
                passed(pe, ect_out, i, v, back=2)
                for j in range(J):
                    last = pe.transpose(ps[0:KE, v % 2, j * P:(j + 1) * P], ec[v % 2][:, j, :], ident_f[:, :])
                last.then_inc(ec_used[v], 1)

            def hidden(i, v):
                passed(pe, ect_out, i, v)
                passed(pe, w_loaded, i, v, by=16)
                passed(pe, z_sum, i, v, back=2)
                for j in range(J):
                    last = pe.matmul(ps[:, 2 + v % 2, j * P:(j + 1) * P], ec_t[v % 2][0:KE, j * P:(j + 1) * P],
                                     w_e[v % 2][0:KE, :], start=True, stop=True)
                last.then_inc(z_ready[v], 1)

            def hidden_t(i, v):
                passed(pe, z_sum, i, v)
                passed(pe, h_ready, i, v, back=1)
                for j in range(J):
                    last = pe.transpose(ps[:, 4, j * P:(j + 1) * P], z_e[v][:, j * P:(j + 1) * P], ident_f[:, :])
                last.then_inc(zt_ready[v], 1)

            def messages(i, v):
                passed(pe, h_ready, i, v)
                passed(pe, m_sum, i, v, back=2)
                for j in range(J):
                    last = pe.matmul(ps[:, 5 + v % 2, j * P:(j + 1) * P], h_t[v % 2][:, j * P:(j + 1) * P], w_c[:, :],
                                     start=True, stop=True)
                last.then_inc(m_ready[v], 1)

            def window(i, v):
                passed(pe, msg_ready, i, v)
                passed(pe, oh_e_ready, i, v)
                passed(pe, win_added, i, v, back=1)
                for j in range(J):
                    last = pe.matmul(ps[:, 7, 0:WIN], msg[v % 2][:, j * P:(j + 1) * P], oh_e[v][:, j, :],
                                     start=(j == 0), stop=(j == J - 1))
                last.then_inc(win_ready[v], 1)

            def step(i, v, first=False, left=2):
                if left >= 1:
                    hidden(*at(i, v + 1))
                hidden_t(i, v)
                if left >= 2:
                    inputs_t(*at(i, v + 2))
                if not first:
                    window(*at(i, v - 1))
                messages(i, v)

            with pe.If_ne(flag, 0):
                scan(pe, MLP, scan_tile)
            with pe.Else():
                inputs_t(0, 0)
                hidden(0, 0)
                inputs_t(0, 1)
                step(0, 0, first=True)
                for v in range(1, SLOTS + 1):
                    step(*at(0, v))
                with pe.Fori(1, NB // SLOTS - 1) as i:
                    for v in range(1, SLOTS + 1):
                        step(*at(i, v))
                for v in range(1, SLOTS):
                    step(NB // SLOTS - 1, v, left=SLOTS - 1 - v)
                window(NB // SLOTS - 1, SLOTS - 1)
            phase_end(pe, 6)

            pe.wait_ge(update_loaded, 48)
            pe.wait_ge(bn_loaded, 16)

            def update(c):
                if c >= 4:
                    pe.wait_ge(lin_used, 2 * NC + c - 3)
                for j in range(CHUNKS[c][1]):
                    k = CHUNKS[c][0] + j
                    o = ps[:, 2 + c % 4, j * D:(j + 1) * D]
                    pe.matmul(o, agg_all[:, k * P:(k + 1) * P], w_a[:, :], start=True, stop=False)
                    last = pe.matmul(o, ident_f[:, :], bias_b[:, :], start=False, stop=True)
                last.then_inc(lin_ready, 1)

            def transposed_weight(loaded, n):
                pe.wait_ge(loaded, n)
                pe.transpose(ps[:, 7, 0:P], w_b[:, :], ident_f[:, :]).then_inc(proj_t, 1)

            def begin_gcn():
                for c in range(4):
                    update(c)
                for c, (k0, nt) in enumerate(CHUNKS):
                    if c + 4 < NC:
                        update(c + 4)
                    if c == 1:
                        transposed_weight(loads[7], 16)
                    pe.wait_ge(low_ready, 2 * NC + c + 1)
                    for k in range(k0, k0 + nt):
                        for u in range(BEGUN):
                            for q in range(3):
                                last = pe.matmul(ps[:, sum_bank(2, u), :], parts[q][:, k, :], adj[:, k, u * CH * P:(u + 1) * CH * P],
                                                 start=(k == 0 and q == 0), stop=(k == NT - 1 and q == 2))
                            if k == NT - 1:
                                last.then_inc(agg_ready, 1)

            def gcn(call, c, nt):
                pe.wait_ge(wt_ready, 1)
                pe.wait_ge(lin_used, lin_base[call] + c)
                pe.wait_ge(agg_out, call * NC + c + 1)
                for j in range(nt):
                    last = pe.matmul(ps[:, 4, j * D:(j + 1) * D], agg_t[:, j * P:(j + 1) * P], w_c[:, :],
                                     start=True, stop=True)
                last.then_inc(lin_ready, 1)

            with pe.If_ne(flag, 0):
                for c in range(NC):
                    update(c)
                transposed_weight(loads[7], 16)
                scan(pe, X2, scan_tile)
                layer(2, gcn, summed, peeled=2)
            with pe.Else():
                begin_gcn()
                layer(2, gcn, aggregate, peeled=2, begun=BEGUN)
            phase_end(pe, 7)
            transposed_weight(loads[9], 80)

            def gin(call, c, nt):
                pe.wait_ge(wt_ready, 2)
                wait_from_one(pe, gin_out, c)
                pe.wait_ge(agg_out, call * NC + c + 1)
                pe.matmul(ps[:, 4, 0:nt * P], w_c[:, :], agg_t[:, 0:nt * P], start=True, stop=True
                          ).then_inc(gin_ready, 1)

            with pe.If_ne(flag, 0):
                scan(pe, X3, scan_tile)
                layer(3, gin, summed, peeled=1)
            with pe.Else():
                layer(3, gin, aggregate, peeled=1)
            phase_end(pe, 8)
            pe.wait_ge(twice_ready, 1)
            for g, (k0, nt) in enumerate(PAIR):
                pe.wait_ge(bn_relu, g + 1)
                if g >= 2:
                    pe.wait_ge(out_ready, g - 1)
                for j in range(nt):
                    k = k0 + j
                    o = ps[:, 2 * (g % 2) + j // CH, (j % CH) * D:(j % CH + 1) * D]
                    for q in range(3):
                        pe.matmul(o, ident_h[:, :], parts[q][:, k, :], start=(q == 0), stop=False)
                    last = pe.matmul(o, agg_all[:, k * P:(k + 1) * P], ident_f[:, :], start=False, stop=True)
                last.then_inc(fin_ready, 1)

        @block.scalar
        def _(act):
            def zero(k0, k1):
                out = words(k0, k1).bitcast(F32)
                act.activation(out, cols[:, 6:7].broadcast_to([P, (k1 - k0) * NP // 2]), ACT.Copy)

            act.wait_ge(zero_ready, 1)
            zero(3, 8)
            for n in range(8):
                half, a = n // 4, n % 4
                dst = (comb, lo_h, drel, src_idx)[a]
                act.wait_ge(prep_t, n + 1)
                act.activation(dst[:, GRP * half:GRP * (half + 1), :],
                               ps[:, n % 2, 0:GRP * J].rearrange("p (j s) -> p s j", j=J), ACT.Copy
                               ).then_inc(prep_out, 1)
            zero(22, 25)
            phase_end(act, 1)

            a_regs = [act.alloc_register(f"act_a{q}") for q in range(8)]

            def to_adj(i, q, b):
                act.wait_ge(cnt_ready, 8 * i + q + 1)
                act.activation(adj[:, :, bass.ds(b, WIN_A)],
                               ps[:, q, 0:NT * WIN_A].rearrange("p (k w) -> p k w", w=WIN_A), ACT.Copy
                               ).then_inc(adj_written, 1)

            with act.Fori(0, GRP // 2) as i:
                b = a_bases(act, a_regs, i)
                for q in range(8):
                    to_adj(i, q, b[q])
            phase_end(act, 2)

            def split(call, scale=None):
                for c, (k0, nt) in enumerate(CHUNKS):
                    if scale is None:
                        act.activation(parts[0][:, k0:k0 + nt, :], xn[:, k0:k0 + nt, :], ACT.Copy).then_inc(hi_ready, 1)
                    else:
                        for k in range(k0, k0 + nt):
                            last = act.activation(parts[0][:, k, :], xn[:, k, :], ACT.Copy, scale=scale[:, k:k + 1])
                        last.then_inc(hi_ready, 1)
                for c, (k0, nt) in enumerate(CHUNKS):
                    act.wait_ge(res_ready, call * NC + c + 1)
                    act.activation(parts[1][:, k0:k0 + nt, :], res[c % 2][:, 0:nt, :], ACT.Copy).then_inc(mid_ready, 1)

            roots = [0]

            def root(nt, o=0):
                roots[0] += 1
                act.wait_ge(var_ready, roots[0])
                act.activation(std[:, o:o + nt], mv[:, o:o + nt, 1], ACT.Sqrt, bias=cols[:, 7:8]).then_inc(std_ready, 1)

            def self_chunks(call, read, n_read, scale=1.0, then=None):
                for c, (k0, nt) in enumerate(CHUNKS):
                    act.wait_ge(self_ready, call * NC + c + 1)
                    act.wait_ge(read, n_read + c)
                    act.activation(self_t[:, 0:nt * P], ps[:, 2, 0:nt * P], ACT.Copy, scale=scale).then_inc(self_out, 1)
                    if then is not None:
                        then(c, k0, nt)

            def scan_tile(s, i, n, first, last):
                if s != MLP:
                    return
                act.wait_ge(tile_pe, 4 * i + 1)
                act.activation(g_e_t[0:R, 0:n], ps[0:R, 7, 0:n], ACT.Copy).then_inc(tile_act, 1)
                act.wait_ge(tile_pe, 4 * i + 3)
                act.activation(g_h[:, 0:n], ps[:, 7, 2 * P:2 * P + n], ACT.Relu, bias=cols[:, 0:1]
                               ).then_inc(tile_act, 1)
                act.wait_ge(tile_dve, 3 * i + 3)
                act.activation(g_msg[0:n, :], g_msg[0:n, :], ACT.Relu).then_inc(tile_act, 1)

            def idle(s):
                scan_end(act, 2 * s + 1)
                scan_end(act, 2 * s + 2)

            act.wait_ge(loads[3], 32)
            split(0)
            flag = is_general(act)
            with act.If_ne(flag, 0):
                idle(ONES)
                idle(X)
            act.wait_ge(deg_ready, 2)
            act.activation(std_deg[:, :], dinv[:, :], ACT.Sqrt).then_inc(deg_ready, 1)

            def relu_pair(c, k0, nt):
                if c % 2 or c == NC - 1:
                    g = c // 2
                    act.wait_ge(lin_used, c + 1)
                    p0, pt = PAIR[g]
                    act.activation(xn[:, p0:p0 + pt, :], node[:, 0:pt, :], ACT.Relu).then_inc(relu_done, 1)

            self_chunks(0, lin_ready, 0, then=relu_pair)
            phase_end(act, 3)

            def root_pair(times):
                def roots_of(c, k0, nt):
                    if c % 2 or c == NC - 1:
                        for _ in range(times):
                            root(PAIR[c // 2][1])
                return roots_of

            split(1)
            with act.If_ne(flag, 0):
                idle(H)
            self_chunks(1, lin_ready, NC, then=root_pair(1))
            phase_end(act, 4)
            for n, h, k0, nt in STEPS5:
                act.wait_ge(proj_t, n + 1)
                if n >= 2:
                    act.wait_ge(proj_ready, n - 1)
                act.activation(x1_t(n)[:, 0:nt * P], ps[:, n % 2, 0:nt * P], ACT.Copy).then_inc(proj_ts, 1)
            phase_end(act, 5)

            act.wait_ge(loads[6], 80)

            def inputs_out(i, v):
                passed(act, ec_used, i, v)
                passed(act, z_ready, i, v, back=2)
                act.activation(ec_t[v % 2][0:KE, :], ps[0:KE, v % 2, :], ACT.Copy).then_inc(ect_out[v], 1)

            def hidden_relu(i, v):
                passed(act, zt_ready, i, v)
                passed(act, m_ready, i, v, back=2)
                act.activation(h_t[v % 2], ps[:, 4, :], ACT.Relu, bias=cols[:, 0:1]).then_inc(h_ready[v], 1)

            def message_relu(i, v):
                passed(act, m_sum, i, v)
                act.activation(msg[v % 2], msg[v % 2], ACT.Relu).then_inc(msg_ready[v], 1)

            def step(i, v, left=2):
                hidden_relu(i, v)
                if left >= 2:
                    inputs_out(*at(i, v + 2))
                message_relu(i, v)

            with act.If_ne(flag, 0):
                scan(act, MLP, scan_tile)
            with act.Else():
                inputs_out(0, 0)
                inputs_out(0, 1)
                for v in range(SLOTS):
                    step(0, v)
                with act.Fori(1, NB // SLOTS - 1) as i:
                    for v in range(SLOTS):
                        step(i, v)
                for v in range(SLOTS):
                    step(NB // SLOTS - 1, v, left=SLOTS - 1 - v)
            phase_end(act, 6)
            norms = [0]

            def norm_factors():
                norms[0] += 1
                act.wait_ge(norm_ready, norms[0])

            def norm_1(c):
                norm_factors()
                for j in range(CHUNKS[c][1]):
                    last = act.activation(node3[c % 3][:, j, :], node3[c % 3][:, j, :], ACT.Identity,
                                          scale=rstd[:, j:j + 1], bias=nbias[:, j:j + 1])
                last.then_inc(normed, 1)

            def norm_2(c):
                k0, nt = CHUNKS[c]
                norm_factors()
                if c >= 3:
                    act.wait_ge(low_ready, 2 * NC + c - 2)
                for j in range(nt):
                    act.activation(res3[c % 3][:, j, :], node3[c % 3][:, j, :], ACT.Identity,
                                   scale=scaled[:, j:j + 1], bias=scaled[:, CH + j:CH + j + 1])
                    last = act.activation(xn[:, k0 + j, :], node3[c % 3][:, j, :], ACT.Identity,
                                          scale=rstd[:, CH + j:CH + j + 1], bias=nbias[:, CH + j:CH + j + 1])
                last.then_inc(xs_ready, 1)
                act.wait_ge(xs_ready, c + 1)
                act.activation(parts[0][:, k0:k0 + nt, :], res3[c % 3][:, 0:nt, :], ACT.Copy).then_inc(hi_ready, 1)

            def mid(c):
                k0, nt = CHUNKS[c]
                act.wait_ge(res_ready, 2 * NC + c + 1)
                act.activation(parts[1][:, k0:k0 + nt, :], res3[c % 3][:, 0:nt, :], ACT.Copy).then_inc(mid_ready, 1)

            for n in range(NC + 2):
                if n < NC:
                    root(CHUNKS[n][1])
                if n - 1 in range(NC):
                    root(CHUNKS[n - 1][1], CH)
                if n < NC:
                    norm_1(n)
                if n - 1 in range(NC):
                    norm_2(n - 1)
                if n >= 2:
                    mid(n - 2)
            act.wait_ge(proj_t, 2 * NC + 1)
            act.activation(w_c[:, :], ps[:, 7, 0:P], ACT.Copy).then_inc(wt_ready, 1)
            with act.If_ne(flag, 0):
                idle(X2)
            def two_roots(c, k0, nt):
                for n in {NC - 2: (CH,), NC - 1: (CH, nt)}.get(c, (2 * CH,) if c % 2 else ()):
                    root(n)
                    root(n)

            self_chunks(2, agg_out, 2 * NC, then=two_roots)
            phase_end(act, 7)
            split(3)
            act.wait_ge(proj_t, 2 * NC + 2)
            act.activation(w_c[:, :], ps[:, 7, 0:P], ACT.Copy).then_inc(wt_ready, 1)
            act.wait_ge(eps_ready, 1)
            with act.If_ne(flag, 0):
                idle(X3)

            def gin_chunk(c, k0, nt):
                act.wait_ge(gin_ready, c + 1)
                act.activation(agg_all[:, k0 * P:(k0 + nt) * P], ps[:, 4, 0:nt * P], ACT.Identity,
                               bias=cols[:, 0:1]).then_inc(gin_out, 1)

            self_chunks(3, agg_out, 3 * NC, scale=cols[:, 4:5], then=gin_chunk)
            root(1)
            phase_end(act, 8)
            for k0, nt in PAIR:
                act.activation(agg_all[:, k0 * P:(k0 + nt) * P], agg_all[:, k0 * P:(k0 + nt) * P], ACT.Relu,
                               bias=cols[:, 6:7], scale=cols[:, 5:6]).then_inc(bn_relu, 1)
            for k0, nt in PAIR:
                root(nt)

        @block.vector
        def _(dve):
            own = Count(dve, v_own)
            dve.memset(cols[:, 7:8], EPS)
            dve.memset(cols[:, 6:7], 0.0).then_inc(zero_ready, 1)
            own.add(dve.memset(off[:, :], 0.0))
            dve.wait_ge(loads[0], 48)
            own.add(dve.tensor_scalar(hi_i[0:GRP, :], raw_src[0:GRP, :], 7, None, ALU.arith_shift_right))
            own.add(dve.tensor_scalar(lo_i[0:GRP, :], raw_src[0:GRP, :], P - 1, None, ALU.bitwise_and))
            own.add(dve.tensor_copy(p_src[0:GRP, :], raw_src[0:GRP, :]))
            dve.wait_ge(loads[1], 48)
            for half in range(2):
                h = slice(512 * half, 512 * half + 512)
                own.add(dve.tensor_scalar(p_drel[0:GRP, h], raw_dst[0:GRP, h],
                                        raw_dst[0:GRP, 512 * half:512 * half + 1], None, ALU.subtract))
            own.wait()
            for h in range(4):
                own.add(dve.tensor_scalar(p_rel[0:GRP, SUB * h:SUB * (h + 1)], raw_dst[0:GRP, SUB * h:SUB * (h + 1)],
                                        raw_dst[0:GRP, SUB * h:SUB * h + 1], None, ALU.subtract))
            firsts = raw_dst[0:GRP, :].rearrange("p (b h e) -> p b h e", h=2, e=SUB)[:, :, :, 0]
            for c, x, y in ((4, 1, 0), (6, 0, 1)):
                own.add(dve.tensor_tensor(off[0:GRP, c:c + 2], firsts[:, :, x], firsts[:, :, y], ALU.subtract))
            own.add(dve.tensor_copy(p_lo[0:GRP, :], lo_i[0:GRP, :]))
            own.wait()
            dve.scalar_tensor_tensor(out=p_comb[0:GRP, :], in0=hi_i[0:GRP, :], scalar=float(WIN_A),
                                     in1=p_rel[0:GRP, :], op0=ALU.mult, op1=ALU.add).then_inc(prep_ready, 1)
            own.add(dve.tensor_reduce(off[0:GRP, 1:2], p_rel[0:GRP, :], mybir.AxisListType.X, ALU.max))
            own.add(dve.tensor_reduce(off[0:GRP, 2:3], p_rel[0:GRP, :], mybir.AxisListType.X, ALU.min))
            own.add(dve.tensor_scalar(off[0:GRP, 4:6], off[0:GRP, 4:6], float(WIN - WIN_A), None, ALU.subtract))
            own.wait()
            own.add(dve.tensor_scalar(off[0:GRP, 1:2], off[0:GRP, 1:2], WIN_A - 1.0, None, ALU.subtract))
            own.add(dve.tensor_scalar(off[0:GRP, 2:3], off[0:GRP, 2:3], -1.0, None, ALU.mult))
            dve.wait_ge(loads[2], 80)
            own.add(dve.tensor_tensor(falls[:, 0:2 * NB - 4], base_a[:, 0:2 * NB - 4], base_a[:, 4:2 * NB], ALU.subtract))
            ends = base_a[:, 2 * NB - 4:2 * NB].rearrange("a (n r) -> a r n", r=2)[:, 0, :]
            starts = base_a[:, 0:4].rearrange("a (n r) -> a r n", r=2)[:, 1, :]
            own.add(dve.tensor_tensor(falls[:, 2 * NB - 4:2 * NB - 2], ends, starts, ALU.subtract))
            own.wait()
            own.add(dve.tensor_reduce(off[0:1, 8:9], falls, mybir.AxisListType.X, ALU.max))
            dve.memset(words(0, 3), 0)
            dve.wait_ge(prep_t, 8)
            own.wait()
            dve.memset(words(20, 22), 0)
            dve.wait_ge(prep_out, 8)
            for a in (comb, drel):
                dve.memset(a[:, NB - 1, 0:DUP // P], -1.0)
                dve.memset(a[0:DUP % P, NB - 1, DUP // P:DUP // P + 1], -1.0)
            phase_end(dve, 1)

            def onehots(i, v):
                s = unit_block(i, v)
                dve.wait_ge(oh_used, 4 * i + v + 1)
                dve.tensor_tensor(oh_src[v], iota_j, lo_h[:, bass.ds(s, 1), :].broadcast_to([P, P, J]), ALU.is_equal)
                for j in range(J):
                    last = dve.tensor_scalar(oh_dst[v][:, j, :], iota_c, comb[:, bass.ds(s, 1), j], None, ALU.is_equal)
                last.then_inc(oh_ready, 1)

            with dve.Fori(0, GRP // 2) as i:
                for v in range(4):
                    onehots(i, v)
            phase_end(dve, 2)

            def split(call, scale=None):
                def low(c):
                    k0, nt = CHUNKS[c]
                    dve.wait_ge(mid_ready, call * NC + c + 1)
                    dve.tensor_tensor(parts[2][:, k0:k0 + nt, :], res[c % 2][:, 0:nt, :], parts[1][:, k0:k0 + nt, :],
                                      ALU.subtract).then_inc(low_ready, 1)

                for c, (k0, nt) in enumerate(CHUNKS):
                    dve.wait_ge(hi_ready, call * NC + c + 1)
                    if c >= 2:
                        dve.wait_ge(low_ready, call * NC + c - 1)
                    if scale is None:
                        last = dve.tensor_tensor(res[c % 2][:, 0:nt, :], xn[:, k0:k0 + nt, :],
                                                 parts[0][:, k0:k0 + nt, :], ALU.subtract)
                    else:
                        for j in range(nt):
                            last = dve.scalar_tensor_tensor(out=res[c % 2][:, j, :], in0=xn[:, k0 + j, :],
                                                            scalar=scale[:, k0 + j:k0 + j + 1], in1=parts[0][:, k0 + j, :],
                                                            op0=ALU.mult, op1=ALU.subtract)
                    last.then_inc(res_ready, 1)
                    if c:
                        low(c - 1)
                low(NC - 1)

            roots = [0]

            def layernorm(src, dst, nt, done=None):
                for j in range(nt):
                    own.add(dve.bn_stats(stats[:, j, :], src[:, j, :]))
                own.wait()
                for j in range(nt):
                    last = dve.bn_aggr(mv[:, j, :], stats[:, j, :])
                last.then_inc(var_ready, 1)
                roots[0] += 1
                dve.wait_ge(std_ready, roots[0])
                own.add(dve.reciprocal(rstd[:, 0:nt], std[:, 0:nt]))
                own.wait()
                for j in range(nt):
                    last = dve.tensor_scalar(dst[:, j, :], src[:, j, :], mv[:, j, 0:1], rstd[:, j:j + 1],
                                             ALU.subtract, ALU.mult)
                    if done is None or j < nt - 1:
                        own.add(last)
                if done is not None:
                    last.then_inc(done, 1)
                own.wait()

            def affine(a, nt):
                for op, b in ((ALU.mult, gamma_b), (ALU.add, beta_b)):
                    own.add(dve.tensor_tensor(a[:, 0:nt, :], a[:, 0:nt, :], over(b, nt), op))
                    own.wait()

            dve.wait_ge(loads[3], 32)
            split(0)
            dve.wait_ge(deg_ready, 1)
            own.add(dve.tensor_reduce(off[:, 3:4], ps[:, 7, 0:NT], mybir.AxisListType.X, ALU.max))
            own.wait()
            own.add(dve.tensor_scalar(off[:, 3:4], off[:, 3:4], 255.0, None, ALU.subtract))
            own.wait()
            dve.tensor_reduce(off[:, 0:1], off[:, 1:9], mybir.AxisListType.X, ALU.max).then_inc(off_ready, 1)
            dve.wait_ge(off_t, 1)
            own.add(dve.tensor_reduce(off[0:1, 3:4], ps[0:1, 7, P:2 * P], mybir.AxisListType.X, ALU.max))
            own.wait()
            dve.tensor_scalar(general[:, :], off[0:1, 3:4], 0.0, None, ALU.is_gt).then_inc(general_ready, 1)

            def scan_tile(s, i, n, first, last):
                dve.wait_ge(tile_loaded[s], loaded(s) * (i + 1))
                dve.tensor_copy(g_dst_f[0:n, :], g_dst[0:n, :]).then_inc(dst_ready, 1)
                dve.wait_ge(dst_ready, s * ET + i + 1)
                if not (s == 0 and first):
                    dve.wait_ge(hot_used, s * ET + i)
                dve.tensor_scalar(g_hot[0:n, :], g_iota[0:n, :], g_dst_f[0:n, 0:1], None, ALU.is_equal
                                  ).then_inc(hot_ready, 1)
                if s == MLP:
                    dve.wait_ge(tile_pe, 4 * i + 2)
                    dve.wait_ge(rows_gathered[s], 32 * (i + 1))
                    for q, rows in enumerate((g_rows, g_rows_b)):
                        z = ps[0:n, 7, D:2 * D] if q == 0 else g_z[0:n, :]
                        if q:
                            dve.wait_ge(tile_dve, 3 * i + 1)
                        dve.tensor_tensor(g_z[0:n, :], z, rows[0:n, :], ALU.add).then_inc(tile_dve, 1)
                    dve.wait_ge(tile_pe, 4 * i + 4)
                    dve.tensor_tensor(g_msg[0:n, :], ps[0:n, 7, 3 * D:4 * D], bias_b[0:n, :], ALU.add
                                      ).then_inc(tile_dve, 1)

            def sums_out(s):
                def leave():
                    dve.wait_ge(hot_used, (s + 1) * ET)
                    dst = agg_all if s == MLP else g_agg
                    for c, (k0, nt) in enumerate(CHUNKS):
                        dve.tensor_copy(dst[:, k0 * P:(k0 + nt) * P], ps[:, c, 0:nt * P])
                return leave

            flag = is_general(dve)
            with dve.If_ne(flag, 0):
                dve.memset(g_ones, 1.0)
                scan(dve, ONES, scan_tile, after=sums_out(ONES))
                scan(dve, X, scan_tile, after=sums_out(X))
            own.add(dve.tensor_scalar(inv_deg[:, :], ps[:, 7, 0:NT], 1.0, None, ALU.max))
            dve.tensor_scalar(dinv[:, :], ps[:, 7, 0:NT], 1.0, None, ALU.add).then_inc(deg_ready, 1)
            own.wait()
            own.add(dve.reciprocal(inv_deg[:, :], inv_deg[:, :]))
            dve.wait_ge(deg_ready, 3)
            dve.reciprocal(dinv[:, :], std_deg[:, :])

            def bank(b, nt):
                return ps[:, b, 0:nt * D].rearrange("p (j d) -> p j d", d=D)

            def combine(call, c):
                k0, nt = CHUNKS[c]
                n = call * NC + c
                half = node[:, CH * (c % 2):CH * (c % 2) + nt, :]
                dve.wait_ge(agg_ready, n + 1)
                dve.wait_ge(lin_ready, n)
                dve.tensor_copy(agg_t[:, 0:nt * P], ps[:, c % 2, 0:nt * P]).then_inc(agg_out, 1)
                dve.wait_ge(lin_ready, n + 1)
                own.add(dve.tensor_tensor(half, bank(3, nt), over(bias_b, nt), ALU.add))
                own.wait()
                for j in range(nt):
                    last = dve.scalar_tensor_tensor(out=half[:, j, :], in0=ps[:, 4, j * D:(j + 1) * D],
                                                    scalar=inv_deg[:, k0 + j:k0 + j + 1], in1=half[:, j, :],
                                                    op0=ALU.mult, op1=ALU.add)
                last.then_inc(lin_used, 1)
                dve.wait_ge(lin_used, n + 1)

            def chunks_of(g):
                return [c for c in (2 * g, 2 * g + 1) if c < NC]

            for g in range(len(PAIR)):
                dve.wait_ge(relu_done, g)
                for c in chunks_of(g):
                    combine(0, c)
            phase_end(dve, 3)
            split(1)
            with dve.If_ne(flag, 0):
                scan(dve, H, scan_tile, after=sums_out(H))
            dve.wait_ge(loads[3], 64)
            for g, (k0, nt) in enumerate(PAIR):
                for c in chunks_of(g):
                    combine(1, c)
                own.add(dve.tensor_tensor(node[:, 0:nt, :], node[:, 0:nt, :], xn[:, k0:k0 + nt, :], ALU.add))
                own.wait()
                layernorm(node, xn[:, k0:k0 + nt, :], nt)
            phase_end(dve, 4)
            def gather_index(i, v, first=False):
                if not first:
                    dve.wait_ge(g_loaded[v], 64 * i)
                dve.tensor_copy(idx[:, v, :], src_idx[:, bass.ds(SLOTS * i + v, 1), :].rearrange("p a j -> p (a j)")
                                ).then_inc(idx_ready[v], 1)

            for v in range(SLOTS):
                gather_index(0, v, first=True)
            for n, h, k0, nt in STEPS5:
                dve.wait_ge(proj_ready, n + 1)
                if n >= 2:
                    hh = STEPS5[n - 2][1]
                    dve.wait_ge(stored[hh][n % 2], 16 * (1 + stores(hh, n % 2).index(n - 2)))
                dve.tensor_copy(proj(n)[:, 0:nt * D], ps[:, 2 + n % 2, 0:nt * D]).then_inc(proj_out, 1)
            phase_end(dve, 5)

            dve.wait_ge(loads[6], 80)

            base_regs = [dve.alloc_register(f"dve_base{v}") for v in range(SLOTS)]

            def block_start(i, v):
                passed(dve, ec_used, i, v, back=2)
                wait_from_one(dve, win_ready[v], i)
                rel = drel[:, bass.ds(SLOTS * i + v, 1), :].rearrange("p a j -> p j a").broadcast_to([P, J, WIN])
                w = win_i[:, :].rearrange("p (a w) -> p a w", a=1).broadcast_to([P, J, WIN])
                dve.tensor_tensor(ec[v % 2][:, :, R:KE], w, rel, ALU.is_equal).then_inc(ec_onehot[v], 1)
                dve.tensor_tensor(oh_e[v], w, rel, ALU.is_equal).then_inc(oh_e_ready[v], 1)

            def add_gathered(i, v):
                passed(dve, z_ready, i, v)
                passed(dve, g_loaded, i, v, by=64)
                dve.tensor_tensor(z_e[v], ps[:, 2 + v % 2, :], z_e[v], ALU.add).then_inc(z_sum[v], 1)

            def add_bias(i, v):
                passed(dve, m_ready, i, v)
                passed(dve, win_ready, i, v, back=2)
                dve.tensor_tensor(msg[v % 2].rearrange("p (j d) -> p j d", d=D), bank(5 + v % 2, J), over(bias_b, J),
                                  ALU.add).then_inc(m_sum[v], 1)

            def add_window(i, v, b):
                passed(dve, win_ready, i, v)
                passed(dve, win_added, i, v, back=1)
                dve.tensor_tensor(agg_all[:, bass.ds(b, WIN)], ps[:, 7, 0:WIN], agg_all[:, bass.ds(b, WIN)], ALU.add
                                  ).then_inc(win_added[v], 1)

            def step(i, v, b=None, left=3, first=False):
                if left >= 1:
                    add_gathered(*at(i, v + 1))
                if b is not None:
                    add_window(*at(i, v - 1), b)
                if left >= 3:
                    if not first:
                        gather_index(*at(i, v + 3))
                    block_start(*at(i, v + 3))
                add_bias(i, v)

            with dve.If_ne(flag, 0):
                scan(dve, MLP, scan_tile, after=sums_out(MLP))
            with dve.Else():
                for v in range(3):
                    block_start(0, v)
                dve.memset(agg_all, 0.0).then_inc(agg_zero, 1)
                dve.wait_ge(agg_zero, 1)
                add_gathered(0, 0)
                step(0, 0, first=True)
                b = bases(dve, base_regs, 0)
                for v in range(1, SLOTS + 1):
                    step(*at(0, v), b[v - 1])
                with dve.Fori(1, NB // SLOTS - 1) as i:
                    b = bases(dve, base_regs, i)
                    for v in range(1, SLOTS + 1):
                        step(*at(i, v), b[v - 1])
                b = bases(dve, base_regs, NB // SLOTS - 1)
                for v in range(1, SLOTS):
                    step(NB // SLOTS - 1, v, b[v - 1], left=SLOTS - 1 - v)
                add_window(NB // SLOTS - 1, SLOTS - 1, b[SLOTS - 1])
            phase_end(dve, 6)

            asked = {}

            def statistics(c, o):
                nt = CHUNKS[c][1]
                for j in range(nt):
                    own.add(dve.bn_stats(stats[:, o + j, :], node3[c % 3][:, j, :]))
                own.wait()
                for j in range(nt):
                    last = dve.bn_aggr(mv[:, o + j, :], stats[:, o + j, :])
                last.then_inc(var_ready, 1)
                roots[0] += 1
                asked[c, o] = roots[0]

            def factors(c, o):
                k0, nt = CHUNKS[c]
                dve.wait_ge(std_ready, asked[c, o])
                own.add(dve.reciprocal(rstd[:, o:o + nt], std[:, o:o + nt]))
                own.wait()
                last = dve.scalar_tensor_tensor(out=nbias[:, o:o + nt], in0=mv[:, o:o + nt, 0], scalar=-1.0,
                                                in1=rstd[:, o:o + nt], op0=ALU.mult, op1=ALU.mult)
                if o:
                    own.add(last)
                    dve.tensor_tensor(scaled[:, 0:nt], rstd[:, o:o + nt], dinv[:, k0:k0 + nt], ALU.mult)
                    own.wait()
                    last = dve.tensor_tensor(scaled[:, CH:CH + nt], nbias[:, o:o + nt], dinv[:, k0:k0 + nt], ALU.mult)
                last.then_inc(norm_ready, 1)

            def residual(c):
                nt = CHUNKS[c][1]
                x1_wait(dve, c)
                dve.wait_ge(lin_ready, 2 * NC + c + 1)
                if c >= 3:
                    dve.wait_ge(hi_ready, 2 * NC + c - 2)
                dve.scalar_tensor_tensor(out=node3[c % 3][:, 0:nt, :], in0=bank(2 + c % 4, nt), scalar=0.0,
                                         in1=x1[c], op0=ALU.max, op1=ALU.add).then_inc(lin_used, 1)
                dve.wait_ge(lin_used, 2 * NC + c + 1)
                statistics(c, 0)

            def residual_2(c):
                nt = CHUNKS[c][1]
                dve.wait_ge(normed, c + 1)
                dve.wait_ge(xb_ready, c + 1)
                for op, b in ((ALU.mult, over(gamma_b, nt)), (ALU.add, x1[c])):
                    own.add(dve.tensor_tensor(node3[c % 3][:, 0:nt, :], node3[c % 3][:, 0:nt, :], b, op))
                    own.wait()
                statistics(c, CH)

            def less_hi(c):
                k0, nt = CHUNKS[c]
                dve.wait_ge(hi_ready, 2 * NC + c + 1)
                dve.tensor_tensor(res3[c % 3][:, 0:nt, :], res3[c % 3][:, 0:nt, :], parts[0][:, k0:k0 + nt, :],
                                  ALU.subtract).then_inc(res_ready, 1)

            def less_mid(c):
                k0, nt = CHUNKS[c]
                dve.wait_ge(mid_ready, 2 * NC + c + 1)
                dve.tensor_tensor(parts[2][:, k0:k0 + nt, :], res3[c % 3][:, 0:nt, :], parts[1][:, k0:k0 + nt, :],
                                  ALU.subtract).then_inc(low_ready, 1)

            for n in range(NC + 3):
                for stage, c in ((residual, n), (residual_2, n - 1), (factors, n), (less_hi, n - 2),
                                 (factors, n - 1), (less_mid, n - 3)):
                    if c not in range(NC):
                        continue
                    if stage is factors:
                        factors(c, 0 if c == n else CH)
                    else:
                        stage(c)

            def scaled_rows():
                for k in range(NT):
                    last = dve.tensor_scalar(g_x[:, k, :], xn[:, k, :], dinv[:, k:k + 1], None, ALU.mult)
                last.then_inc(gx_ready, 1)

            with dve.If_ne(flag, 0):
                scan(dve, X2, scan_tile, before=scaled_rows, after=sums_out(X2))

            def add_self(call, c, read, n_read):
                nt = CHUNKS[c][1]
                n = call * NC + c
                dve.wait_ge(agg_ready, n + 1)
                dve.wait_ge(read, n_read + c)
                dve.wait_ge(self_out, n + 1)
                dve.tensor_tensor(agg_t[:, 0:nt * P], ps[:, sum_bank(call, c), 0:nt * P], self_t[:, 0:nt * P], ALU.add
                                  ).then_inc(agg_out, 1)

            dve.wait_ge(loads[8], 48)

            def gcn_nodes(c):
                k0, nt = CHUNKS[c]
                add_self(2, c, lin_ready, 3 * NC)
                dve.wait_ge(lin_ready, 3 * NC + c + 1)
                for j in range(nt):
                    last = dve.scalar_tensor_tensor(out=node[:, CH * (c % 2) + j, :], in0=ps[:, 4, j * D:(j + 1) * D],
                                                    scalar=dinv[:, k0 + j:k0 + j + 1], in1=bias_b[:, :],
                                                    op0=ALU.mult, op1=ALU.add)
                last.then_inc(lin_used, 1)

            def gcn_norms(c, nt):
                k0 = CHUNKS[c][0]
                some = node[:, CH * (c % 2):CH * (c % 2) + nt, :]
                dve.wait_ge(lin_used, 3 * NC + c + (nt + CH - 1) // CH)
                layernorm(some, some, nt)
                affine(some, nt)
                own.add(dve.tensor_tensor(some, some, xn[:, k0:k0 + nt, :], ALU.add))
                own.wait()
                layernorm(some, xn[:, k0:k0 + nt, :], nt)

            for c in range(0, NC - 3, 2):
                gcn_nodes(c)
                gcn_nodes(c + 1)
                gcn_norms(c, 2 * CH)
            gcn_nodes(NC - 3)
            gcn_nodes(NC - 2)
            gcn_norms(NC - 3, CH)
            gcn_nodes(NC - 1)
            gcn_norms(NC - 2, CH)
            gcn_norms(NC - 1, CHUNKS[-1][1])
            phase_end(dve, 7)

            dve.wait_ge(loads[9], 80)
            dve.tensor_scalar(cols[:, 4:5], cols[:, 3:4], 1.0, None, ALU.add).then_inc(eps_ready, 1)
            split(3)
            with dve.If_ne(flag, 0):
                scan(dve, X3, scan_tile, after=sums_out(X3))

            def zt_stats(c):
                k0, nt = CHUNKS[c]
                dve.wait_ge(gin_out, c + 1)
                w = nt * P if nt == CH else TAIL
                own.add(dve.bn_stats(stats[:, c, :], agg_all[:, k0 * P:k0 * P + w]))

            for c in range(NC):
                add_self(3, c, gin_ready, 0)
                zt_stats(c)
            own.wait()
            dve.bn_aggr(mv[:, 0, :], stats[:, 0:NC, :]).then_inc(var_ready, 1)
            roots[0] += 1
            dve.wait_ge(std_ready, roots[0])
            own.add(dve.reciprocal(rstd[:, 0:1], std[:, 0:1]))
            own.wait()
            own.add(dve.tensor_tensor(cols[:, 5:6], rstd[:, 0:1], cols[:, 1:2], ALU.mult))
            own.wait()
            own.add(dve.tensor_tensor(rstd[:, 1:2], cols[:, 5:6], mv[:, 0, 0:1], ALU.mult))
            own.wait()
            dve.tensor_tensor(cols[:, 6:7], cols[:, 2:3], rstd[:, 1:2], ALU.subtract)
            phase_end(dve, 8)
            dve.tensor_scalar(ident_h[:, :], ident_h[:, :], 2.0, None, ALU.mult).then_inc(twice_ready, 1)
            for g, (k0, nt) in enumerate(PAIR):
                dve.wait_ge(fin_ready, g + 1)
                b = 2 * (g % 2)
                layernorm(ps[:, b:b + 2, :].rearrange("p a (j d) -> p (a j) d", d=D), xn[:, k0:k0 + nt, :], nt, done=out_ready)


_INS = ["x", "src", "dst", "edge_attr_64", "L0_gnn_W_self1", "L0_gnn_W_neigh1", "L0_gnn_b1", "L0_gnn_W_self2",
        "L0_gnn_W_neigh2", "L0_gnn_b2", "L1_gnn_W1", "L1_gnn_b1", "L1_gnn_W2", "L1_gnn_b2", "L1_gnn_Wn", "L1_gnn_bn",
        "L1_gnn_gamma", "L1_gnn_beta", "L2_gnn_W", "L2_gnn_b", "L2_gnn_gamma", "L2_gnn_beta", "L3_gnn_W", "L3_gnn_b",
        "L3_gnn_gamma", "L3_gnn_beta", "L3_gnn_gin_eps"]


def kernel(**inputs):
    import numpy as _np
    import concourse.bacc as _bacc
    from concourse import mybir as _mybir
    from concourse.bass_utils import run_bass_kernel_spmd as _run

    nc = _bacc.Bacc("TRN2", target_bir_lowering=False, num_devices=1)
    arrays, t = {}, {}
    for name in _INS:
        a = _np.ascontiguousarray(inputs[name])
        arrays[f"in_{name}"] = a
        t[name] = nc.dram_tensor(f"in_{name}", a.shape, _mybir.dt.from_np(a.dtype), kind="ExternalInput").ap()
    out = nc.dram_tensor("out_x", (N, D), F32, kind="ExternalOutput").ap()
    x1_d = nc.dram_tensor("x1_spill", (NP, D), F32, kind="Internal").ap()
    xa_d = nc.dram_tensor("x1_w1a", (NP, D), F32, kind="Internal").ap()
    xb_d = nc.dram_tensor("x1_w1b", (NP, D), F32, kind="Internal").ap()
    table_d = nc.dram_tensor("gathered_rows", (NP, D), F32, kind="Internal").ap()
    build(nc, t, out, x1_d, xa_d, xb_d, table_d)
    r = _run(nc, [arrays], core_ids=[0])
    return r.results[0]["out_x"]
```
